# Optimizing a Trainium2 kernel written in Bass

```python
import numpy as np
import jax
import jax.numpy as jnp

def _softmax(x, axis=-1):
    return jax.nn.softmax(x, axis=axis)

def _gelu(x):
    return jax.nn.gelu(x, approximate=True)

def _silu(x):
    return jax.nn.silu(x)

def _sigmoid(x):
    return jax.nn.sigmoid(x)

def _layernorm(x, axis=-1, eps=1e-05):
    m = jnp.mean(x, axis=axis, keepdims=True)
    v = jnp.var(x, axis=axis, keepdims=True)
    return (x - m) / jnp.sqrt(v + eps)

def _scatter_add(tgt, idx, src, axis=0):
    return tgt.at[idx].add(src)

def _segment_sum(src, seg, n):
    return jax.ops.segment_sum(src, seg, n)
kernel_name = 'mk_prb_d2_jaxref_r8_8bfe52'

def setup_inputs(seed: int=0):
    np.random.seed(seed)
    _w = jnp.asarray

    def _L0_attn_setup():
        import jax, jax.numpy as jnp
        import numpy as np
        D_MODEL = 128
        N_HEADS = 16
        D_HEAD = D_MODEL // N_HEADS
        B, T = (2, 256)
        key = jax.random.key(seed)
        ks = jax.random.split(key, 8)
        s = 1.0 / np.sqrt(D_MODEL)
        return {'x': jax.random.normal(ks[0], (B, T, D_MODEL), dtype=jnp.float32), 'ln_g': jnp.ones((D_MODEL,), jnp.float32), 'ln_b': jnp.zeros((D_MODEL,), jnp.float32), 'w_qkv': jax.random.normal(ks[1], (D_MODEL, 3 * D_MODEL), jnp.float32) * s, 'b_qkv': jnp.zeros((3 * D_MODEL,), jnp.float32), 'w_gate': jax.random.normal(ks[2], (D_MODEL, D_MODEL), jnp.float32) * s, 'b_gate': jnp.zeros((D_MODEL,), jnp.float32), 'w_proj': jax.random.normal(ks[3], (D_MODEL, D_MODEL), jnp.float32) * s, 'b_proj': jnp.zeros((D_MODEL,), jnp.float32)}
    _L0_attn_in = _L0_attn_setup()

    def _L0_ffn_setup():
        import jax, jax.numpy as jnp
        import numpy as np
        B, S, H, E, K = (2, 256, 128, 8, 2)
        FF = 4 * H
        EPS = 1e-05
        key = jax.random.key(seed)
        ks = jax.random.split(key, 5)
        rn = lambda k, shape, scale: jax.random.normal(k, shape, dtype=jnp.float32) * scale
        return {'x': rn(ks[0], (B, S, H), 1.0), 'router_W': rn(ks[1], (H, E), H ** (-0.5)), 'router_b': jnp.zeros((E,), jnp.float32), 'ln_g': jnp.ones((E, H), jnp.float32), 'ln_b': jnp.zeros((E, H), jnp.float32), 'W1': rn(ks[2], (E, H, FF), H ** (-0.5)), 'b1': jnp.zeros((E, FF), jnp.float32), 'W2': rn(ks[3], (E, FF, H), FF ** (-0.5)), 'b2': jnp.zeros((E, H), jnp.float32)}
    _L0_ffn_in = _L0_ffn_setup()

    def _L1_attn_setup():
        import jax, jax.numpy as jnp
        import numpy as np
        import math
        DIM = 128
        NUM_HEADS = 16
        HEAD_DIM = DIM // NUM_HEADS
        BATCH = 4
        SEQ = 512

        def _feature_map(x, R):
            x = x / math.sqrt(HEAD_DIM)
            proj = jnp.einsum('bhnd,dm->bhnm', x, R)
            sq_norm = jnp.sum(x * x, axis=-1, keepdims=True)
            return jnp.exp(proj - 0.5 * sq_norm)
        key = jax.random.key(seed)
        ks = jax.random.split(key, 10)
        s = 1.0 / math.sqrt(DIM)
        return {'x': jax.random.normal(ks[0], (BATCH, SEQ, DIM), dtype=jnp.float32), 'Wq': jax.random.normal(ks[1], (DIM, DIM), dtype=jnp.float32) * s, 'bq': jax.random.normal(ks[2], (DIM,), dtype=jnp.float32) * 0.01, 'Wk': jax.random.normal(ks[3], (DIM, DIM), dtype=jnp.float32) * s, 'bk': jax.random.normal(ks[4], (DIM,), dtype=jnp.float32) * 0.01, 'Wv': jax.random.normal(ks[5], (DIM, DIM), dtype=jnp.float32) * s, 'bv': jax.random.normal(ks[6], (DIM,), dtype=jnp.float32) * 0.01, 'Wo': jax.random.normal(ks[7], (DIM, DIM), dtype=jnp.float32) * s, 'bo': jax.random.normal(ks[8], (DIM,), dtype=jnp.float32) * 0.01, 'R': jax.random.normal(ks[9], (HEAD_DIM, HEAD_DIM), dtype=jnp.float32) * 0.4}
    _L1_attn_in = _L1_attn_setup()

    def _L1_ffn_setup():
        import jax, jax.numpy as jnp
        import numpy as np
        DIM = 128
        DEPTH = 2
        HEADS = 8
        DIM_HEAD = 64
        WINDOW = 64
        INNER = HEADS * DIM_HEAD
        HID = int(DIM * 4 * 2 / 3)
        B, N = (2, 1024)
        QK_SCALE = 8.0

        def shift_token(t):
            t1, t2 = jnp.split(t, 2, axis=-1)
            t2 = jnp.pad(t2, ((0, 0), (1, 0), (0, 0)))[:, :-1]
            return jnp.concatenate([t1, t2], axis=-1)

        def l2norm(t):
            return t / jnp.clip(jnp.linalg.norm(t, axis=-1, keepdims=True), 1e-12)

        def rotate_half(x):
            x1, x2 = jnp.split(x, 2, axis=-1)
            return jnp.concatenate([-x2, x1], axis=-1)

        def rotary_xpos(q, k):
            n = q.shape[-2]
            half_idx = jnp.arange(0, DIM_HEAD, 2, dtype=jnp.float32)
            inv_freq = 1.0 / 10000.0 ** (half_idx / DIM_HEAD)
            t = jnp.arange(n, dtype=jnp.float32)
            freqs = t[:, None] * inv_freq[None, :]
            freqs = jnp.concatenate([freqs, freqs], axis=-1)
            base = (half_idx + 0.4 * DIM_HEAD) / (1.4 * DIM_HEAD)
            power = (t - n // 2) / float(WINDOW // 2)
            scale = base[None, :] ** power[:, None]
            scale = jnp.concatenate([scale, scale], axis=-1)
            cos, sin = (jnp.cos(freqs), jnp.sin(freqs))
            q = q * cos * scale + rotate_half(q) * sin * scale
            k = k * cos / scale + rotate_half(k) * sin / scale
            return (q, k)

        def local_attention(q, k, v):
            b, h, n, d = q.shape
            w = n // WINDOW
            bq = q.reshape(b, h, w, WINDOW, d) * QK_SCALE
            bk = k.reshape(b, h, w, WINDOW, d)
            bv = v.reshape(b, h, w, WINDOW, d)

            def look_around(t):
                p = jnp.pad(t, ((0, 0), (0, 0), (1, 0), (0, 0), (0, 0)))
                return jnp.concatenate([p[:, :, :w], p[:, :, 1:]], axis=3)
            bk, bv = (look_around(bk), look_around(bv))
            bt = jnp.arange(n).reshape(w, WINDOW)
            btp = jnp.pad(bt, ((1, 0), (0, 0)), constant_values=-1)
            btk = jnp.concatenate([btp[:w], btp[1:]], axis=1)
            sim = jnp.einsum('bhwid,bhwjd->bhwij', bq, bk)
            i = bt[:, :, None]
            j = btk[:, None, :]
            mask = (i < j) | (i > j + WINDOW) | (j == -1)
            sim = jnp.where(mask, -jnp.finfo(sim.dtype).max, sim)
            attn = jax.nn.softmax(sim, axis=-1)
            out = jnp.einsum('bhwij,bhwjd->bhwid', attn, bv)
            return out.reshape(b, h, n, d)

        def _layer(x, wqkv, qs, ksc, wo, lg, lb, w1, b1, w2, b2):
            b, n, _ = x.shape
            h = shift_token(x)
            qkv = h @ wqkv
            q, k, v = jnp.split(qkv, 3, axis=-1)
            to_heads = lambda t: t.reshape(b, n, HEADS, DIM_HEAD).transpose(0, 2, 1, 3)
            q, k, v = (to_heads(q), to_heads(k), to_heads(v))
            q = l2norm(q) * qs
            k = l2norm(k) * ksc
            q, k = rotary_xpos(q, k)
            o = local_attention(q, k, v)
            o = o.transpose(0, 2, 1, 3).reshape(b, n, INNER)
            x = x + o @ wo
            h = shift_token(x)
            mu = h.mean(-1, keepdims=True)
            var = h.var(-1, keepdims=True)
            h = (h - mu) / jnp.sqrt(var + 1e-05) * lg + lb
            h = h @ w1 + b1
            a, g = jnp.split(h, 2, axis=-1)
            h = a * jax.nn.gelu(g, approximate=False)
            x = x + h @ w2 + b2
            return x
        key = jax.random.key(seed)
        ks = jax.random.split(key, 6)
        return {'x': jax.random.normal(ks[0], (B, N, DIM), jnp.float32), 'wqkv': jax.random.normal(ks[1], (DEPTH, DIM, 3 * INNER), jnp.float32) * 0.02, 'q_scale': jnp.ones((DEPTH, DIM_HEAD), jnp.float32), 'k_scale': jnp.ones((DEPTH, DIM_HEAD), jnp.float32), 'wo': jax.random.normal(ks[2], (DEPTH, INNER, DIM), jnp.float32) * 0.02, 'ln_g': jnp.ones((DEPTH, DIM), jnp.float32), 'ln_b': jnp.zeros((DEPTH, DIM), jnp.float32), 'w1': jax.random.normal(ks[3], (DEPTH, DIM, 2 * HID), jnp.float32) * 0.02, 'b1': jnp.zeros((DEPTH, 2 * HID), jnp.float32), 'w2': jax.random.normal(ks[4], (DEPTH, HID, DIM), jnp.float32) * 0.02, 'b2': jnp.zeros((DEPTH, DIM), jnp.float32)}
    _L1_ffn_in = _L1_ffn_setup()
    _d = {'L0_attn_x': _L0_attn_in['x'], 'L0_attn_ln_g': _L0_attn_in['ln_g'], 'L0_attn_ln_b': _L0_attn_in['ln_b'], 'L0_attn_w_qkv': _L0_attn_in['w_qkv'], 'L0_attn_b_qkv': _L0_attn_in['b_qkv'], 'L0_attn_w_gate': _L0_attn_in['w_gate'], 'L0_attn_b_gate': _L0_attn_in['b_gate'], 'L0_attn_w_proj': _L0_attn_in['w_proj'], 'L0_attn_b_proj': _L0_attn_in['b_proj'], 'L0_ffn_router_W': _L0_ffn_in['router_W'], 'L0_ffn_router_b': _L0_ffn_in['router_b'], 'L0_ffn_ln_g': _L0_ffn_in['ln_g'], 'L0_ffn_ln_b': _L0_ffn_in['ln_b'], 'L0_ffn_W1': _L0_ffn_in['W1'], 'L0_ffn_b1': _L0_ffn_in['b1'], 'L0_ffn_W2': _L0_ffn_in['W2'], 'L0_ffn_b2': _L0_ffn_in['b2'], 'L1_attn_Wq': _L1_attn_in['Wq'], 'L1_attn_bq': _L1_attn_in['bq'], 'L1_attn_Wk': _L1_attn_in['Wk'], 'L1_attn_bk': _L1_attn_in['bk'], 'L1_attn_Wv': _L1_attn_in['Wv'], 'L1_attn_bv': _L1_attn_in['bv'], 'L1_attn_Wo': _L1_attn_in['Wo'], 'L1_attn_bo': _L1_attn_in['bo'], 'L1_attn_R': _L1_attn_in['R'], 'L1_ffn_wqkv': _L1_ffn_in['wqkv'], 'L1_ffn_q_scale': _L1_ffn_in['q_scale'], 'L1_ffn_k_scale': _L1_ffn_in['k_scale'], 'L1_ffn_wo': _L1_ffn_in['wo'], 'L1_ffn_ln_g': _L1_ffn_in['ln_g'], 'L1_ffn_ln_b': _L1_ffn_in['ln_b'], 'L1_ffn_w1': _L1_ffn_in['w1'], 'L1_ffn_b1': _L1_ffn_in['b1'], 'L1_ffn_w2': _L1_ffn_in['w2'], 'L1_ffn_b2': _L1_ffn_in['b2']}
    _x0 = _d['L0_attn_x']
    _d['L0_attn_x'] = jax.random.normal(jax.random.fold_in(jax.random.key(seed), 1), (4, 512, 128), dtype=_x0.dtype)
    del _x0
    return _d

def reference(L0_attn_x, L0_attn_ln_g, L0_attn_ln_b, L0_attn_w_qkv, L0_attn_b_qkv, L0_attn_w_gate, L0_attn_b_gate, L0_attn_w_proj, L0_attn_b_proj, L0_ffn_router_W, L0_ffn_router_b, L0_ffn_ln_g, L0_ffn_ln_b, L0_ffn_W1, L0_ffn_b1, L0_ffn_W2, L0_ffn_b2, L1_attn_Wq, L1_attn_bq, L1_attn_Wk, L1_attn_bk, L1_attn_Wv, L1_attn_bv, L1_attn_Wo, L1_attn_bo, L1_attn_R, L1_ffn_wqkv, L1_ffn_q_scale, L1_ffn_k_scale, L1_ffn_wo, L1_ffn_ln_g, L1_ffn_ln_b, L1_ffn_w1, L1_ffn_b1, L1_ffn_w2, L1_ffn_b2):

    def _L0_attn_ref(x, ln_g, ln_b, w_qkv, b_qkv, w_gate, b_gate, w_proj, b_proj):
        import jax, jax.numpy as jnp
        import numpy as np
        D_MODEL = 128
        N_HEADS = 16
        D_HEAD = D_MODEL // N_HEADS
        B, T = (2, 256)
        Bb, Tt, Dd = x.shape
        H, dh = (N_HEADS, D_HEAD)
        mu = jnp.mean(x, axis=-1, keepdims=True)
        var = jnp.mean((x - mu) ** 2, axis=-1, keepdims=True)
        x_norm = (x - mu) / jnp.sqrt(var + 1e-05) * ln_g + ln_b
        qkv = x_norm @ w_qkv + b_qkv
        q, k, v = jnp.split(qkv, 3, axis=-1)
        gate_sig = jax.nn.sigmoid(x @ w_gate + b_gate)
        gate_norm = gate_sig / (jnp.mean(gate_sig, axis=-1, keepdims=True) + 1e-05)
        q = q * gate_norm
        k = k * gate_norm

        def to_heads(t):
            return t.reshape(Bb, Tt, H, dh).transpose(0, 2, 1, 3)
        q, k, v = (to_heads(q), to_heads(k), to_heads(v))
        q = jax.nn.elu(q) + 1.0
        k = jax.nn.elu(k) + 1.0
        kv = jnp.einsum('bhtd,bhtm->bhtdm', k, v)
        kv_cumsum = jnp.cumsum(kv, axis=2)
        out_num = jnp.einsum('bhtd,bhtdm->bhtm', q, kv_cumsum)
        k_cumsum = jnp.cumsum(k, axis=2)
        out_den = jnp.einsum('bhtd,bhtd->bht', q, k_cumsum)[..., None] + 1e-05
        out = out_num / out_den
        out = out.transpose(0, 2, 1, 3).reshape(Bb, Tt, Dd)
        return out @ w_proj + b_proj

    def _L0_ffn_ref(x, router_W, router_b, ln_g, ln_b, W1, b1, W2, b2):
        import jax, jax.numpy as jnp
        import numpy as np
        B, S, H, E, K = (2, 256, 128, 8, 2)
        FF = 4 * H
        EPS = 1e-05
        logits = x @ router_W + router_b
        w, idx = jax.lax.top_k(logits, K)
        w = jax.nn.softmax(w, axis=-1)
        gates = jnp.einsum('bske,bsk->bse', jax.nn.one_hot(idx, E, dtype=x.dtype), w)
        mu = jnp.mean(x, axis=-1, keepdims=True)
        var = jnp.mean(jnp.square(x - mu), axis=-1, keepdims=True)
        xhat = (x - mu) * jax.lax.rsqrt(var + EPS)
        h = xhat[:, :, None, :] * ln_g + ln_b
        a = jax.nn.gelu(jnp.einsum('bseh,ehf->bsef', h, W1) + b1, approximate=False)
        y = jnp.einsum('bsef,efh->bseh', a, W2) + b2
        y = y + x[:, :, None, :]
        out = jnp.einsum('bseh,bse->bsh', y, gates)
        return out

    def _L1_attn_ref(x, Wq, bq, Wk, bk, Wv, bv, Wo, bo, R):
        import jax, jax.numpy as jnp
        import numpy as np
        import math
        DIM = 128
        NUM_HEADS = 16
        HEAD_DIM = DIM // NUM_HEADS
        BATCH = 4
        SEQ = 512

        def _feature_map(x, R):
            x = x / math.sqrt(HEAD_DIM)
            proj = jnp.einsum('bhnd,dm->bhnm', x, R)
            sq_norm = jnp.sum(x * x, axis=-1, keepdims=True)
            return jnp.exp(proj - 0.5 * sq_norm)
        b, n, _ = x.shape
        h, d = (NUM_HEADS, HEAD_DIM)

        def split_heads(t):
            return t.reshape(b, n, h, d).transpose(0, 2, 1, 3)
        q = split_heads(x @ Wq.T + bq)
        k = split_heads(x @ Wk.T + bk)
        v = split_heads(x @ Wv.T + bv)
        q_prime = _feature_map(q, R)
        k_prime = _feature_map(k, R)
        kv = jnp.einsum('bhnd,bhne->bhde', k_prime, v)
        z = 1.0 / (jnp.sum(q_prime, axis=-1) + 1e-08)
        out = jnp.einsum('bhnd,bhde,bhn->bhne', q_prime, kv, z)
        out = out.transpose(0, 2, 1, 3).reshape(b, n, DIM)
        return out @ Wo.T + bo

    def _L1_ffn_ref(x, wqkv, q_scale, k_scale, wo, ln_g, ln_b, w1, b1, w2, b2):
        import jax, jax.numpy as jnp
        import numpy as np
        DIM = 128
        DEPTH = 2
        HEADS = 8
        DIM_HEAD = 64
        WINDOW = 64
        INNER = HEADS * DIM_HEAD
        HID = int(DIM * 4 * 2 / 3)
        B, N = (2, 1024)
        QK_SCALE = 8.0

        def shift_token(t):
            t1, t2 = jnp.split(t, 2, axis=-1)
            t2 = jnp.pad(t2, ((0, 0), (1, 0), (0, 0)))[:, :-1]
            return jnp.concatenate([t1, t2], axis=-1)

        def l2norm(t):
            return t / jnp.clip(jnp.linalg.norm(t, axis=-1, keepdims=True), 1e-12)

        def rotate_half(x):
            x1, x2 = jnp.split(x, 2, axis=-1)
            return jnp.concatenate([-x2, x1], axis=-1)

        def rotary_xpos(q, k):
            n = q.shape[-2]
            half_idx = jnp.arange(0, DIM_HEAD, 2, dtype=jnp.float32)
            inv_freq = 1.0 / 10000.0 ** (half_idx / DIM_HEAD)
            t = jnp.arange(n, dtype=jnp.float32)
            freqs = t[:, None] * inv_freq[None, :]
            freqs = jnp.concatenate([freqs, freqs], axis=-1)
            base = (half_idx + 0.4 * DIM_HEAD) / (1.4 * DIM_HEAD)
            power = (t - n // 2) / float(WINDOW // 2)
            scale = base[None, :] ** power[:, None]
            scale = jnp.concatenate([scale, scale], axis=-1)
            cos, sin = (jnp.cos(freqs), jnp.sin(freqs))
            q = q * cos * scale + rotate_half(q) * sin * scale
            k = k * cos / scale + rotate_half(k) * sin / scale
            return (q, k)

        def local_attention(q, k, v):
            b, h, n, d = q.shape
            w = n // WINDOW
            bq = q.reshape(b, h, w, WINDOW, d) * QK_SCALE
            bk = k.reshape(b, h, w, WINDOW, d)
            bv = v.reshape(b, h, w, WINDOW, d)

            def look_around(t):
                p = jnp.pad(t, ((0, 0), (0, 0), (1, 0), (0, 0), (0, 0)))
                return jnp.concatenate([p[:, :, :w], p[:, :, 1:]], axis=3)
            bk, bv = (look_around(bk), look_around(bv))
            bt = jnp.arange(n).reshape(w, WINDOW)
            btp = jnp.pad(bt, ((1, 0), (0, 0)), constant_values=-1)
            btk = jnp.concatenate([btp[:w], btp[1:]], axis=1)
            sim = jnp.einsum('bhwid,bhwjd->bhwij', bq, bk)
            i = bt[:, :, None]
            j = btk[:, None, :]
            mask = (i < j) | (i > j + WINDOW) | (j == -1)
            sim = jnp.where(mask, -jnp.finfo(sim.dtype).max, sim)
            attn = jax.nn.softmax(sim, axis=-1)
            out = jnp.einsum('bhwij,bhwjd->bhwid', attn, bv)
            return out.reshape(b, h, n, d)

        def _layer(x, wqkv, qs, ksc, wo, lg, lb, w1, b1, w2, b2):
            b, n, _ = x.shape
            h = shift_token(x)
            qkv = h @ wqkv
            q, k, v = jnp.split(qkv, 3, axis=-1)
            to_heads = lambda t: t.reshape(b, n, HEADS, DIM_HEAD).transpose(0, 2, 1, 3)
            q, k, v = (to_heads(q), to_heads(k), to_heads(v))
            q = l2norm(q) * qs
            k = l2norm(k) * ksc
            q, k = rotary_xpos(q, k)
            o = local_attention(q, k, v)
            o = o.transpose(0, 2, 1, 3).reshape(b, n, INNER)
            x = x + o @ wo
            h = shift_token(x)
            mu = h.mean(-1, keepdims=True)
            var = h.var(-1, keepdims=True)
            h = (h - mu) / jnp.sqrt(var + 1e-05) * lg + lb
            h = h @ w1 + b1
            a, g = jnp.split(h, 2, axis=-1)
            h = a * jax.nn.gelu(g, approximate=False)
            x = x + h @ w2 + b2
            return x
        for l in range(DEPTH):
            x = _layer(x, wqkv[l], q_scale[l], k_scale[l], wo[l], ln_g[l], ln_b[l], w1[l], b1[l], w2[l], b2[l])
        return x
    x = L0_attn_x
    xn = _layernorm(x, axis=-1)
    x = x + _L0_attn_ref(xn, L0_attn_ln_g, L0_attn_ln_b, L0_attn_w_qkv, L0_attn_b_qkv, L0_attn_w_gate, L0_attn_b_gate, L0_attn_w_proj, L0_attn_b_proj) + _L0_ffn_ref(xn, L0_ffn_router_W, L0_ffn_router_b, L0_ffn_ln_g, L0_ffn_ln_b, L0_ffn_W1, L0_ffn_b1, L0_ffn_W2, L0_ffn_b2)
    xn = _layernorm(x, axis=-1)
    x = x + _L1_attn_ref(xn, L1_attn_Wq, L1_attn_bq, L1_attn_Wk, L1_attn_bk, L1_attn_Wv, L1_attn_bv, L1_attn_Wo, L1_attn_bo, L1_attn_R) + _L1_ffn_ref(xn, L1_ffn_wqkv, L1_ffn_q_scale, L1_ffn_k_scale, L1_ffn_wo, L1_ffn_ln_g, L1_ffn_ln_b, L1_ffn_w1, L1_ffn_b1, L1_ffn_w2, L1_ffn_b2)
    return x

_drawn_inputs = setup_inputs


def setup_inputs(seed=0):
    import zlib

    import numpy as np

    out = dict(_drawn_inputs(seed))
    spreads = {'L0_attn_ln_g': (1.0, 0.2),
     'L0_attn_ln_b': (0.0, 0.1),
     'L0_attn_b_qkv': (0.0, 0.1),
     'L0_attn_b_gate': (0.0, 2.0),
     'L0_attn_b_proj': (0.0, 0.1),
     'L0_ffn_router_b': (0.0, 0.1),
     'L0_ffn_ln_g': (1.0, 0.2),
     'L0_ffn_ln_b': (0.0, 0.1),
     'L0_ffn_b1': (0.0, 0.1),
     'L0_ffn_b2': (0.0, 0.1),
     'L1_ffn_q_scale': (1.0, 0.6),
     'L1_ffn_k_scale': (1.0, 0.6),
     'L1_ffn_ln_g': (1.0, 0.6),
     'L1_ffn_ln_b': (0.0, 0.8),
     'L1_ffn_b1': (0.0, 0.8),
     'L1_ffn_b2': (0.0, 0.8)}
    factors = {'L1_attn_bq': 64.0,
     'L1_attn_bk': 61.71,
     'L1_attn_bo': 200.0,
     'L1_ffn_wqkv': 8.0,
     'L1_ffn_wo': 8.0,
     'L1_ffn_w1': 8.0,
     'L1_ffn_w2': 8.0,
     'L0_attn_w_gate': 2.703}
    for name, (base, spread) in spreads.items():
        noise = np.random.default_rng([zlib.crc32(name.encode()), seed]).standard_normal(out[name].shape)
        drawn = base * np.exp(spread * noise) if base else spread * noise
        out[name] = jnp.asarray(drawn.astype(out[name].dtype))
    for name, factor in factors.items():
        out[name] = (out[name] * factor).astype(out[name].dtype)
    return out
```

```python
from contextlib import ExitStack

import concourse.bass as bass
from concourse import mybir

F32 = mybir.dt.float32
U32 = mybir.dt.uint32
ALU = mybir.AluOpType
ACT = mybir.ActivationFunctionType
AX_X = mybir.AxisListType.X

P = 128
B, N = 4, 512
T = N // P
U = 2
H0, D0 = 16, 8
HV = H0 * (D0 + 1)
E, FF = 8, 512
FC = FF // P
L, H1, D1, W = 2, 8, 64, 64
HP = H1 // 2
HID = 341
HC = [(0, 128), (128, 128), (256, 85)]
KEYS = P + W
EPS = 1e-5
QK_SCALE = 8.0
NEG = -1.0e30

C_ID, C_CAUSAL, C_HM, C_BAND, C_IOTA, C_MHALF, C_NHB = 0, 128, 256, 272, 464, 472, 488
NC = 616
NR, NCV = 1032, 68


def shape_constants(np):
    c = np.zeros((P, NC), np.float32)
    p, k = np.arange(P)[:, None], np.arange(P)[None, :]
    c[:, C_ID:C_ID + P] = p == k
    c[:, C_CAUSAL:C_CAUSAL + P] = p <= k
    c[:, C_HM:C_HM + H0] = p // D0 == np.arange(H0)[None, :]
    kk = np.arange(KEYS)[None, :]
    c[:, C_BAND:C_BAND + KEYS] = np.where((p <= kk) & (kk <= p + W), 0.0, NEG)
    c[:, C_IOTA:C_IOTA + E] = np.arange(E)[None, :]
    c[:, C_MHALF:C_MHALF + 16] = -0.5
    c[:, C_NHB:C_NHB + P] = np.where(p // D0 == k // D0, -0.5, 0.0)
    half = np.arange(0, D1, 2, dtype=np.float32)
    inv = (1.0 / 10000.0 ** (half / D1)).astype(np.float32)
    t = np.arange(N, dtype=np.float32)
    f = t[:, None] * inv[None, :]
    f = np.concatenate([f, f], -1).astype(np.float32)
    base = ((half + 0.4 * D1) / (1.4 * D1)).astype(np.float32)
    power = ((t - N // 2) / float(W // 2)).astype(np.float32)
    s = base[None, :] ** power[:, None]
    s = np.concatenate([s, s], -1)
    sign = np.where(np.arange(D1) < D1 // 2, -1.0, 1.0).astype(np.float32)
    rot = np.stack([np.stack([np.cos(f) * s, np.cos(f) / s], 1),
                    np.stack([np.sin(f) * s * sign, np.sin(f) / s * sign], 1)], 1)
    rot = rot.reshape(T, P, 2, 2, D1).transpose(1, 2, 0, 3, 4)
    return c, np.ascontiguousarray(rot, dtype=np.float32).reshape(P, -1)


def build(nc, A, out):
    with ExitStack() as ctx:
        def sb(name, shape, dt=F32):
            return ctx.enter_context(nc.sbuf_tensor(name, shape, dt))

        def sem(name):
            return ctx.enter_context(nc.semaphore(name))

        def bc(ap, axis, n):
            v = ap.unsqueeze(axis)
            return v.broadcast_to(v.shape[:axis] + (n,) + v.shape[axis + 1:])

        cst = sb("cst", [P, NC])
        ident = cst[:, C_ID:C_ID + P]
        causal = cst[:, C_CAUSAL:C_CAUSAL + P]
        headmask = cst[:, C_HM:C_HM + H0]
        band = cst[:, C_BAND:C_BAND + KEYS]
        iota = cst[:, C_IOTA:C_IOTA + E]
        mhalf = cst[:, C_MHALF:C_MHALF + 16]
        nhb = cst[:, C_NHB:C_NHB + P]
        tabs = sb("tabs", [P, L, 2, T, 2, D1])
        w0 = sb("w0", [P, 512])
        rows = sb("rows", [P, NR])
        colv = sb("colv", [P, NCV])
        bias0 = rows[:, 0:512]
        rb = rows[:, 512:520]
        bvo = rows[:, 520:776].rearrange("p (i d) -> p i d", i=2)
        b2l = rows[:, 776:1032].rearrange("p (l d) -> p l d", l=L)
        lncol = colv[:, 0:2]
        elg = colv[:, 2:18].rearrange("p (i e) -> p i e", i=2)
        b1c = colv[:, 18:50].rearrange("p (e f) -> p e f", e=E)
        lgb = colv[:, 50:54].rearrange("p (l i) -> p l i", l=L)
        b1l = colv[:, 54:66].rearrange("p (l i j) -> p l i j", l=L, i=2)
        rW = sb("rW", [P, E])
        wproj = sb("wproj", [P, P])
        b2ext = sb("b2ext", [E + 1, P])
        W1 = sb("W1", [P, E, FF])
        W2 = sb("W2", [P, E, FC, P])
        wl1 = sb("wl1", [P, 4, P])
        bl1 = sb("bl1", [P, 2])
        Rblk = sb("Rblk", [P, P])
        wqkv = sb("wqkv", [P, L, 3 * H1 * D1])
        wo = sb("wo", [P, L, HP, P])
        w1 = sb("w1", [P, L, 2 * HID])
        w2 = sb("w2", [P, L, 3, P])

        x = sb("x", [P, U, T, P])
        xn = sb("xn", [P, U, T, P])
        ring = sb("ring", [P, 2, FC * N])
        stats = sb("stats", [P, U, T, 6])
        mv = sb("mv", [P, U, T, 2])
        ve = sb("ve", [P, U, T])
        rstd = sb("rstd", [P, U, T])
        lg = sb("lg", [P, U, T, E])
        top = sb("top", [P, U, T, 8])
        topi = sb("topi", [P, U, T, 8], U32)
        topf = sb("topf", [P, U, T, 2])
        wts = sb("wts", [P, U, 4, T])
        gate_a = sb("gate_a", [P, U, T, E + 1])
        gate_b = sb("gate_b", [P, U, T, E])
        gsum = sb("gsum", [P, U, T])
        gs = sb("gs", [P, U, T])
        den0 = sb("den0", [P, U, T, H0])
        ssq = sb("ssq", [P, U, 16])
        rn = sb("rn", [P, U, 2, 16])
        mx = sb("mx", [P, U, 2, 2])
        nmx = sb("nmx", [P, U, 2, 2])
        rs = sb("rs", [P, U, 2, H1])
        rsi = sb("rsi", [P, U, H1])
        NA = 13056
        arena = sb("arena", [P, U, NA])

        def carve(sizes, at=0):
            got = {}
            for name, size in sizes:
                got[name] = arena[:, :, at:at + size]
                at += size
            assert at <= NA, at
            return got

        a0 = carve([("xhat", 512), ("xnT", 512), ("xnormT", 512), ("xhatT", 512), ("qkvg", 2048),
                    ("gn", 512), ("me", 1024), ("qk", 1024), ("vext", T * HV), ("qT", 512), ("kT", 512),
                    ("sT", 1024), ("att", 512), ("attT", 512), ("gT", 512), ("S", 3 * HV), ("xe", 1024)])
        a1 = carve([("kT", 2048), ("qT", 1024), ("qn", 1024), ("t1", 1024), ("t2", 1024),
                    ("sm", 768), ("P", 1024), ("PT", 1024), ("on", 512), ("oT", 512), ("hT", 512)])
        a2 = carve([("x1T", 512), ("qs", 512), ("ks", 512), ("sqq", 512), ("sqk", 512), ("qp", 512),
                    ("kp", 512), ("vt", 512), ("kve", HV), ("o1", 512), ("o1T", 512)])
        a1["v"] = ring
        hid = a1["kT"][:, :, 0:1536]
        gg = a1["qn"]
        hn, hnT = a1["on"], a1["oT"]

        def tiles(ap, u, t):
            return ap[:, u, t * P:(t + 1) * P]

        ps = ctx.enter_context(nc.psum_tensor("ps", [P, 8, 512], F32))

        def bank(u, i):
            return ps[:, 4 * u + i, :]

        def cols(ap, t, w=P):
            return ap[:, t * w:(t + 1) * w]

        small_loaded = sem("small_loaded")
        first_loaded = sem("first_loaded")
        experts_loaded = sem("experts_loaded")
        l1_loaded = sem("l1_loaded")
        layers_loaded = sem("layers_loaded")
        tabs_made = sem("tabs_made")

        loop_sems = []

        def lsem(name):
            s = sem(name)
            loop_sems.append(s)
            return s

        x_loaded = [lsem("x_loaded0"), lsem("x_loaded1")]
        dve_step = lsem("dve_step")
        var_ready = lsem("var_ready"); rstd_ready = lsem("rstd_ready")
        xn_ready = lsem("xn_ready"); xhat_ready = lsem("xhat_ready")
        norm_transposed = lsem("norm_transposed"); normT_ready = lsem("normT_ready")
        logits_done = lsem("logits_done"); logits_read = lsem("logits_read")
        top2_ready = lsem("top2_ready"); ew_ready = lsem("ew_ready"); gates_ready = lsem("gates_ready")
        qkvg_done = lsem("qkvg_done"); qkvg_biased = lsem("qkvg_biased")
        gate_exp = lsem("gate_exp"); qk_min = lsem("qk_min"); qk_exp = lsem("qk_exp")
        qk_ready = lsem("qk_ready"); v_ready = lsem("v_ready")
        qkT_done = lsem("qkT_done"); qkT_ready = lsem("qkT_ready")
        state_done = lsem("state_done"); state_ready = lsem("state_ready")
        qexp_ready = lsem("qexp_ready"); scores0_done = lsem("scores0_done"); sT_masked = lsem("sT_masked")
        out0_done = lsem("out0_done"); att_ready = lsem("att_ready")
        attT_done = lsem("attT_done"); attT_ready = lsem("attT_ready"); proj_done = lsem("proj_done")
        x_base = lsem("x_base")
        xe_ready = lsem("xe_ready"); h0_done = lsem("h0_done"); gelu_done = lsem("gelu_done")
        y0_done = lsem("y0_done"); y_added = lsem("y_added")
        y_transposed = lsem("y_transposed"); hT_ready = lsem("hT_ready"); zeros_ready = lsem("zeros_ready")
        l1_qkv = lsem("l1_qkv"); l1_qs = lsem("l1_qs"); l1_sq = lsem("l1_sq"); l1_v = lsem("l1_v")
        l1_feat = lsem("l1_feat"); l1_exp = lsem("l1_exp"); l1_kv = lsem("l1_kv"); l1_kve = lsem("l1_kve")
        l1_num = lsem("l1_num"); l1_o = lsem("l1_o"); l1_oT_done = lsem("l1_oT_done")
        l1_oT = lsem("l1_oT"); l1_out = lsem("l1_out"); l1_bo = lsem("l1_bo"); x_l1 = lsem("x_l1")
        qk1_done = lsem("qk1_done"); sq_ready = lsem("sq_ready"); ss_ready = lsem("ss_ready")
        rn_ready = lsem("rn_ready"); raw_ready = lsem("raw_ready"); rot_sum = lsem("rot_sum"); rot2_ready = lsem("rot2_ready")
        rotated = lsem("rotated"); v1_done = lsem("v1_done"); v1_ready = lsem("v1_ready")
        qkT1_done = lsem("qkT1_done"); qkT1_ready = lsem("qkT1_ready")
        scores1_done = lsem("scores1_done"); masked = lsem("masked"); exp_done = lsem("exp_done")
        PT_done = lsem("PT_done"); PT_ready = [lsem("PT_ready_act"), lsem("PT_ready_dve")]
        av_done = lsem("av_done"); o_normed = lsem("o_normed"); oT_done = lsem("oT_done")
        oT_ready = lsem("oT_ready"); wo_done = lsem("wo_done"); y_updated = lsem("y_updated")
        h_back = lsem("h_back"); hn_ready = lsem("hn_ready"); hnT_done = lsem("hnT_done")
        hnT_ready = lsem("hnT_ready"); g_done = lsem("g_done"); a_done = lsem("a_done")
        gelu1_done = lsem("gelu1_done"); hid_ready = lsem("hid_ready"); ffn_out = lsem("ffn_out")
        y_b2 = lsem("y_b2"); y_final = lsem("y_final")
        out_ready = lsem("out_ready"); out_stored = lsem("out_stored")

        rot_raw = arena[:, 0, 0:1024].rearrange("p (c t q d) -> p c t q d", c=2, t=T, q=2)
        qksc = arena[:, 0, 1024:1536].rearrange("p (c l q d) -> p c l q d", c=2, l=L, q=2)
        R8 = arena[:, 0, 1536:1536 + D0]
        bl1_raw = colv[:, 66:68]
        HD = D1 // 2

        with nc.Block() as block:
            @block.sync
            def _(sp):
                small = [(cst[:], A["cst"]), (rows[:], A["rows"].partition_broadcast(P)), (colv[:], A["colv"]),
                         (arena[:, 0, 0:1024], A["rot"]), (arena[:, 0, 1024:1536], A["qksc"].partition_broadcast(P)),
                         (R8, A["L1_attn_R"].partition_broadcast(H0))]
                for dst, src in small:
                    sp.dma_start(dst, src).then_inc(small_loaded, 16)
                first = [(w0[:, 0:384], A["L0_attn_w_qkv"]), (w0[:, 384:512], A["L0_attn_w_gate"]),
                         (rW[:], A["L0_ffn_router_W"]),
                         (wproj[:], A["L0_attn_w_proj"]), (b2ext[0:E, :], A["L0_ffn_b2"]),
                         (b2ext[E:E + 1, :], A["L0_attn_b_proj"].unsqueeze(0))]
                for dst, src in first:
                    sp.dma_start(dst, src).then_inc(first_loaded, 16)
                sp.dma_start(W1[:], A["L0_ffn_W1"].rearrange("e h f -> h e f")).then_inc(experts_loaded, 16)
                for e in range(E):
                    sp.dma_start(W2[:, e], A["L0_ffn_W2"][e].rearrange("(f p) h -> p f h", p=P)).then_inc(experts_loaded, 16)

            @block.gpsimd
            def _(pool):
                for i, name in enumerate(("WqT", "WkT", "WvT", "WoT")):
                    pool.dma_start(wl1[:, i, :], A[name]).then_inc(l1_loaded, 16)
                pool.dma_start(wqkv[:], A["L1_ffn_wqkv"].rearrange("l h n -> h l n")).then_inc(layers_loaded, 16)
                pool.dma_start(w1[:], A["L1_ffn_w1"].rearrange("l h n -> h l n")).then_inc(layers_loaded, 16)
                for l in range(L):
                    pool.dma_start(wo[:, l], A["L1_ffn_wo"][l].rearrange("(c p) h -> p c h", p=P)).then_inc(layers_loaded, 16)
                    for j, (c0, n) in enumerate(HC):
                        pool.dma_start(w2[0:n, l, j], A["L1_ffn_w2"][l][c0:c0 + n]).then_inc(layers_loaded, 16)

            @block.vector
            def _(dve):
                dve.wait_ge(small_loaded, 16 * 6)
                for l in range(L):
                    for c in range(2):
                        for q in range(2):
                            nc.vector.tensor_tensor(tabs[:, l, c, :, q, :], rot_raw[:, c, :, q, :],
                                                    bc(qksc[:, c, l, q, :], 1, T), ALU.mult)
                nc.vector.tensor_scalar(bl1[:], bl1_raw, D0 ** -0.5, None, ALU.mult)
                nc.vector.tensor_tensor(Rblk[:].rearrange("p (h d) -> p h d", h=H0), bc(R8, 1, H0),
                                        bc(headmask, 2, D0), ALU.mult).then_inc(tabs_made, 1)
                dve.wait_ge(tabs_made, 1)
        nc.all_engine_barrier()
        N_FIRST, N_EXPERTS, N_L1, N_LAYERS = 16 * 6, 16 * (1 + E), 16 * 4, 16 * (2 + L * 4)

        xv = A["x"].rearrange("b (t p) d -> p b t d", p=P)
        ov = out.rearrange("b (t p) d -> p b t d", p=P)

        SCORE, PTB, OB, PREP = (0, 1), (2, 3), (4, 5), (6, 7)
        SLOTS = HP * T

        def prep_index(l, t, u):
            return (l * T + t) * U + u

        def unit_index(l, s, u):
            return (l * SLOTS + s) * U + u

        def keys_of(t):
            return (t * P - W, (t + 1) * P, 0) if t else (0, P, W)

        with nc.Fori(0, B // U) as it:
            with nc.Block() as block:

                @block.sync
                def _(sp):
                    for u in range(U):
                        sp.dma_start(x[:, u], xv[:, bass.ds(it * U + u, 1)].rearrange("p b t d -> p (b t) d")).then_inc(x_loaded[u], 16)
                    for u in range(U):
                        sp.wait_ge(out_ready, u + 1)
                        sp.dma_start(ov[:, bass.ds(it * U + u, 1)].rearrange("p b t d -> p (b t) d"), x[:, u]).then_inc(out_stored, 16)
                    sp.wait_ge(out_stored, 16 * U)

                @block.gpsimd
                def _(pool):
                    g = nc.gpsimd

                    def rsqrt_var(n):
                        u = n % U
                        pool.wait_ge(var_ready, n + 1)
                        g.tensor_tensor(rstd[:, u], ve[:, u], mhalf[:, 0:T], ALU.pow).then_inc(rstd_ready, 1)

                    for n in range(4):
                        rsqrt_var(n)
                    for u in range(U):
                        pool.wait_ge(qkvg_biased, u + 1)
                        v = a0["vext"][:, u].rearrange("p (t h d) -> p t h d", t=T, h=H0)
                        g.memset(v[:, :, :, D0:D0 + 1], 1.0)
                        src = a0["qkvg"][:, u].rearrange("p (t c) -> p t c", t=T)[:, :, 256:384]
                        for t in range(T):
                            last = g.tensor_copy(v[:, t, :, 0:D0], src[:, t].rearrange("p (h d) -> p h d", h=H0))
                        last.then_inc(v_ready, 1)
                    for t in range(T):
                        for u in range(U):
                            n = t * U + u
                            pool.wait_ge(qkT_ready, 2 * u + 1)
                            if n >= 2:
                                pool.wait_ge(scores0_done, 4 * (n - 1))
                            g.tensor_tensor(ring[:, n % 2].rearrange("p (h t) -> p h t", h=H0),
                                            bc(tiles(a0["qT"], u, t), 1, H0), bc(headmask, 2, P),
                                            ALU.mult).then_inc(qexp_ready, 1)
                    pool.wait_ge(experts_loaded, N_EXPERTS)
                    for u in range(U):
                        for e in range(E):
                            n = u * E + e
                            if e >= 2:
                                pool.wait_ge(h0_done, 4 * (n - 1))
                            elif e == 0:
                                pool.wait_ge(normT_ready, 2 * u + 2)
                            g.tensor_scalar(a0["xe"][:, u, (e % 2) * N:(e % 2 + 1) * N], a0["xhatT"][:, u],
                                            elg[:, 0, e:e + 1], elg[:, 1, e:e + 1], ALU.mult, ALU.add).then_inc(xe_ready, 1)
                            if u == 1 and e == 3:
                                rsqrt_var(4)
                    rsqrt_var(5)
                    pool.wait_ge(l1_loaded, N_L1)
                    for u in range(U):
                        pool.wait_ge(xn_ready, U + u + 1)
                        g.memset(a1["hT"][:, u, 0:1], 0.0)
                        g.memset(a1["P"][:, u].rearrange("p (s k) -> p s k", k=2 * P)[:, :, 0:W], 0.0)
                        g.tensor_copy(a2["kve"][:, u, P:HV], headmask).then_inc(zeros_ready, 1)
                        g.tensor_tensor(x[:, u], x[:, u], bc(bvo[:, 1, :], 1, T), ALU.add).then_inc(l1_bo, 1)
                    for u in range(U):
                        for i, (s, d) in enumerate((("qs", "sqq"), ("ks", "sqk"))):
                            pool.wait_ge(l1_qs, 2 * u + i + 1)
                            g.tensor_tensor(a2[d][:, u], a2[s][:, u], a2[s][:, u], ALU.mult).then_inc(l1_sq, 1)

                    def rotate2(l, t, u):
                        pool.wait_ge(raw_ready, prep_index(l, t, u) + 1)
                        q = a1["qn"][:, u].rearrange("p (q h d) -> p q h d", q=2, h=H1)
                        o = a1["t2"][:, u].rearrange("p (q h d) -> p q h d", q=2, h=H1)
                        for a, b in ((0, HD), (HD, 0)):
                            last = g.tensor_tensor(o[:, :, :, a:a + HD], q[:, :, :, b:b + HD],
                                                   bc(tabs[:, l, 1, t, :, a:a + HD], 2, H1), ALU.mult)
                        last.then_inc(rot2_ready, 1)

                    def inverse_norms(l, t, u):
                        pool.wait_ge(ss_ready, prep_index(l, t, u) + 1)
                        g.tensor_tensor(rn[:, u, t % 2], ssq[:, u], mhalf, ALU.pow).then_inc(rn_ready, 1)

                    def scale_k(l, t, u):
                        pi = prep_index(l, t, u)
                        pool.wait_ge(rot_sum, pi + 1)
                        pool.wait_ge(rn_ready, pi + 1)
                        k = a1["t1"][:, u, 512:1024].rearrange("p (h d) -> p h d", h=H1)
                        g.tensor_tensor(k, k, bc(rn[:, u, t % 2, H1:16], 2, D1), ALU.mult).then_inc(rotated, 1)

                    pool.wait_ge(layers_loaded, N_LAYERS)
                    for l in range(L):
                        for t in range(T):
                            rotate2(l, t, 0)
                            inverse_norms(l, t, 0)
                            rotate2(l, t, 1)
                            scale_k(l, t, 0)
                            inverse_norms(l, t, 1)
                            scale_k(l, t, 1)
                        for u in range(U):
                            pool.wait_ge(y_transposed, 2 + 4 * l + u + 1)
                            g.tensor_tensor(xn[:, u], xn[:, u], bc(b2l[:, l], 1, T), ALU.add).then_inc(y_b2, 1)
                        for u in range(U):
                            rsqrt_var(6 + 2 * l + u)

                @block.scalar
                def _(act):
                    a = nc.scalar

                    act.wait_ge(first_loaded, N_FIRST)
                    for u in range(U):
                        act.wait_ge(norm_transposed, 2 * u + 1)
                        a.activation(a0["xnT"][:, u], bank(u, 0), ACT.Copy).then_inc(normT_ready, 1)
                        act.wait_ge(norm_transposed, 2 * u + 2)
                        a.activation(a0["xnormT"][:, u], bank(u, 1), ACT.Identity, bias=lncol[:, 1:2], scale=lncol[:, 0:1])
                        a.activation(a0["xhatT"][:, u], bank(u, 1), ACT.Copy).then_inc(normT_ready, 1)
                    for u in range(U):
                        act.wait_ge(top2_ready, u + 1)
                        a.activation(wts[:, u, 1], wts[:, u, 0], ACT.Exp).then_inc(ew_ready, 1)
                    for u in range(U):
                        act.wait_ge(qkvg_biased, u + 1)
                        src = a0["qkvg"][:, u].rearrange("p (t c) -> p t c", t=T)[:, :, 384:512]
                        a.activation(a0["gn"][:, u].rearrange("p (t c) -> p t c", t=T), src, ACT.Exp, scale=-1.0).then_inc(gate_exp, 1)
                    for u in range(U):
                        act.wait_ge(qk_min, u + 1)
                        a.activation(a0["me"][:, u], a0["me"][:, u], ACT.Exp).then_inc(qk_exp, 1)
                    for u in range(U):
                        for i, name in enumerate(("qT", "kT")):
                            act.wait_ge(qkT_done, 2 * u + i + 1)
                            a.activation(a0[name][:, u], bank(u, i), ACT.Copy).then_inc(qkT_ready, 1)
                    for u in range(U):
                        act.wait_ge(attT_done, 2 * u + 1)
                        a.activation(a0["attT"][:, u], bank(u, 0), ACT.Copy).then_inc(attT_ready, 1)
                        act.wait_ge(attT_done, 2 * u + 2)
                        a.activation(a0["gT"][0:E + 1, u], bank(u, 1)[0:E + 1], ACT.Copy).then_inc(attT_ready, 1)
                    act.wait_ge(experts_loaded, N_EXPERTS)
                    for u in range(U):
                        for e in range(E):
                            n = u * E + e
                            if n >= 2:
                                act.wait_ge(y0_done, n - 1)
                            for f in range(FC):
                                hc = n * FC + f
                                act.wait_ge(h0_done, hc + 1)
                                a.activation(ring[:, n % 2, f * N:(f + 1) * N], bank(u, hc % 2), ACT.Gelu,
                                             bias=b1c[:, e, f:f + 1]).then_inc(gelu_done, 1)

                    def shifted(inst, u):
                        act.wait_ge(y_transposed, inst + 1)
                        if inst < U:
                            a.activation(a2["x1T"][:, u], bank(u, 0), ACT.Copy)
                            act.wait_ge(zeros_ready, u + 1)
                        a.activation(a1["hT"][0:64, u], bank(u, 0)[0:64], ACT.Copy)
                        a.activation(a1["hT"][64:128, u, 1:N], bank(u, 0)[64:128, 0:N - 1], ACT.Copy).then_inc(hT_ready, 1)

                    for u in range(U):
                        shifted(u, u)
                    for u in range(U):
                        for i, name in enumerate(("qs", "ks")):
                            act.wait_ge(l1_qkv, 3 * u + i + 1)
                            a.activation(a2[name][:, u], bank(u, 1 + i), ACT.Identity, bias=bl1[:, i:i + 1],
                                         scale=D0 ** -0.5).then_inc(l1_qs, 1)
                    for u in range(U):
                        for i, name in enumerate(("qp", "kp")):
                            act.wait_ge(l1_feat, 2 * u + i + 1)
                            a.activation(a2[name][:, u], bank(u, i), ACT.Exp).then_inc(l1_exp, 1)
                    for u in range(U):
                        act.wait_ge(l1_oT_done, u + 1)
                        a.activation(a2["o1T"][:, u], bank(u, 1), ACT.Copy).then_inc(l1_oT, 1)

                    act.wait_ge(layers_loaded, N_LAYERS)
                    for l in range(L):
                        def raw(t, u):
                            pi = prep_index(l, t, u)
                            act.wait_ge(qk1_done, pi + 1)
                            if t:
                                act.wait_ge(rot2_ready, pi - 1)
                                act.wait_ge(rot_sum, pi - 1)
                            a.activation(a1["qn"][:, u].rearrange("p (q c) -> p q c", q=2), ps[:, 6:8, :], ACT.Copy).then_inc(raw_ready, 1)

                        def squares(t, u):
                            pi = prep_index(l, t, u)
                            act.wait_ge(raw_ready, pi + 1)
                            if t:
                                act.wait_ge(qkT1_done, 2 * pi - 2)
                            a.activation(a1["t1"][:, u], a1["qn"][:, u], ACT.Square).then_inc(sq_ready, 1)

                        def values(t, u):
                            pi = prep_index(l, t, u)
                            act.wait_ge(v1_done, pi + 1)
                            a.activation(a1["v"][:, u, t * 512:(t + 1) * 512], ps[:, 6, :], ACT.Copy).then_inc(v1_ready, 1)

                        def qk_transposed(t, u):
                            pi = prep_index(l, t, u)
                            act.wait_ge(qkT1_done, 2 * pi + 1)
                            a.activation(a1["qT"][:, u, (t % 2) * 512:(t % 2 + 1) * 512], ps[:, 7, :], ACT.Copy).then_inc(qkT1_ready, 1)
                            act.wait_ge(qkT1_done, 2 * pi + 2)
                            kv = a1["kT"][:, u].rearrange("p (c k) -> p c k", c=HP)[:, :, t * P:(t + 1) * P]
                            a.activation(kv, ps[:, 6, :].rearrange("p (c k) -> p c k", c=HP), ACT.Copy).then_inc(qkT1_ready, 1)

                        def exps(s, u):
                            t, hp = s // HP, s % HP
                            ui = unit_index(l, s, u)
                            k0, k1, _ = keys_of(t)
                            n = k1 - k0
                            act.wait_ge(masked, ui + 1)
                            if s >= 2:
                                act.wait_ge(PT_done, ui - 3)
                            for i in range(2):
                                smv = a1["sm"][:, u].rearrange("p (r i k) -> p r i k", r=2, i=2)[:, s % 2, i, 0:n]
                                pv = a1["P"][:, u].rearrange("p (r i k) -> p r i k", r=2, i=2)[:, s % 2, i, 2 * P - n:2 * P]
                                last = a.activation(pv, smv, ACT.Exp, scale=rn[:, u, t % 2, 2 * hp + i:2 * hp + i + 1],
                                                    bias=nmx[:, u, s % 2, i:i + 1],
                                                    accum_out=rs[:, u, t % 2, 2 * hp + i:2 * hp + i + 1])
                            last.then_inc(exp_done, 1)

                        def probs_moved(s):
                            u, t = 0, s // HP
                            ui = unit_index(l, s, u)
                            act.wait_ge(PT_done, ui + 1)
                            if s >= 2:
                                act.wait_ge(av_done, ui - 3)
                            b0 = 0 if t else 1
                            dst = a1["PT"][:, u, (s % 2) * 512:(s % 2 + 1) * 512].rearrange("p (i b k) -> p i b k", i=2, b=2)[:, :, b0:2]
                            a.activation(dst, ps[:, PTB[u], :].rearrange("p (i b k) -> p i b k", i=2, b=2)[:, :, b0:2], ACT.Copy).then_inc(PT_ready[0], 1)

                        for u in range(U):
                            raw(0, u)
                            squares(0, u)
                            values(0, u)
                        qk_transposed(0, 0)
                        qk_transposed(0, 1)
                        for s in range(SLOTS + HP):
                            t1, ph = s // HP + 1, s % HP
                            if s < SLOTS:
                                exps(s, 0)
                            if 1 <= s <= SLOTS:
                                probs_moved(s - 1)
                            if t1 < T:
                                if ph < 2:
                                    raw(t1, ph)
                                if ph == 3:
                                    qk_transposed(t1, 0)
                            if s < SLOTS:
                                exps(s, 1)
                            if t1 < T:
                                if ph < 2:
                                    squares(t1, ph)
                                    values(t1, ph)
                                if ph == 3:
                                    qk_transposed(t1, 1)
                            if s >= 6 and ph == 2:
                                for u in range(U):
                                    pi = prep_index(l, (s - 6) // HP, u)
                                    act.wait_ge(oT_done, pi + 1)
                                    a.activation(a1["oT"][:, u], ps[:, PTB[u], :], ACT.Copy).then_inc(oT_ready, 1)

                        for u in range(U):
                            shifted(2 + 4 * l + u, u)
                        for u in range(U):
                            act.wait_ge(hnT_done, 2 * l + u + 1)
                            a.activation(hnT[:, u], bank(u, 2), ACT.Identity, bias=lgb[:, l, 1:2], scale=lgb[:, l, 0:1]).then_inc(hnT_ready, 1)
                        for u in range(U):
                            for j, (_, n) in enumerate(HC):
                                gi = (2 * l + u) * 3 + j
                                act.wait_ge(g_done, gi + 1)
                                if j == 2:
                                    act.wait_ge(hid_ready, gi - 1)
                                a.activation(gg[0:n, u, (j % 2) * N:(j % 2 + 1) * N], bank(u, j % 2)[0:n], ACT.Gelu,
                                             bias=b1l[0:n, l, 1, j:j + 1]).then_inc(gelu1_done, 1)
                        if l + 1 < L:
                            for u in range(U):
                                shifted(4 + 4 * l + u, u)

                @block.vector
                def _(dve):
                    v = nc.vector
                    steps = [0]

                    def step(ins):
                        steps[0] += 1
                        return ins.then_inc(dve_step, 1)

                    def settle():
                        dve.wait_ge(dve_step, steps[0])

                    def norm_stats(u, src):
                        for t in range(T):
                            last = v.bn_stats(stats[:, u, t], src(t))
                        step(last)
                        settle()
                        for t in range(T):
                            last = v.bn_aggr(mv[:, u, t], stats[:, u, t])
                        step(last)
                        settle()
                        v.tensor_scalar(ve[:, u], mv[:, u, :, 1], EPS, None, ALU.add).then_inc(var_ready, 1)

                    def norm_apply(n, u, dst, src, ready):
                        dve.wait_ge(rstd_ready, n + 1)
                        for t in range(T):
                            last = v.tensor_scalar(dst(t), src(t), mv[:, u, t, 0:1], rstd[:, u, t:t + 1], ALU.subtract, ALU.mult)
                        last.then_inc(ready, 1)

                    for u in range(U):
                        dve.wait_ge(x_loaded[u], 16)
                        norm_stats(u, lambda t: x[:, u, t])
                    for u in range(U):
                        norm_apply(u, u, lambda t: xn[:, u, t], lambda t: x[:, u, t], xn_ready)
                    for u in range(U):
                        dve.wait_ge(xn_ready, u + 1)
                        norm_stats(u, lambda t: xn[:, u, t])
                    for u in range(U):
                        norm_apply(U + u, u, lambda t: tiles(a0["xhat"], u, t), lambda t: xn[:, u, t], xhat_ready)

                    for u in range(U):
                        dve.wait_ge(logits_done, u + 1)
                        v.tensor_tensor(lg[:, u], bank(u, 3)[:, 0:T * E].rearrange("p (t e) -> p t e", t=T),
                                        bc(rb, 1, T), ALU.add).then_inc(logits_read, 1)
                        dve.wait_ge(logits_read, u + 1)
                        for t in range(T):
                            last = v.max(top[:, u, t], lg[:, u, t])
                        step(last)
                        settle()
                        v.tensor_tensor(wts[:, u, 0], top[:, u, :, 1], top[:, u, :, 0], ALU.subtract).then_inc(top2_ready, 1)
                        for t in range(T):
                            last = v.max_index(topi[:, u, t], top[:, u, t], lg[:, u, t])
                        step(last)
                        settle()
                        step(v.tensor_copy(topf[:, u], topi[:, u, :, 0:2]))

                    for u in range(U):
                        for t in range(T):
                            dve.wait_ge(qkvg_done, u * T + t + 1)
                            last = v.tensor_tensor(a0["qkvg"][:, u, t * 512:(t + 1) * 512], bank(u, t), bias0, ALU.add)
                        last.then_inc(qkvg_biased, 1)

                    for u in range(U):
                        dve.wait_ge(ew_ready, u + 1)
                        step(v.tensor_scalar(wts[:, u, 2], wts[:, u, 1], 1.0, None, ALU.add))
                        settle()
                        step(v.reciprocal(wts[:, u, 2], wts[:, u, 2]))
                        settle()
                        step(v.tensor_tensor(wts[:, u, 3], wts[:, u, 1], wts[:, u, 2], ALU.mult))
                        settle()
                        v.tensor_tensor(gsum[:, u], wts[:, u, 2], wts[:, u, 3], ALU.add)
                        v.memset(gate_a[:, u, :, E:E + 1], 1.0)
                        for t in range(T):
                            v.tensor_scalar(gate_a[:, u, t, 0:E], iota, topf[:, u, t, 0:1], wts[:, u, 2, t:t + 1], ALU.is_equal, ALU.mult)
                            last = v.tensor_scalar(gate_b[:, u, t], iota, topf[:, u, t, 1:2], wts[:, u, 3, t:t + 1], ALU.is_equal, ALU.mult)
                        step(last)
                        settle()
                        v.tensor_tensor(gate_a[:, u, :, 0:E], gate_a[:, u, :, 0:E], gate_b[:, u], ALU.add).then_inc(gates_ready, 1)

                    for u in range(U):
                        gn = a0["gn"][:, u]
                        gn3 = gn.rearrange("p (t c) -> p t c", t=T)
                        qk3 = a0["qkvg"][:, u].rearrange("p (t c) -> p t c", t=T)[:, :, 0:256]
                        dve.wait_ge(gate_exp, u + 1)
                        step(v.tensor_scalar(gn, gn, 1.0, None, ALU.add))
                        settle()
                        step(v.reciprocal(gn, gn))
                        settle()
                        step(v.reduce_sum(gs[:, u], gn3, AX_X))
                        settle()
                        step(v.tensor_scalar(gs[:, u], gs[:, u], 1.0 / P, EPS, ALU.mult, ALU.add))
                        settle()
                        step(v.reciprocal(gs[:, u], gs[:, u]))
                        settle()
                        step(v.tensor_tensor(gn3, gn3, bc(gs[:, u], 2, P), ALU.mult))
                        settle()
                        for i in range(2):
                            last = v.tensor_tensor(qk3[:, :, i * P:(i + 1) * P], qk3[:, :, i * P:(i + 1) * P], gn3, ALU.mult)
                        step(last)
                        settle()
                        v.tensor_scalar(a0["me"][:, u].rearrange("p (t c) -> p t c", t=T), qk3, 0.0, None, ALU.min).then_inc(qk_min, 1)
                    for u in range(U):
                        qk3 = a0["qkvg"][:, u].rearrange("p (t c) -> p t c", t=T)[:, :, 0:256]
                        dve.wait_ge(qk_exp, u + 1)
                        v.scalar_tensor_tensor(out=a0["qk"][:, u].rearrange("p (t c) -> p t c", t=T), in0=qk3, scalar=0.0,
                                               in1=a0["me"][:, u].rearrange("p (t c) -> p t c", t=T),
                                               op0=ALU.max, op1=ALU.add).then_inc(qk_ready, 1)

                    for u in range(U):
                        for t in range(T):
                            v.scalar_tensor_tensor(out=x[:, u, t], in0=xn[:, u, t], scalar=gsum[:, u, t:t + 1],
                                                   in1=x[:, u, t], op0=ALU.mult, op1=ALU.add)

                    for u in range(U):
                        dve.wait_ge(state_done, u + 1)
                        v.tensor_tensor(a0["S"][:, u].rearrange("p (c h d) -> p c h d", c=3, h=H0),
                                        bank(u, 2)[:, 0:3 * HV].rearrange("p (c h d) -> p c h d", c=3, h=H0),
                                        bc(bc(headmask, 2, D0 + 1), 1, 3), ALU.mult).then_inc(state_ready, 1)

                    def attended(n):
                        t, u = n // U, n % U
                        dve.wait_ge(out0_done, 4 * n + 4)
                        o = bank(u, 2 + t // 2)[:, (t % 2) * HV:(t % 2 + 1) * HV].rearrange("p (h d) -> p h d", h=H0)
                        step(v.tensor_scalar(den0[:, u, t], o[:, :, D0], EPS, None, ALU.add))
                        settle()
                        step(v.reciprocal(den0[:, u, t], den0[:, u, t]))
                        settle()
                        v.tensor_tensor(tiles(a0["att"], u, t).rearrange("p (h d) -> p h d", h=H0), o[:, :, 0:D0],
                                        bc(den0[:, u, t], 2, D0), ALU.mult).then_inc(att_ready, 1)

                    for i in range(T * U * 4):
                        n, hg = i // 4, i % 4
                        t, u = n // U, n % U
                        dve.wait_ge(scores0_done, i + 1)
                        before = i - 2 if hg >= 2 else i - 6
                        if before >= 0:
                            dve.wait_ge(out0_done, before + 1)
                        v.tensor_tensor(a0["sT"][:, u, (hg % 2) * 512:(hg % 2 + 1) * 512].rearrange("p (h t) -> p h t", h=4),
                                        bank(u, hg % 2).rearrange("p (h t) -> p h t", h=4), bc(causal, 1, 4),
                                        ALU.mult).then_inc(sT_masked, 1)
                        if i >= 5 and (i - 5) % 4 == 0:
                            attended((i - 5) // 4)
                    attended(T * U - 1)

                    for u in range(U):
                        dve.wait_ge(proj_done, u + 1)
                        v.tensor_tensor(x[:, u].rearrange("p t d -> p (t d)"), x[:, u].rearrange("p t d -> p (t d)"),
                                        bank(u, 2), ALU.add).then_inc(x_base, 1)

                    for u in range(U):
                        for e in range(E):
                            n = u * E + e
                            dve.wait_ge(y0_done, n + 1)
                            if e:
                                dve.wait_ge(y_added, n)
                            else:
                                dve.wait_ge(x_base, u + 1)
                            for t in range(T):
                                last = v.scalar_tensor_tensor(out=x[:, u, t], in0=cols(bank(u, 2 + (e + 1) % 2), t),
                                                              scalar=gate_a[:, u, t, e:e + 1], in1=x[:, u, t],
                                                              op0=ALU.mult, op1=ALU.add)
                            last.then_inc(y_added, 1)
                            if u == 1 and e == 1:
                                norm_stats(0, lambda t: x[:, 0, t])
                            if u == 1 and e == 4:
                                norm_apply(4, 0, lambda t: xn[:, 0, t], lambda t: x[:, 0, t], xn_ready)
                    dve.wait_ge(y_added, U * E)
                    norm_stats(1, lambda t: x[:, 1, t])
                    norm_apply(5, 1, lambda t: xn[:, 1, t], lambda t: x[:, 1, t], xn_ready)

                    dve.wait_ge(l1_loaded, N_L1)
                    for u in range(U):
                        dve.wait_ge(l1_qkv, 3 * u + 3)
                        v.tensor_tensor(a2["vt"][:, u].rearrange("p (t c) -> p t c", t=T), bank(u, 3).rearrange("p (t c) -> p t c", t=T),
                                        bc(bvo[:, 0, :], 1, T), ALU.add).then_inc(l1_v, 1)
                    for u in range(U):
                        dve.wait_ge(l1_kv, u + 1)
                        v.tensor_tensor(a2["kve"][:, u, 0:P].rearrange("p (h d) -> p h d", h=H0),
                                        bank(u, 2)[:, 0:P].rearrange("p (h d) -> p h d", h=H0),
                                        bc(headmask, 2, D0), ALU.mult).then_inc(l1_kve, 1)
                    for u in range(U):
                        dve.wait_ge(l1_num, u + 1)
                        for half, bk in enumerate((3, 0)):
                            o = bank(u, bk)[:, 0:2 * HV].rearrange("p (t c) -> p t c", t=2)
                            last = v.tensor_scalar(den0[:, u, 2 * half:2 * half + 2], o[:, :, P:HV], 1e-8, None, ALU.add)
                        step(last)
                        settle()
                        step(v.reciprocal(den0[:, u], den0[:, u]))
                        settle()
                        for t in range(T):
                            o = bank(u, (3, 0)[t // 2])[:, (t % 2) * HV:(t % 2) * HV + P].rearrange("p (h d) -> p h d", h=H0)
                            last = v.tensor_tensor(tiles(a2["o1"], u, t).rearrange("p (h d) -> p h d", h=H0), o,
                                                   bc(den0[:, u, t], 2, D0), ALU.mult)
                        last.then_inc(l1_o, 1)
                    for u in range(U):
                        dve.wait_ge(l1_out, u + 1)
                        dve.wait_ge(l1_bo, u + 1)
                        v.tensor_tensor(x[:, u].rearrange("p t d -> p (t d)"), x[:, u].rearrange("p t d -> p (t d)"),
                                        bank(u, 2), ALU.add).then_inc(x_l1, 1)

                    for l in range(L):
                        def sums(t, u):
                            pi = prep_index(l, t, u)
                            dve.wait_ge(sq_ready, pi + 1)
                            step(v.reduce_sum(ssq[:, u], a1["t1"][:, u].rearrange("p (g d) -> p g d", d=D1), AX_X))
                            settle()
                            v.tensor_scalar(ssq[:, u, 0:H1], ssq[:, u, 0:H1], 1e-24, QK_SCALE ** -2, ALU.max, ALU.mult)
                            v.tensor_scalar(ssq[:, u, H1:16], ssq[:, u, H1:16], 1e-24, None, ALU.max).then_inc(ss_ready, 1)

                        def rotate1(t, u):
                            dve.wait_ge(raw_ready, prep_index(l, t, u) + 1)
                            step(v.tensor_tensor(a1["t1"][:, u].rearrange("p (q h d) -> p q h d", q=2, h=H1),
                                                 a1["qn"][:, u].rearrange("p (q h d) -> p q h d", q=2, h=H1),
                                                 bc(tabs[:, l, 0, t], 2, H1), ALU.mult))

                        def rotate(t, u):
                            dve.wait_ge(rot2_ready, prep_index(l, t, u) + 1)
                            settle()
                            v.tensor_tensor(a1["t1"][:, u], a1["t1"][:, u], a1["t2"][:, u], ALU.add).then_inc(rot_sum, 1)

                        def mask_max(s, u):
                            t = s // HP
                            ui = unit_index(l, s, u)
                            k0, k1, b0 = keys_of(t)
                            n = k1 - k0
                            dve.wait_ge(scores1_done, ui + 1)
                            if s >= 2:
                                dve.wait_ge(exp_done, ui - 3)
                            if s % HP == 0:
                                dve.wait_ge(rn_ready, prep_index(l, t, u) + 1)
                            for i in range(2):
                                smv = a1["sm"][:, u].rearrange("p (r i k) -> p r i k", r=2, i=2)[:, s % 2, i, 0:n]
                                last = v.tensor_tensor_reduce(out=smv, in0=ps[:, SCORE[i], 0:n],
                                                              in1=band[:, b0:b0 + n], scale=1.0, scalar=3 * NEG,
                                                              op0=ALU.add, op1=ALU.max, accum_out=mx[:, u, s % 2, i:i + 1])
                            step(last)
                            settle()
                            hp = s % HP
                            v.scalar_tensor_tensor(out=nmx[:, u, s % 2], in0=mx[:, u, s % 2], scalar=-1.0,
                                                   in1=rn[:, u, t % 2, 2 * hp:2 * hp + 2], op0=ALU.mult, op1=ALU.mult).then_inc(masked, 1)

                        def probs_moved(s):
                            u, t = 1, s // HP
                            ui = unit_index(l, s, u)
                            dve.wait_ge(PT_done, ui + 1)
                            if s >= 2:
                                dve.wait_ge(av_done, ui - 3)
                            b0 = 0 if t else 1
                            dst = a1["PT"][:, u, (s % 2) * 512:(s % 2 + 1) * 512].rearrange("p (i b k) -> p i b k", i=2, b=2)[:, :, b0:2]
                            v.tensor_copy(dst, ps[:, PTB[u], :].rearrange("p (i b k) -> p i b k", i=2, b=2)[:, :, b0:2]).then_inc(PT_ready[1], 1)

                        for u in range(U):
                            sums(0, u)
                            rotate1(0, u)
                        for u in range(U):
                            rotate(0, u)
                        for s in range(SLOTS + HP):
                            t1, ph = s // HP + 1, s % HP
                            if s < SLOTS:
                                mask_max(s, 0)
                            if t1 < T:
                                if 1 <= ph <= 2:
                                    sums(t1, ph - 1)
                                if ph >= 2:
                                    rotate(t1, ph - 2)
                            if s < SLOTS:
                                mask_max(s, 1)
                            if 1 <= s <= SLOTS:
                                probs_moved(s - 1)
                            if t1 < T and 1 <= ph <= 2:
                                rotate1(t1, ph - 1)
                            if s >= 5 and ph == 1:
                                t = (s - 5) // HP
                                for u in range(U):
                                    pi = prep_index(l, t, u)
                                    step(v.reciprocal(rsi[:, u], rs[:, u, t % 2]))
                                    dve.wait_ge(av_done, unit_index(l, HP * t + HP - 1, u) + 1)
                                    settle()
                                    v.tensor_tensor(a1["on"][:, u].rearrange("p (h d) -> p h d", h=H1),
                                                    ps[:, OB[u], :].rearrange("p (h d) -> p h d", h=H1),
                                                    bc(rsi[:, u], 2, D1), ALU.mult).then_inc(o_normed, 1)
                            if s >= 7 and ph == 3:
                                t = (s - 7) // HP
                                for u in range(U):
                                    pi = prep_index(l, t, u)
                                    dve.wait_ge(wo_done, pi + 1)
                                    v.tensor_tensor(xn[:, u, t], xn[:, u, t], ps[:, PTB[u], 0:P], ALU.add).then_inc(y_updated, 1)

                        for u in range(U):
                            dve.wait_ge(h_back, 2 * l + u + 1)
                            norm_stats(u, lambda t: cols(bank(u, 1), t))
                        for u in range(U):
                            norm_apply(6 + 2 * l + u, u, lambda t: tiles(hn, u, t), lambda t: cols(bank(u, 1), t), hn_ready)
                        for u in range(U):
                            for j, (_, n) in enumerate(HC):
                                gi = (2 * l + u) * 3 + j
                                dve.wait_ge(a_done, gi + 1)
                                dve.wait_ge(gelu1_done, gi + 1)
                                v.scalar_tensor_tensor(out=hid[0:n, u, j * N:(j + 1) * N], in0=bank(u, 2 + j % 2)[0:n],
                                                       scalar=b1l[0:n, l, 0, j:j + 1], in1=gg[0:n, u, (j % 2) * N:(j % 2 + 1) * N],
                                                       op0=ALU.add, op1=ALU.mult).then_inc(hid_ready, 1)
                        for u in range(U):
                            dve.wait_ge(ffn_out, 2 * l + u + 1)
                            dve.wait_ge(y_b2, 2 * l + u + 1)
                            v.tensor_tensor(xn[:, u].rearrange("p t d -> p (t d)"), xn[:, u].rearrange("p t d -> p (t d)"),
                                            bank(u, 1), ALU.add).then_inc(y_final, 1)

                    for u in range(U):
                        dve.wait_ge(y_final, 2 * (L - 1) + u + 1)
                        v.tensor_tensor(x[:, u], x[:, u], xn[:, u], ALU.add).then_inc(out_ready, 1)

                @block.tensor
                def _(pe):
                    mm = nc.tensor.matmul

                    def transpose(dst, src):
                        return nc.tensor.transpose(dst, src, ident)

                    for u in range(U):
                        pe.wait_ge(xn_ready, u + 1)
                        for t in range(T):
                            last = transpose(cols(bank(u, 0), t), xn[:, u, t])
                        last.then_inc(norm_transposed, 1)
                        pe.wait_ge(xhat_ready, u + 1)
                        for t in range(T):
                            last = transpose(cols(bank(u, 1), t), tiles(a0["xhat"], u, t))
                        last.then_inc(norm_transposed, 1)
                    pe.wait_ge(first_loaded, N_FIRST)
                    for u in range(U):
                        pe.wait_ge(normT_ready, 2 * u + 1)
                        for t in range(T):
                            last = mm(bank(u, 3)[:, t * E:(t + 1) * E], tiles(a0["xnT"], u, t), rW[:], start=True, stop=True)
                        last.then_inc(logits_done, 1)
                    for u in range(U):
                        pe.wait_ge(normT_ready, 2 * u + 2)
                        for t in range(T):
                            if t == 3:
                                pe.wait_ge(logits_read, u + 1)
                            mm(bank(u, t)[:, 0:384], tiles(a0["xnormT"], u, t), w0[:, 0:384], start=True, stop=True)
                            mm(bank(u, t)[:, 384:512], tiles(a0["xnT"], u, t), w0[:, 384:512], start=True, stop=True).then_inc(qkvg_done, 1)

                    qk = a0["qk"]
                    for u in range(U):
                        pe.wait_ge(qk_ready, u + 1)
                        for i in range(2):
                            for t in range(T):
                                last = transpose(cols(bank(u, i), t), qk[:, u, t * 256 + i * P:t * 256 + (i + 1) * P])
                            last.then_inc(qkT_done, 1)
                        pe.wait_ge(v_ready, u + 1)
                        for c in range(1, T):
                            for t in range(c):
                                last = mm(bank(u, 2)[:, (c - 1) * HV:c * HV], qk[:, u, t * 256 + P:(t + 1) * 256],
                                          a0["vext"][:, u, t * HV:(t + 1) * HV], start=(t == 0), stop=(t == c - 1))
                        last.then_inc(state_done, 1)

                    def scores0(i):
                        n, hg = i // 4, i % 4
                        t, u = n // U, n % U
                        if hg == 0:
                            pe.wait_ge(qexp_ready, n + 1)
                            pe.wait_ge(qkT_ready, 2 * u + 2)
                        before = i - 2 if hg >= 2 else i - 6
                        if before >= 0:
                            pe.wait_ge(sT_masked, before + 1)
                        mm(bank(u, hg % 2), tiles(a0["kT"], u, t), ring[:, n % 2, hg * 512:(hg + 1) * 512],
                           start=True, stop=True).then_inc(scores0_done, 1)

                    def out0(i):
                        n, hg = i // 4, i % 4
                        t, u = n // U, n % U
                        o = bank(u, 2 + t // 2)[:, (t % 2) * HV:(t % 2 + 1) * HV]
                        pe.wait_ge(sT_masked, i + 1)
                        if hg == 0:
                            pe.wait_ge(state_ready, u + 1)
                            if t:
                                mm(o, tiles(a0["qT"], u, t), a0["S"][:, u, (t - 1) * HV:t * HV], start=True, stop=False)
                        for j in range(4):
                            h = 4 * hg + j
                            last = mm(o[:, h * 9:(h + 1) * 9], a0["sT"][:, u, (hg % 2) * 512 + j * P:(hg % 2) * 512 + (j + 1) * P],
                                      a0["vext"][:, u, t * HV + h * 9:t * HV + (h + 1) * 9], start=(t == 0), stop=(t == 0 or h == H0 - 1))
                        last.then_inc(out0_done, 1)

                    for i in range(T * U * 4 + 1):
                        if i < T * U * 4:
                            scores0(i)
                        if i:
                            out0(i - 1)

                    for u in range(U):
                        pe.wait_ge(att_ready, (T - 1) * U + u + 1)
                        for t in range(T):
                            last = transpose(cols(bank(u, 0), t), tiles(a0["att"], u, t))
                        last.then_inc(attT_done, 1)
                        pe.wait_ge(gates_ready, u + 1)
                        for t in range(T):
                            last = transpose(cols(bank(u, 1), t)[0:E + 1], gate_a[:, u, t])
                        last.then_inc(attT_done, 1)
                    for u in range(U):
                        pe.wait_ge(attT_ready, 2 * u + 2)
                        for t in range(T):
                            mm(cols(bank(u, 2), t), tiles(a0["attT"], u, t), wproj[:], start=True, stop=False)
                            last = mm(cols(bank(u, 2), t), a0["gT"][0:E + 1, u, t * P:(t + 1) * P], b2ext[:], start=False, stop=True)
                        last.then_inc(proj_done, 1)

                    def hidden(n):
                        u, e = n // E, n % E
                        pe.wait_ge(xe_ready, n + 1)
                        for f in range(FC):
                            hc = n * FC + f
                            if e or f >= 2:
                                pe.wait_ge(gelu_done, hc - 1)
                            mm(bank(u, hc % 2), W1[:, e, f * P:(f + 1) * P], a0["xe"][:, u, (e % 2) * N:(e % 2 + 1) * N],
                               start=True, stop=True).then_inc(h0_done, 1)

                    def expert_out(n):
                        u, e = n // E, n % E
                        pe.wait_ge(gelu_done, n * FC + FC)
                        if e >= 2:
                            pe.wait_ge(y_added, n - 1)
                        elif e == 1:
                            pe.wait_ge(x_base, u + 1)
                        for t in range(T):
                            for f in range(FC):
                                last = mm(cols(bank(u, 2 + (e + 1) % 2), t), ring[:, n % 2, f * N + t * P:f * N + (t + 1) * P],
                                          W2[:, e, f, :], start=(f == 0), stop=(f == FC - 1))
                        last.then_inc(y0_done, 1)

                    pe.wait_ge(experts_loaded, N_EXPERTS)
                    for n in range(U * E + 1):
                        if n < U * E:
                            hidden(n)
                        if n:
                            expert_out(n - 1)

                    def transpose_state(u):
                        for t in range(T):
                            last = transpose(cols(bank(u, 0), t), xn[:, u, t])
                        last.then_inc(y_transposed, 1)

                    for u in range(U):
                        pe.wait_ge(xn_ready, U + u + 1)
                        transpose_state(u)

                    pe.wait_ge(l1_loaded, N_L1)
                    for u in range(U):
                        pe.wait_ge(hT_ready, u + 1)
                        for i in range(2):
                            mm(bank(u, 1 + i), wl1[:, i, :], a2["x1T"][:, u], start=True, stop=True).then_inc(l1_qkv, 1)
                        for t in range(T):
                            last = mm(cols(bank(u, 3), t), tiles(a2["x1T"], u, t), wl1[:, 2, :], start=True, stop=True)
                        last.then_inc(l1_qkv, 1)
                    for u in range(U):
                        pe.wait_ge(l1_sq, 2 * u + 1)
                        mm(bank(u, 0), Rblk[:], a2["qs"][:, u], start=True, stop=False)
                        mm(bank(u, 0), nhb, a2["sqq"][:, u], start=False, stop=True).then_inc(l1_feat, 1)
                        pe.wait_ge(l1_sq, 2 * u + 2)
                        for t in range(T):
                            mm(cols(bank(u, 1), t), tiles(a2["ks"], u, t), Rblk[:], start=True, stop=False)
                            last = mm(cols(bank(u, 1), t), tiles(a2["sqk"], u, t), nhb, start=False, stop=True)
                        last.then_inc(l1_feat, 1)
                    for u in range(U):
                        pe.wait_ge(l1_exp, 2 * u + 2)
                        pe.wait_ge(l1_v, u + 1)
                        for t in range(T):
                            last = mm(bank(u, 2)[:, 0:P], tiles(a2["kp"], u, t), tiles(a2["vt"], u, t), start=(t == 0), stop=(t == T - 1))
                        last.then_inc(l1_kv, 1)
                    for u in range(U):
                        pe.wait_ge(l1_kve, u + 1)
                        for t in range(T):
                            last = mm(bank(u, (3, 0)[t // 2])[:, (t % 2) * HV:(t % 2 + 1) * HV], tiles(a2["qp"], u, t), a2["kve"][:, u],
                                      start=True, stop=True)
                        last.then_inc(l1_num, 1)
                    for u in range(U):
                        pe.wait_ge(l1_o, u + 1)
                        for t in range(T):
                            last = transpose(cols(bank(u, 1), t), tiles(a2["o1"], u, t))
                        last.then_inc(l1_oT_done, 1)
                    for u in range(U):
                        pe.wait_ge(l1_oT, u + 1)
                        for t in range(T):
                            last = mm(cols(bank(u, 2), t), tiles(a2["o1T"], u, t), wl1[:, 3, :], start=True, stop=True)
                        last.then_inc(l1_out, 1)

                    pe.wait_ge(layers_loaded, N_LAYERS)
                    for l in range(L):
                        if l == 0:
                            pe.wait_ge(x_l1, U)
                        pe.wait_ge(hT_ready, 4 * l + U)

                        def project_qk(t, u):
                            pi = prep_index(l, t, u)
                            if u:
                                pe.wait_ge(v1_ready, pi)
                            elif t:
                                pe.wait_ge(qkT1_ready, 2 * pi)
                            for i in range(2):
                                last = mm(ps[:, PREP[i], :], tiles(a1["hT"], u, t), wqkv[:, l, i * 512:(i + 1) * 512], start=True, stop=True)
                            last.then_inc(qk1_done, 1)

                        def project_v(t, u):
                            pi = prep_index(l, t, u)
                            pe.wait_ge(raw_ready, pi + 1)
                            mm(ps[:, 6, :], tiles(a1["hT"], u, t), wqkv[:, l, 1024:1536], start=True, stop=True).then_inc(v1_done, 1)

                        def transpose_qk(t, u):
                            pi = prep_index(l, t, u)
                            pe.wait_ge(rotated, pi + 1)
                            for i, bk in enumerate((7, 6)):
                                if u:
                                    pe.wait_ge(qkT1_ready, 2 * pi - 1 + i)
                                elif i == 1:
                                    pe.wait_ge(v1_ready, pi + 2)
                                else:
                                    pe.wait_ge(raw_ready, pi + 2)
                                for c in range(HP):
                                    last = transpose(cols(ps[:, bk, :], c), a1["t1"][:, u, i * 512 + c * P:i * 512 + (c + 1) * P])
                                last.then_inc(qkT1_done, 1)

                        def scores(s, u):
                            t, hp = s // HP, s % HP
                            ui = unit_index(l, s, u)
                            k0, k1, _ = keys_of(t)
                            pe.wait_ge(qkT1_ready, 2 * prep_index(l, t, u) + 2)
                            if s or u:
                                pe.wait_ge(masked, ui)
                            for i in range(2):
                                r = slice(64 * i, 64 * i + 64)
                                last = mm(ps[:, SCORE[i], 0:k1 - k0],
                                          a1["qT"][r, u, (t % 2) * 512 + hp * P:(t % 2) * 512 + (hp + 1) * P],
                                          a1["kT"][r, u, hp * N + k0:hp * N + k1], start=True, stop=True)
                            last.then_inc(scores1_done, 1)

                        def transpose_probs(s, u):
                            t = s // HP
                            ui = unit_index(l, s, u)
                            if s:
                                pe.wait_ge(PT_ready[u], l * SLOTS + s)
                            if s >= 7 and s % HP == 3:
                                pe.wait_ge(y_updated, prep_index(l, (s - 7) // HP, u) + 1)
                            if s >= 6 and s % HP == 2:
                                pe.wait_ge(oT_ready, prep_index(l, (s - 6) // HP, u) + 1)
                            pe.wait_ge(exp_done, ui + 1)
                            for i in range(2):
                                for b in range(0 if t else 1, 2):
                                    src = a1["P"][:, u, ((s % 2) * 2 + i) * 256 + b * P:((s % 2) * 2 + i) * 256 + (b + 1) * P]
                                    last = transpose(cols(ps[:, PTB[u], :], 2 * i + b), src)
                            last.then_inc(PT_done, 1)

                        def weigh_values(s, u):
                            t, hp = s // HP, s % HP
                            ui = unit_index(l, s, u)
                            pe.wait_ge(PT_ready[u], l * SLOTS + s + 1)
                            if hp == 0 and t:
                                pe.wait_ge(o_normed, prep_index(l, t - 1, u) + 1)
                            for i in range(2):
                                h = 2 * hp + i
                                for b in range(0 if t else 1, 2):
                                    vs = t - 1 + b
                                    last = mm(ps[:, OB[u], h * D1:(h + 1) * D1],
                                              a1["PT"][:, u, (s % 2) * 512 + (2 * i + b) * P:(s % 2) * 512 + (2 * i + b + 1) * P],
                                              a1["v"][:, u, vs * 512 + h * D1:vs * 512 + (h + 1) * D1],
                                              start=(b == 0 or t == 0), stop=(b == 1))
                            last.then_inc(av_done, 1)

                        project_qk(0, 0)
                        project_v(0, 0)
                        project_qk(0, 1)
                        project_v(0, 1)
                        transpose_qk(0, 0)
                        transpose_qk(0, 1)
                        for s in range(SLOTS + HP):
                            t1, ph = s // HP + 1, s % HP
                            for u in range(U):
                                if s < SLOTS:
                                    scores(s, u)
                                if 1 <= s <= SLOTS:
                                    transpose_probs(s - 1, u)
                                if 2 <= s <= SLOTS + 1:
                                    weigh_values(s - 2, u)
                                if t1 < T:
                                    if ph < 2:
                                        (project_qk, project_v)[u](t1, ph)
                                    if ph == 3:
                                        transpose_qk(t1, u)
                            if s >= 6 and ph == 2:
                                for u in range(U):
                                    pi = prep_index(l, (s - 6) // HP, u)
                                    pe.wait_ge(o_normed, pi + 1)
                                    pe.wait_ge(PT_ready[u], l * SLOTS + min(s, SLOTS))
                                    for c in range(HP):
                                        last = transpose(cols(ps[:, PTB[u], :], c), a1["on"][:, u, c * P:(c + 1) * P])
                                    last.then_inc(oT_done, 1)
                            if s >= 7 and ph == 3:
                                for u in range(U):
                                    pi = prep_index(l, (s - 7) // HP, u)
                                    pe.wait_ge(oT_ready, pi + 1)
                                    pe.wait_ge(PT_ready[u], l * SLOTS + min(s, SLOTS))
                                    for c in range(HP):
                                        last = mm(ps[:, PTB[u], 0:P], a1["oT"][:, u, c * P:(c + 1) * P], wo[:, l, c, :],
                                                  start=(c == 0), stop=(c == HP - 1))
                                    last.then_inc(wo_done, 1)

                        pe.wait_ge(y_updated, (l + 1) * T * U)
                        for u in range(U):
                            transpose_state(u)
                        for u in range(U):
                            pe.wait_ge(hT_ready, 2 + 4 * l + u + 1)
                            for t in range(T):
                                last = transpose(cols(bank(u, 1), t), tiles(a1["hT"], u, t))
                            last.then_inc(h_back, 1)
                        for u in range(U):
                            pe.wait_ge(hn_ready, 2 * l + u + 1)
                            for t in range(T):
                                last = transpose(cols(bank(u, 2), t), tiles(hn, u, t))
                            last.then_inc(hnT_done, 1)
                        for u in range(U):
                            pe.wait_ge(hnT_ready, 2 * l + u + 1)
                            for j, (c0, n) in enumerate(HC):
                                gi = (2 * l + u) * 3 + j
                                if j == 2:
                                    pe.wait_ge(gelu1_done, gi - 1)
                                    pe.wait_ge(hid_ready, gi - 1)
                                mm(bank(u, j % 2)[0:n], w1[:, l, HID + c0:HID + c0 + n], hnT[:, u], start=True, stop=True).then_inc(g_done, 1)
                                mm(bank(u, 2 + j % 2)[0:n], w1[:, l, c0:c0 + n], hnT[:, u], start=True, stop=True).then_inc(a_done, 1)
                        for u in range(U):
                            pe.wait_ge(hid_ready, (2 * l + u) * 3 + 3)
                            for t in range(T):
                                for j, (_, n) in enumerate(HC):
                                    last = mm(cols(bank(u, 1), t), hid[0:n, u, j * N + t * P:j * N + (t + 1) * P], w2[0:n, l, j, :],
                                              start=(j == 0), stop=(j == 2))
                            last.then_inc(ffn_out, 1)
                        if l + 1 < L:
                            for u in range(U):
                                pe.wait_ge(y_final, 2 * l + u + 1)
                                transpose_state(u)

            nc.all_engine_barrier()
            for s in loop_sems:
                nc.sync.sem_clear(s)
            nc.all_engine_barrier()


_INS = ["L0_attn_w_qkv", "L0_attn_w_gate", "L0_attn_w_proj", "L0_attn_b_proj", "L0_ffn_router_W", "L0_ffn_W1",
        "L0_ffn_W2", "L0_ffn_b2", "L1_attn_R", "L1_ffn_wqkv", "L1_ffn_wo", "L1_ffn_w1", "L1_ffn_w2"]


def kernel(**inputs):
    import numpy as np
    import concourse.bacc as bacc
    from concourse.bass_utils import run_bass_kernel_spmd

    inputs = {name: np.asarray(a) for name, a in inputs.items()}
    arrays = {name: np.ascontiguousarray(inputs[name]) for name in _INS}
    arrays["x"] = np.ascontiguousarray(inputs["L0_attn_x"])
    for n in "qkvo":
        arrays[f"W{n}T"] = np.ascontiguousarray(inputs[f"L1_attn_W{n}"].T)
    arrays["rows"] = np.concatenate([inputs[n].reshape(-1) for n in (
        "L0_attn_b_qkv", "L0_attn_b_gate", "L0_ffn_router_b", "L1_attn_bv", "L1_attn_bo", "L1_ffn_b2")])
    qk = np.stack([inputs["L1_ffn_q_scale"], inputs["L1_ffn_k_scale"]], 1)
    swapped = np.concatenate([qk[..., D1 // 2:], qk[..., :D1 // 2]], -1)
    arrays["qksc"] = np.concatenate([qk.reshape(-1), swapped.reshape(-1)])
    b1l = np.zeros((L, 2, 3, P), np.float32)
    for j, (c0, n) in enumerate(HC):
        b1l[:, :, j, :n] = inputs["L1_ffn_b1"].reshape(L, 2, HID)[:, :, c0:c0 + n]
    lgb = np.stack([inputs["L1_ffn_ln_g"], inputs["L1_ffn_ln_b"]], 1).reshape(2 * L, P)
    arrays["colv"] = np.ascontiguousarray(np.concatenate([
        inputs["L0_attn_ln_g"][None], inputs["L0_attn_ln_b"][None], inputs["L0_ffn_ln_g"], inputs["L0_ffn_ln_b"],
        inputs["L0_ffn_b1"].reshape(E * FC, P), lgb, b1l.reshape(-1, P), inputs["L1_attn_bq"][None],
        inputs["L1_attn_bk"][None]]).T)
    arrays["cst"], arrays["rot"] = shape_constants(np)

    nc = bacc.Bacc("TRN2", target_bir_lowering=False, num_devices=1)
    A, feed = {}, {}
    for name, a in arrays.items():
        A[name] = nc.dram_tensor(f"in_{name}", a.shape, mybir.dt.from_np(a.dtype), kind="ExternalInput").ap()
        feed[f"in_{name}"] = a
    out = nc.dram_tensor("out", (B, N, P), F32, kind="ExternalOutput").ap()
    build(nc, A, out)
    r = run_bass_kernel_spmd(nc, [feed], core_ids=[0])
    return r.results[0]["out"]
```

```python
from contextlib import ExitStack

import concourse.bass as bass
from concourse import mybir

F32 = mybir.dt.float32
U32 = mybir.dt.uint32
ALU = mybir.AluOpType
ACT = mybir.ActivationFunctionType
AX_X = mybir.AxisListType.X

P = 128
B, N = 4, 512
T = N // P
U = 2
H0, D0 = 16, 8
HV = H0 * (D0 + 1)
E, FF = 8, 512
FC = FF // P
L, H1, D1, W = 2, 8, 64, 64
EXPERT_STEPS = (U * E + 1) * FC
ITEMS = T * 4 * U
HP = H1 // 2
SLOTS = T * HP
AHEAD = 10
HID = 341
HC = [(0, 128), (128, 128), (256, 85)]
KEYS = P + W
EPS = 1e-5
QK_SCALE = 8.0
NEG = -1.0e30

C_ID, C_CAUSAL, C_HM, C_BAND, C_IOTA, C_MHALF, C_NHB = 0, 128, 256, 272, 464, 472, 488
NC = 616
NR, NCV = 1032, 68


def shape_constants(np):
    c = np.zeros((P, NC), np.float32)
    p, k = np.arange(P)[:, None], np.arange(P)[None, :]
    c[:, C_ID:C_ID + P] = p == k
    c[:, C_CAUSAL:C_CAUSAL + P] = p <= k
    c[:, C_HM:C_HM + H0] = p // D0 == np.arange(H0)[None, :]
    kk = np.arange(KEYS)[None, :]
    c[:, C_BAND:C_BAND + KEYS] = np.where((p <= kk) & (kk <= p + W), 0.0, NEG)
    c[:, C_IOTA:C_IOTA + E] = np.arange(E)[None, :]
    c[:, C_MHALF:C_MHALF + 16] = -0.5
    c[:, C_NHB:C_NHB + P] = np.where(p // D0 == k // D0, -0.5, 0.0)
    half = np.arange(0, D1, 2, dtype=np.float32)
    inv = (1.0 / 10000.0 ** (half / D1)).astype(np.float32)
    t = np.arange(N, dtype=np.float32)
    f = t[:, None] * inv[None, :]
    f = np.concatenate([f, f], -1).astype(np.float32)
    base = ((half + 0.4 * D1) / (1.4 * D1)).astype(np.float32)
    power = ((t - N // 2) / float(W // 2)).astype(np.float32)
    s = base[None, :] ** power[:, None]
    s = np.concatenate([s, s], -1)
    sign = np.where(np.arange(D1) < D1 // 2, -1.0, 1.0).astype(np.float32)
    rot = np.stack([np.stack([np.cos(f) * s, np.cos(f) / s], 1),
                    np.stack([np.sin(f) * s * sign, np.sin(f) / s * sign], 1)], 1)
    rot = rot.reshape(T, P, 2, 2, D1).transpose(1, 2, 0, 3, 4)
    return c, np.ascontiguousarray(rot, dtype=np.float32).reshape(P, -1)


def stream_groups(u):
    groups = [[(name, u)] for name in ("norm1", "state_T", "l1_qkv", "l1_feat", "l1_kv", "l1_num", "l1_oT", "l1_out")]
    for l in range(L):
        groups += [[("project_qk", u, l, 0)], [("project_v", u, l, 0), ("norms", u, l, 0)],
                   [("rotate", u, l, 0)], [("transpose_qk", u, l, 0)]]
        for s in range(SLOTS + HP):
            t1, ph = s // HP + 1, s % HP
            group = []
            if s < SLOTS:
                group.append(("scores", u, l, s))
            if 1 <= s <= SLOTS:
                group.append(("transpose_probs", u, l, s - 1))
            if 2 <= s <= SLOTS + 1:
                group.append(("weigh_values", u, l, s - 2))
            if s >= 5 and ph == 1:
                group.append(("normalise_out", u, l, (s - 5) // HP))
            if 1 <= s <= SLOTS:
                group.append(("probs_moved", u, l, s - 1))
            if t1 < T:
                group += [[("project_qk", u, l, t1)], [("project_v", u, l, t1), ("norms", u, l, t1)],
                          [("rotate", u, l, t1)], [("transpose_qk", u, l, t1)]][ph]
            if s >= 6 and ph == 2:
                group.append(("transpose_out", u, l, (s - 6) // HP))
            if s >= 7 and ph == 3:
                group.append(("project_out", u, l, (s - 7) // HP))
            groups.append(group)
        groups += [[("state_T", u)], [("shift_back", u, l)], [("normed_T", u, l)]]
        groups += [[("hidden", u, l, j)] for j in range(len(HC))]
        groups.append([("ffn_out", u, l)])
        if l + 1 < L:
            groups.append([("state_T", u)])
    return groups + [[("final", u)]]


def make_plan():
    plan, at = [], [0]

    def experts(k):
        for _ in range(k):
            if at[0] < EXPERT_STEPS:
                plan.append(("expert", at[0]))
                at[0] += 1

    for k in range(U * T):
        plan.append(("qkvg", k))
        if k % T == T - 1:
            plan.append(("gate_exp", k // T))
        experts(k % 2)
    for u in range(U):
        plan.append(("gates", u))
        experts(1)
    for u in range(U):
        plan.append(("gating", u))
        experts(4)
    for u in range(U):
        plan.append(("elu", u))
        experts(1)
    for u in range(U):
        plan.append(("q_T", u))
        plan.append(("states", u))
        experts(1)
    for i in range(ITEMS + 1):
        if i < ITEMS:
            if i // U % 4 == 0 and i >= 4 * U:
                plan.append(("from_state", i // (4 * U) * U + i % U))
            plan.append(("from_tile", i))
            experts(i % 2)
        if i:
            plan.append(("summed", i - 1))
            if (i - 1) // U % 4 == 3:
                plan.append(("attended", (i - 1) // (4 * U) * U + (i - 1) % U))
    for name in ("att_T", "project0"):
        for u in range(U):
            plan.append((name, u))
            experts(1)
    first, second = stream_groups(0), stream_groups(1)
    for group in first[:AHEAD]:
        plan += group
        experts(2)
    experts(EXPERT_STEPS)
    plan.append(("last_expert", 0))
    for k in range(len(first)):
        plan += second[k]
        if k + AHEAD < len(first):
            plan += first[k + AHEAD]
    return plan


def build(nc, A, out):
    with ExitStack() as ctx:
        def sb(name, shape, dt=F32):
            return ctx.enter_context(nc.sbuf_tensor(name, shape, dt))

        def sem(name):
            return ctx.enter_context(nc.semaphore(name))

        def bc(ap, axis, n):
            v = ap.unsqueeze(axis)
            return v.broadcast_to(v.shape[:axis] + (n,) + v.shape[axis + 1:])

        cst = sb("cst", [P, NC])
        ident = cst[:, C_ID:C_ID + P]
        causal = cst[:, C_CAUSAL:C_CAUSAL + P]
        headmask = cst[:, C_HM:C_HM + H0]
        band = cst[:, C_BAND:C_BAND + KEYS]
        iota = cst[:, C_IOTA:C_IOTA + E]
        mhalf = cst[:, C_MHALF:C_MHALF + 16]
        nhb = cst[:, C_NHB:C_NHB + P]
        tabs = sb("tabs", [P, L, 2, T, 2, D1])
        w0 = sb("w0", [P, 512])
        rows = sb("rows", [P, NR])
        colv = sb("colv", [P, NCV])
        bias0 = rows[:, 0:512]
        rb = rows[:, 512:520]
        bvo = rows[:, 520:776].rearrange("p (i d) -> p i d", i=2)
        b2l = rows[:, 776:1032].rearrange("p (l d) -> p l d", l=L)
        lncol = colv[:, 0:2]
        elg = colv[:, 2:18].rearrange("p (i e) -> p i e", i=2)
        b1c = colv[:, 18:50].rearrange("p (e f) -> p e f", e=E)
        lgb = colv[:, 50:54].rearrange("p (l i) -> p l i", l=L)
        b1l = colv[:, 54:66].rearrange("p (l i j) -> p l i j", l=L, i=2)
        rW = sb("rW", [P, E])
        wproj = sb("wproj", [P, P])
        b2ext = sb("b2ext", [E + 1, P])
        W1 = sb("W1", [P, E, FF])
        W2 = sb("W2", [P, E, FC, P])
        wl1 = sb("wl1", [P, 4, P])
        bl1 = sb("bl1", [P, 2])
        Rblk = sb("Rblk", [P, P])
        wqkv = sb("wqkv", [P, L, 3 * H1 * D1])
        wo = sb("wo", [P, L, HP, P])
        w1 = sb("w1", [P, L, 2 * HID])
        w2 = sb("w2", [P, L, 3, P])

        x = sb("x", [P, U, T, P])
        xn = sb("xn", [P, U, T, P])
        ring = sb("ring", [P, 2, FC * N])
        stats = sb("stats", [P, U, T, 6])
        mv = sb("mv", [P, U, T, 2])
        ve = sb("ve", [P, U, T])
        rstd = sb("rstd", [P, U, T])
        lg = sb("lg", [P, U, T, E])
        top = sb("top", [P, U, T, 8])
        topi = sb("topi", [P, U, T, 8], U32)
        topf = sb("topf", [P, U, T, 2])
        wts = sb("wts", [P, U, 4, T])
        gate_a = sb("gate_a", [P, U, T, E + 1])
        gate_b = sb("gate_b", [P, U, T, E])
        gsum = sb("gsum", [P, U, T])
        gs = sb("gs", [P, U, T])
        den0 = sb("den0", [P, U, T, H0])
        ssq = sb("ssq", [P, U, 16])
        rn = sb("rn", [P, U, 2, 16])
        mx = sb("mx", [P, U, 2, 2])
        nmx = sb("nmx", [P, U, 2, 2])
        rs = sb("rs", [P, U, 2, H1])
        rsi = sb("rsi", [P, U, H1])
        NA = 13056
        arena = sb("arena", [P, U, NA])

        def carve(sizes, at=0):
            got = {}
            for name, size in sizes:
                got[name] = arena[:, :, at:at + size]
                at += size
            assert at <= NA, at
            return got

        a0 = carve([("xhat", 512), ("xnT", 512), ("xnormT", 512), ("xhatT", 512), ("qkvg", 2048),
                    ("gn", 512), ("me", 1024), ("qk", 1024), ("vext", T * HV), ("qT", 512),
                    ("prod", 576), ("sums", HV), ("att", 512), ("attT", 512), ("gT", 512), ("S", 3 * HV), ("xe", 1024)])
        kv_at = 4 * 512
        a0["kv"] = arena[:, :, kv_at:kv_at + 2 * HV * D0]
        assert 2 * HV * D0 <= 2048 + 512
        a1 = carve([("kT", 2048), ("qT", 1024), ("qn", 1024), ("t1", 1024), ("t2", 1024),
                    ("sm", 768), ("P", 1024), ("PT", 1024), ("on", 512), ("oT", 512), ("hT", 512), ("v0", 512)])
        a2 = carve([("x1T", 512), ("qs", 512), ("ks", 512), ("sqq", 512), ("sqk", 512), ("qp", 512),
                    ("kp", 512), ("vt", 512), ("kve", HV), ("o1", 512), ("o1T", 512)])
        hid = a1["kT"][:, :, 0:1536]
        gg = a1["qn"]
        hn, hnT = a1["on"], a1["oT"]

        def tiles(ap, u, t):
            return ap[:, u, t * P:(t + 1) * P]

        def v_tile(u, t):
            return ring[:, u, t * 512:(t + 1) * 512] if t else a1["v0"][:, u]

        ps = ctx.enter_context(nc.psum_tensor("ps", [P, 8, 512], F32))

        def bank_a(u):
            return ps[:, 2 * u, :]

        def bank_b(u):
            return ps[:, 2 * u + 1, :]

        def bank_y(n):
            return ps[:, 4 + n % 2, :]

        def bank_h(hc):
            return ps[:, 6 + hc % 2, :]

        def cols(ap, t, w=P):
            return ap[:, t * w:(t + 1) * w]

        small_loaded = sem("small_loaded")
        first_loaded = sem("first_loaded")
        experts_loaded = sem("experts_loaded")
        l1_loaded = sem("l1_loaded")
        layers_loaded = sem("layers_loaded")
        tabs_made = sem("tabs_made")

        loop_sems = []

        def lsem(name):
            s = sem(name)
            loop_sems.append(s)
            return s

        def lsem2(name):
            return [lsem(name + "0"), lsem(name + "1")]

        dve_step = lsem("dve_step")
        xhat_ready = lsem("xhat_ready"); norm_transposed = lsem("norm_transposed"); normT_ready = lsem("normT_ready")
        logits_done = lsem("logits_done"); logits_read = lsem("logits_read")
        top2_ready = lsem("top2_ready"); ew_ready = lsem("ew_ready"); gates_ready = lsem("gates_ready")
        qkvg_done = lsem("qkvg_done"); qkvg_biased = lsem("qkvg_biased")
        gate_exp = lsem("gate_exp"); qk_min = lsem("qk_min"); qk_exp = lsem("qk_exp")
        qk_ready = lsem("qk_ready"); v_ready = lsem("v_ready")
        qT_done = lsem("qT_done"); qT_ready = lsem("qT_ready")
        state_done = lsem("state_done"); state_ready = lsem("state_ready")
        kv_ready = lsem("kv_ready"); tile_part_done = lsem("tile_part_done"); times_q = lsem("times_q")
        state_part_done = lsem("state_part_done"); att_ready = lsem("att_ready")
        attT_done = lsem("attT_done"); attT_ready = lsem("attT_ready"); proj_done = lsem("proj_done")
        x_base = lsem("x_base")
        xe_ready = lsem("xe_ready"); h0_done = lsem("h0_done"); gelu_done = lsem("gelu_done")
        y0_done = lsem("y0_done"); y_added = lsem("y_added")
        zeros_ready = lsem("zeros_ready")
        l1_qkv = lsem("l1_qkv"); l1_qs = lsem("l1_qs"); l1_sq = lsem("l1_sq"); l1_v = lsem("l1_v")
        l1_feat = lsem("l1_feat"); l1_exp = lsem("l1_exp"); l1_kv = lsem("l1_kv"); l1_kve = lsem("l1_kve")
        l1_num = lsem("l1_num"); l1_o = lsem("l1_o"); l1_oT_done = lsem("l1_oT_done")
        l1_oT = lsem("l1_oT"); l1_out = lsem("l1_out"); l1_bo = lsem("l1_bo"); x_l1 = lsem("x_l1")
        x_loaded = lsem2("x_loaded")
        var_ready = lsem2("var_ready"); rstd_ready = lsem2("rstd_ready"); xn_ready = lsem2("xn_ready")
        y_transposed = lsem2("y_transposed"); hT_ready = lsem2("hT_ready")
        qk1_done = lsem2("qk1_done"); raw_ready = lsem2("raw_ready"); sq_ready = lsem2("sq_ready")
        ss_ready = lsem2("ss_ready"); rn_ready = lsem2("rn_ready"); rot2_ready = lsem2("rot2_ready")
        rot_sum = lsem2("rot_sum"); rotated = lsem2("rotated"); v1_done = lsem2("v1_done"); v1_ready = lsem2("v1_ready")
        qkT1_done = lsem2("qkT1_done"); qkT1_ready = lsem2("qkT1_ready")
        scores1_done = lsem2("scores1_done"); masked = lsem2("masked"); exp_done = lsem2("exp_done")
        PT_done = lsem2("PT_done"); PT_ready = lsem2("PT_ready"); av_done = lsem2("av_done")
        o_normed = lsem2("o_normed"); oT_done = lsem2("oT_done"); oT_ready = lsem2("oT_ready")
        wo_done = lsem2("wo_done"); y_updated = lsem2("y_updated")
        h_back = lsem2("h_back"); hn_ready = lsem2("hn_ready"); hnT_done = lsem2("hnT_done")
        hnT_ready = lsem2("hnT_ready"); g_done = lsem2("g_done"); a_done = lsem2("a_done")
        gelu1_done = lsem2("gelu1_done"); hid_ready = lsem2("hid_ready"); ffn_out = lsem2("ffn_out")
        y_b2 = lsem2("y_b2"); y_final = lsem2("y_final")
        out_ready = lsem("out_ready"); out_stored = lsem("out_stored")

        rot_raw = arena[:, 0, 0:1024].rearrange("p (c t q d) -> p c t q d", c=2, t=T, q=2)
        qksc = arena[:, 0, 1024:1536].rearrange("p (c l q d) -> p c l q d", c=2, l=L, q=2)
        R8 = arena[:, 0, 1536:1536 + D0]
        bl1_raw = colv[:, 66:68]
        HD = D1 // 2

        with nc.Block() as block:
            @block.sync
            def _(sp):
                small = [(cst[:], A["cst"]), (rows[:], A["rows"].partition_broadcast(P)), (colv[:], A["colv"]),
                         (arena[:, 0, 0:1024], A["rot"]), (arena[:, 0, 1024:1536], A["qksc"].partition_broadcast(P)),
                         (R8, A["L1_attn_R"].partition_broadcast(H0))]
                for dst, src in small:
                    sp.dma_start(dst, src).then_inc(small_loaded, 16)
                first = [(w0[:, 0:384], A["L0_attn_w_qkv"]), (w0[:, 384:512], A["L0_attn_w_gate"]),
                         (rW[:], A["L0_ffn_router_W"]),
                         (wproj[:], A["L0_attn_w_proj"]), (b2ext[0:E, :], A["L0_ffn_b2"]),
                         (b2ext[E:E + 1, :], A["L0_attn_b_proj"].unsqueeze(0))]
                for dst, src in first:
                    sp.dma_start(dst, src).then_inc(first_loaded, 16)
                sp.dma_start(W1[:], A["L0_ffn_W1"].rearrange("e h f -> h e f")).then_inc(experts_loaded, 16)
                for e in range(E):
                    sp.dma_start(W2[:, e], A["L0_ffn_W2"][e].rearrange("(f p) h -> p f h", p=P)).then_inc(experts_loaded, 16)

            @block.gpsimd
            def _(pool):
                for i, name in enumerate(("WqT", "WkT", "WvT", "WoT")):
                    pool.dma_start(wl1[:, i, :], A[name]).then_inc(l1_loaded, 16)
                pool.dma_start(wqkv[:], A["L1_ffn_wqkv"].rearrange("l h n -> h l n")).then_inc(layers_loaded, 16)
                pool.dma_start(w1[:], A["L1_ffn_w1"].rearrange("l h n -> h l n")).then_inc(layers_loaded, 16)
                for l in range(L):
                    pool.dma_start(wo[:, l], A["L1_ffn_wo"][l].rearrange("(c p) h -> p c h", p=P)).then_inc(layers_loaded, 16)
                    for j, (c0, n) in enumerate(HC):
                        pool.dma_start(w2[0:n, l, j], A["L1_ffn_w2"][l][c0:c0 + n]).then_inc(layers_loaded, 16)

            @block.vector
            def _(dve):
                dve.wait_ge(small_loaded, 16 * 6)
                for l in range(L):
                    for c in range(2):
                        for q in range(2):
                            nc.vector.tensor_tensor(tabs[:, l, c, :, q, :], rot_raw[:, c, :, q, :],
                                                    bc(qksc[:, c, l, q, :], 1, T), ALU.mult)
                nc.vector.tensor_scalar(bl1[:], bl1_raw, D0 ** -0.5, None, ALU.mult)
                nc.vector.tensor_tensor(Rblk[:].rearrange("p (h d) -> p h d", h=H0), bc(R8, 1, H0),
                                        bc(headmask, 2, D0), ALU.mult).then_inc(tabs_made, 1)
                dve.wait_ge(tabs_made, 1)
        nc.all_engine_barrier()
        N_FIRST, N_EXPERTS, N_L1, N_LAYERS = 16 * 6, 16 * (1 + E), 16 * 4, 16 * (2 + L * 4)

        xv = A["x"].rearrange("b (t p) d -> p b t d", p=P)
        ov = out.rearrange("b (t p) d -> p b t d", p=P)

        PREP, TB, OB, SCORE = (0, 1), (2, 3), (4, 5), (6, 7)
        LIN = ((0, 1, 2, 3), (0, 1, 3, 5))

        def lin(u, i):
            return ps[:, LIN[u][i], :]

        def keys_of(t):
            return (t * P - W, (t + 1) * P, 0) if t else (0, P, W)

        plan = make_plan()

        def item(i):
            return i // (4 * U), i // U % 4, i % U

        def kv_cols(u, t, h0, h1):
            at = (t % 2) * HV * D0
            return a0["kv"][:, u, at + h0 * 72:at + h1 * 72]

        with nc.Fori(0, B // U) as it:
            with nc.Block() as block:

                @block.sync
                def _(sp):
                    for u in range(U):
                        sp.dma_start(x[:, u], xv[:, bass.ds(it * U + u, 1)].rearrange("p b t d -> p (b t) d")).then_inc(x_loaded[u], 16)
                    for u in range(U):
                        sp.wait_ge(out_ready, u + 1)
                        sp.dma_start(ov[:, bass.ds(it * U + u, 1)].rearrange("p b t d -> p (b t) d"), x[:, u]).then_inc(out_stored, 16)
                    sp.wait_ge(out_stored, 16 * U)

                @block.gpsimd
                def _(pool):
                    g = nc.gpsimd

                    def rsqrt_var(u, n):
                        pool.wait_ge(var_ready[u], n + 1)
                        g.tensor_tensor(rstd[:, u], ve[:, u], mhalf[:, 0:T], ALU.pow).then_inc(rstd_ready[u], 1)

                    def ones_behind_v(u):
                        pool.wait_ge(qkvg_biased, T * (u + 1))
                        v = a0["vext"][:, u].rearrange("p (t h d) -> p t h d", t=T, h=H0)
                        g.memset(v[:, :, :, D0:D0 + 1], 1.0)
                        src = a0["qkvg"][:, u].rearrange("p (t c) -> p t c", t=T)[:, :, 256:384]
                        for t in range(T):
                            last = g.tensor_copy(v[:, t, :, 0:D0], src[:, t].rearrange("p (h d) -> p h d", h=H0))
                        last.then_inc(v_ready, 1)

                    def k_times_v(n):
                        t, u = n // U, n % U
                        if t == 0:
                            pool.wait_ge(qk_ready, u + 1)
                            pool.wait_ge(v_ready, u + 1)
                        if t >= 2:
                            pool.wait_ge(tile_part_done, ((t - 2) * 4 + 3) * U + u + 1)
                        k = a0["qk"][:, u, t * 256 + P:(t + 1) * 256].rearrange("p (h d) -> p h d", h=H0)
                        v = a0["vext"][:, u, t * HV:(t + 1) * HV].rearrange("p (h m) -> p h m", h=H0)
                        g.tensor_tensor(kv_cols(u, t, 0, H0).rearrange("p (h d m) -> p h d m", h=H0, d=D0),
                                        bc(k, 3, D0 + 1), bc(v, 2, D0), ALU.mult).then_inc(kv_ready, 1)

                    def expert_input(n):
                        u, e = n // E, n % E
                        if n == 0:
                            pool.wait_ge(experts_loaded, N_EXPERTS)
                        if e == 0:
                            pool.wait_ge(normT_ready, 2 * u + 2)
                        else:
                            pool.wait_ge(h0_done, 4 * (n - 1))
                        g.tensor_scalar(a0["xe"][:, u, (e % 2) * N:(e % 2 + 1) * N], a0["xhatT"][:, u],
                                        elg[:, 0, e:e + 1], elg[:, 1, e:e + 1], ALU.mult, ALU.add).then_inc(xe_ready, 1)

                    def rotate2(u, l, t):
                        pool.wait_ge(raw_ready[u], l * T + t + 1)
                        q = a1["qn"][:, u].rearrange("p (q h d) -> p q h d", q=2, h=H1)
                        o = a1["t2"][:, u].rearrange("p (q h d) -> p q h d", q=2, h=H1)
                        for a, b in ((0, HD), (HD, 0)):
                            last = g.tensor_tensor(o[:, :, :, a:a + HD], q[:, :, :, b:b + HD],
                                                   bc(tabs[:, l, 1, t, :, a:a + HD], 2, H1), ALU.mult)
                        last.then_inc(rot2_ready[u], 1)

                    def inverse_norms(u, l, t):
                        pool.wait_ge(ss_ready[u], l * T + t + 1)
                        g.tensor_tensor(rn[:, u, t % 2], ssq[:, u], mhalf, ALU.pow).then_inc(rn_ready[u], 1)

                    def scale_k(u, l, t):
                        pool.wait_ge(rot_sum[u], l * T + t + 1)
                        pool.wait_ge(rn_ready[u], l * T + t + 1)
                        k = a1["t1"][:, u, 512:1024].rearrange("p (h d) -> p h d", h=H1)
                        g.tensor_tensor(k, k, bc(rn[:, u, t % 2, H1:16], 2, D1), ALU.mult).then_inc(rotated[u], 1)

                    for n in range(2):
                        for u in range(U):
                            rsqrt_var(u, n)
                    expert_input(0)
                    for name, i, *rest in plan:
                        if name == "expert" and i % FC == 0 and i // FC + 1 < U * E:
                            expert_input(i // FC + 1)
                        if name == "gates":
                            ones_behind_v(i)
                        if name == "elu":
                            k_times_v(i)
                        if name == "from_tile" and i % (4 * U) < U and i + 4 * U < ITEMS:
                            k_times_v((i // (4 * U) + 1) * U + i % U)
                        if name == "norm1":
                            rsqrt_var(i, 2)
                            if i == 0:
                                pool.wait_ge(l1_loaded, N_L1)
                            pool.wait_ge(xn_ready[i], 2)
                            g.memset(a1["hT"][:, i, 0:1], 0.0)
                            g.memset(a1["P"][:, i].rearrange("p (s k) -> p s k", k=2 * P)[:, :, 0:W], 0.0)
                            g.tensor_copy(a2["kve"][:, i, P:HV], headmask).then_inc(zeros_ready, 1)
                            g.tensor_tensor(x[:, i], x[:, i], bc(bvo[:, 1, :], 1, T), ALU.add).then_inc(l1_bo, 1)
                        if name == "l1_qkv":
                            for c, (a, b) in enumerate((("qs", "sqq"), ("ks", "sqk"))):
                                pool.wait_ge(l1_qs, 2 * i + c + 1)
                                g.tensor_tensor(a2[b][:, i], a2[a][:, i], a2[a][:, i], ALU.mult).then_inc(l1_sq, 1)
                        if name == "project_qk":
                            if i == 0 and rest == [0, 0]:
                                pool.wait_ge(layers_loaded, N_LAYERS)
                            rotate2(i, *rest)
                        if name == "norms":
                            inverse_norms(i, *rest)
                        if name == "rotate":
                            scale_k(i, *rest)
                        if name == "shift_back":
                            l = rest[0]
                            pool.wait_ge(y_transposed[i], 2 + 2 * l)
                            g.tensor_tensor(xn[:, i], xn[:, i], bc(b2l[:, l], 1, T), ALU.add).then_inc(y_b2[i], 1)
                            rsqrt_var(i, 3 + l)

                @block.scalar
                def _(act):
                    a = nc.scalar

                    act.wait_ge(first_loaded, N_FIRST)
                    for u in range(U):
                        act.wait_ge(norm_transposed, 2 * u + 1)
                        a.activation(a0["xnT"][:, u], bank_a(u), ACT.Copy).then_inc(normT_ready, 1)
                        act.wait_ge(norm_transposed, 2 * u + 2)
                        a.activation(a0["xnormT"][:, u], bank_b(u), ACT.Identity, bias=lncol[:, 1:2], scale=lncol[:, 0:1])
                        a.activation(a0["xhatT"][:, u], bank_b(u), ACT.Copy).then_inc(normT_ready, 1)
                    for u in range(U):
                        act.wait_ge(top2_ready, u + 1)
                        a.activation(wts[:, u, 1], wts[:, u, 0], ACT.Exp).then_inc(ew_ready, 1)

                    def shifted(u, inst):
                        act.wait_ge(y_transposed[u], inst + 1)
                        if inst == 0:
                            a.activation(a2["x1T"][:, u], ps[:, TB[u]], ACT.Copy)
                            act.wait_ge(zeros_ready, u + 1)
                        a.activation(a1["hT"][0:64, u], ps[0:64, TB[u]], ACT.Copy)
                        a.activation(a1["hT"][64:128, u, 1:N], ps[64:128, TB[u], 0:N - 1], ACT.Copy).then_inc(hT_ready[u], 1)

                    def raw(u, l, t):
                        pi = l * T + t
                        act.wait_ge(qk1_done[u], pi + 1)
                        if pi:
                            act.wait_ge(rot2_ready[u], pi)
                            act.wait_ge(rot_sum[u], pi)
                        if pi and t == 0:
                            act.wait_ge(hid_ready[u], 3 * l)
                        a.activation(a1["qn"][:, u].rearrange("p (q c) -> p q c", q=2), ps[:, PREP[0]:PREP[1] + 1, :], ACT.Copy).then_inc(raw_ready[u], 1)

                    def squares(u, l, t):
                        pi = l * T + t
                        act.wait_ge(raw_ready[u], pi + 1)
                        if pi:
                            act.wait_ge(qkT1_done[u], 2 * pi)
                        a.activation(a1["t1"][:, u], a1["qn"][:, u], ACT.Square).then_inc(sq_ready[u], 1)

                    def values(u, l, t):
                        act.wait_ge(v1_done[u], l * T + t + 1)
                        a.activation(v_tile(u, t), ps[:, PREP[0], :], ACT.Copy).then_inc(v1_ready[u], 1)

                    def qk_transposed(u, l, t):
                        pi = l * T + t
                        act.wait_ge(qkT1_done[u], 2 * pi + 1)
                        a.activation(a1["qT"][:, u, (t % 2) * 512:(t % 2 + 1) * 512], ps[:, PREP[1], :], ACT.Copy).then_inc(qkT1_ready[u], 1)
                        act.wait_ge(qkT1_done[u], 2 * pi + 2)
                        kv = a1["kT"][:, u].rearrange("p (c k) -> p c k", c=HP)[:, :, t * P:(t + 1) * P]
                        a.activation(kv, ps[:, PREP[0], :].rearrange("p (c k) -> p c k", c=HP), ACT.Copy).then_inc(qkT1_ready[u], 1)

                    def exps(u, l, s):
                        t, hp = s // HP, s % HP
                        ui = l * SLOTS + s
                        k0, k1, _ = keys_of(t)
                        n = k1 - k0
                        act.wait_ge(masked[u], ui + 1)
                        if ui >= 2:
                            act.wait_ge(PT_done[u], ui - 1)
                        for i in range(2):
                            smv = a1["sm"][:, u].rearrange("p (r i k) -> p r i k", r=2, i=2)[:, s % 2, i, 0:n]
                            pv = a1["P"][:, u].rearrange("p (r i k) -> p r i k", r=2, i=2)[:, s % 2, i, 2 * P - n:2 * P]
                            last = a.activation(pv, smv, ACT.Exp, scale=rn[:, u, t % 2, 2 * hp + i:2 * hp + i + 1],
                                                bias=nmx[:, u, s % 2, i:i + 1],
                                                accum_out=rs[:, u, t % 2, 2 * hp + i:2 * hp + i + 1])
                        last.then_inc(exp_done[u], 1)

                    def probs_moved(u, l, s):
                        t, ui = s // HP, l * SLOTS + s
                        act.wait_ge(PT_done[u], ui + 1)
                        if ui >= 2:
                            act.wait_ge(av_done[u], ui - 1)
                        b0 = 0 if t else 1
                        dst = a1["PT"][:, u, (s % 2) * 512:(s % 2 + 1) * 512].rearrange("p (i b k) -> p i b k", i=2, b=2)[:, :, b0:2]
                        a.activation(dst, ps[:, TB[u], :].rearrange("p (i b k) -> p i b k", i=2, b=2)[:, :, b0:2], ACT.Copy).then_inc(PT_ready[u], 1)

                    shifts = [0, 0]
                    for name, i, *rest in plan:
                        if name == "expert" and i // FC < U * E:
                            n, f = i // FC, i % FC
                            if f == 0 and n == 0:
                                act.wait_ge(experts_loaded, N_EXPERTS)
                            if f == 0 and n >= 2:
                                act.wait_ge(y0_done, n - 1)
                            act.wait_ge(h0_done, i + 1)
                            a.activation(ring[:, n % 2, f * N:(f + 1) * N], bank_h(i), ACT.Gelu,
                                         bias=b1c[:, n % E, f:f + 1]).then_inc(gelu_done, 1)
                        if name == "gate_exp":
                            act.wait_ge(qkvg_biased, T * (i + 1))
                            src = a0["qkvg"][:, i].rearrange("p (t c) -> p t c", t=T)[:, :, 384:512]
                            a.activation(a0["gn"][:, i].rearrange("p (t c) -> p t c", t=T), src, ACT.Exp, scale=-1.0).then_inc(gate_exp, 1)
                        if name == "elu":
                            act.wait_ge(qk_min, i + 1)
                            a.activation(a0["me"][:, i], a0["me"][:, i], ACT.Exp).then_inc(qk_exp, 1)
                        if name == "q_T":
                            act.wait_ge(qT_done, i + 1)
                            a.activation(a0["qT"][:, i], bank_a(i), ACT.Copy).then_inc(qT_ready, 1)
                        if name == "att_T":
                            act.wait_ge(attT_done, 2 * i + 1)
                            a.activation(a0["attT"][:, i], bank_a(i), ACT.Copy).then_inc(attT_ready, 1)
                            act.wait_ge(attT_done, 2 * i + 2)
                            a.activation(a0["gT"][0:E + 1, i], bank_b(i)[0:E + 1], ACT.Copy).then_inc(attT_ready, 1)
                        if name == "state_T":
                            shifted(i, shifts[i])
                            shifts[i] += 1
                        if name == "l1_qkv":
                            for c, dst in enumerate(("qs", "ks")):
                                act.wait_ge(l1_qkv, 3 * i + c + 1)
                                a.activation(a2[dst][:, i], lin(i, c), ACT.Identity, bias=bl1[:, c:c + 1],
                                             scale=D0 ** -0.5).then_inc(l1_qs, 1)
                        if name == "l1_feat":
                            for c, dst in enumerate(("qp", "kp")):
                                act.wait_ge(l1_feat, 2 * i + c + 1)
                                a.activation(a2[dst][:, i], lin(i, c), ACT.Exp).then_inc(l1_exp, 1)
                        if name == "l1_oT":
                            act.wait_ge(l1_oT_done, i + 1)
                            a.activation(a2["o1T"][:, i], lin(i, 0), ACT.Copy).then_inc(l1_oT, 1)
                        if name == "project_qk":
                            if i == 0 and rest == [0, 0]:
                                act.wait_ge(layers_loaded, N_LAYERS)
                            raw(i, *rest)
                            squares(i, *rest)
                        if name == "project_v":
                            values(i, *rest)
                        if name == "transpose_qk":
                            qk_transposed(i, *rest)
                        if name == "scores":
                            exps(i, *rest)
                        if name == "probs_moved" and i == 0:
                            probs_moved(i, *rest)
                        if name == "transpose_out":
                            pi = rest[0] * T + rest[1]
                            act.wait_ge(oT_done[i], pi + 1)
                            a.activation(a1["oT"][:, i], ps[:, TB[i], :], ACT.Copy).then_inc(oT_ready[i], 1)
                        if name == "normed_T":
                            l = rest[0]
                            act.wait_ge(hnT_done[i], l + 1)
                            a.activation(hnT[:, i], ps[:, TB[i], :], ACT.Identity, bias=lgb[:, l, 1:2], scale=lgb[:, l, 0:1]).then_inc(hnT_ready[i], 1)
                        if name == "hidden":
                            l, j = rest
                            gi, n = l * 3 + j, HC[j][1]
                            act.wait_ge(g_done[i], gi + 1)
                            if j == 2:
                                act.wait_ge(hid_ready[i], gi - 1)
                            a.activation(gg[0:n, i, (j % 2) * N:(j % 2 + 1) * N], ps[0:n, PREP[0]], ACT.Gelu,
                                         bias=b1l[0:n, l, 1, j:j + 1]).then_inc(gelu1_done[i], 1)

                @block.vector
                def _(dve):
                    v = nc.vector
                    steps = [0]

                    def step(ins):
                        steps[0] += 1
                        return ins.then_inc(dve_step, 1)

                    def settle():
                        dve.wait_ge(dve_step, steps[0])

                    def norm_stats(u, src):
                        for t in range(T):
                            last = v.bn_stats(stats[:, u, t], src(t))
                        step(last)
                        settle()
                        for t in range(T):
                            last = v.bn_aggr(mv[:, u, t], stats[:, u, t])
                        step(last)
                        settle()
                        v.tensor_scalar(ve[:, u], mv[:, u, :, 1], EPS, None, ALU.add).then_inc(var_ready[u], 1)

                    def norm_apply(n, u, dst, src, ready):
                        dve.wait_ge(rstd_ready[u], n + 1)
                        for t in range(T):
                            last = v.tensor_scalar(dst(t), src(t), mv[:, u, t, 0:1], rstd[:, u, t:t + 1], ALU.subtract, ALU.mult)
                        last.then_inc(ready, 1)

                    for u in range(U):
                        dve.wait_ge(x_loaded[u], 16)
                        norm_stats(u, lambda t: x[:, u, t])
                    for u in range(U):
                        norm_apply(0, u, lambda t: xn[:, u, t], lambda t: x[:, u, t], xn_ready[u])
                    for u in range(U):
                        dve.wait_ge(xn_ready[u], 1)
                        norm_stats(u, lambda t: xn[:, u, t])
                    for u in range(U):
                        norm_apply(1, u, lambda t: tiles(a0["xhat"], u, t), lambda t: xn[:, u, t], xhat_ready)

                    for u in range(U):
                        dve.wait_ge(logits_done, u + 1)
                        v.tensor_tensor(lg[:, u], bank_a(u)[:, 0:T * E].rearrange("p (t e) -> p t e", t=T),
                                        bc(rb, 1, T), ALU.add).then_inc(logits_read, 1)
                        dve.wait_ge(logits_read, u + 1)
                        for t in range(T):
                            last = v.max(top[:, u, t], lg[:, u, t])
                        step(last)
                        settle()
                        v.tensor_tensor(wts[:, u, 0], top[:, u, :, 1], top[:, u, :, 0], ALU.subtract).then_inc(top2_ready, 1)
                        for t in range(T):
                            last = v.max_index(topi[:, u, t], top[:, u, t], lg[:, u, t])
                        step(last)
                        settle()
                        step(v.tensor_copy(topf[:, u], topi[:, u, :, 0:2]))

                    x_written = [None, None]

                    def x_settled(u):
                        if x_written[u]:
                            dve.wait_ge(*x_written[u])

                    def biased(k):
                        u, t = k // T, k % T
                        dve.wait_ge(qkvg_done, k + 1)
                        v.tensor_tensor(a0["qkvg"][:, u, t * 512:(t + 1) * 512], ps[:, k % 4, :], bias0, ALU.add).then_inc(qkvg_biased, 1)

                    def gates(u):
                        dve.wait_ge(ew_ready, u + 1)
                        step(v.tensor_scalar(wts[:, u, 2], wts[:, u, 1], 1.0, None, ALU.add))
                        settle()
                        step(v.reciprocal(wts[:, u, 2], wts[:, u, 2]))
                        settle()
                        step(v.tensor_tensor(wts[:, u, 3], wts[:, u, 1], wts[:, u, 2], ALU.mult))
                        settle()
                        v.tensor_tensor(gsum[:, u], wts[:, u, 2], wts[:, u, 3], ALU.add)
                        v.memset(gate_a[:, u, :, E:E + 1], 1.0)
                        for t in range(T):
                            v.tensor_scalar(gate_a[:, u, t, 0:E], iota, topf[:, u, t, 0:1], wts[:, u, 2, t:t + 1], ALU.is_equal, ALU.mult)
                            last = v.tensor_scalar(gate_b[:, u, t], iota, topf[:, u, t, 1:2], wts[:, u, 3, t:t + 1], ALU.is_equal, ALU.mult)
                        step(last)
                        settle()
                        v.tensor_tensor(gate_a[:, u, :, 0:E], gate_a[:, u, :, 0:E], gate_b[:, u], ALU.add).then_inc(gates_ready, 1)
                        for t in range(T):
                            last = v.scalar_tensor_tensor(out=x[:, u, t], in0=xn[:, u, t], scalar=gsum[:, u, t:t + 1],
                                                          in1=x[:, u, t], op0=ALU.mult, op1=ALU.add)
                        step(last)
                        x_written[u] = (dve_step, steps[0])
                        dve.wait_ge(gates_ready, u + 1)

                    def gating(u):
                        gn = a0["gn"][:, u]
                        gn3 = gn.rearrange("p (t c) -> p t c", t=T)
                        qk3 = a0["qkvg"][:, u].rearrange("p (t c) -> p t c", t=T)[:, :, 0:256]
                        dve.wait_ge(gate_exp, u + 1)
                        step(v.tensor_scalar(gn, gn, 1.0, None, ALU.add))
                        settle()
                        step(v.reciprocal(gn, gn))
                        settle()
                        step(v.reduce_sum(gs[:, u], gn3, AX_X))
                        settle()
                        step(v.tensor_scalar(gs[:, u], gs[:, u], 1.0 / P, EPS, ALU.mult, ALU.add))
                        settle()
                        step(v.reciprocal(gs[:, u], gs[:, u]))
                        settle()
                        step(v.tensor_tensor(gn3, gn3, bc(gs[:, u], 2, P), ALU.mult))
                        settle()
                        for i in range(2):
                            last = v.tensor_tensor(qk3[:, :, i * P:(i + 1) * P], qk3[:, :, i * P:(i + 1) * P], gn3, ALU.mult)
                        step(last)
                        settle()
                        v.tensor_scalar(a0["me"][:, u].rearrange("p (t c) -> p t c", t=T), qk3, 0.0, None, ALU.min).then_inc(qk_min, 1)

                    def elu(u):
                        qk3 = a0["qkvg"][:, u].rearrange("p (t c) -> p t c", t=T)[:, :, 0:256]
                        dve.wait_ge(qk_exp, u + 1)
                        v.scalar_tensor_tensor(out=a0["qk"][:, u].rearrange("p (t c) -> p t c", t=T), in0=qk3, scalar=0.0,
                                               in1=a0["me"][:, u].rearrange("p (t c) -> p t c", t=T),
                                               op0=ALU.max, op1=ALU.add).then_inc(qk_ready, 1)

                    def states(u):
                        dve.wait_ge(state_done, u + 1)
                        v.tensor_tensor(a0["S"][:, u].rearrange("p (c h d) -> p c h d", c=3, h=H0),
                                        bank_b(u)[:, 0:3 * HV].rearrange("p (c h d) -> p c h d", c=3, h=H0),
                                        bc(bc(headmask, 2, D0 + 1), 1, 3), ALU.mult).then_inc(state_ready, 1)

                    def times_q_of(i):
                        t, hg, u = item(i)
                        dve.wait_ge(tile_part_done, i + 1)
                        q = a0["qk"][:, u, t * 256 + hg * 32:t * 256 + (hg + 1) * 32]
                        v.tensor_tensor(a0["prod"][:, u, (hg % 2) * 288:(hg % 2 + 1) * 288].rearrange("p (c m) -> p c m", m=D0 + 1),
                                        bank_a(u)[:, 0:288].rearrange("p (c m) -> p c m", m=D0 + 1), bc(q, 2, D0 + 1),
                                        ALU.mult).then_inc(times_q, 1)

                    def summed(i):
                        t, hg, u = item(i)
                        dve.wait_ge(times_q, i + 1)
                        step(v.reduce_sum(a0["sums"][:, u, hg * 36:(hg + 1) * 36].rearrange("p (h m) -> p h m", h=4),
                                          a0["prod"][:, u, (hg % 2) * 288:(hg % 2 + 1) * 288].rearrange("p (h d m) -> p h m d", h=4, d=D0), AX_X))

                    def attended(n):
                        t, u = n // U, n % U
                        settle()
                        o = a0["sums"][:, u]
                        if t:
                            dve.wait_ge(state_part_done, n - U + 1)
                            step(v.tensor_tensor(o, o, bank_b(u)[:, 0:HV], ALU.add))
                            settle()
                        o = o.rearrange("p (h d) -> p h d", h=H0)
                        step(v.tensor_scalar(den0[:, u, t], o[:, :, D0], EPS, None, ALU.add))
                        settle()
                        step(v.reciprocal(den0[:, u, t], den0[:, u, t]))
                        settle()
                        v.tensor_tensor(tiles(a0["att"], u, t).rearrange("p (h d) -> p h d", h=H0), o[:, :, 0:D0],
                                        bc(den0[:, u, t], 2, D0), ALU.mult).then_inc(att_ready, 1)

                    def projected(u):
                        dve.wait_ge(proj_done, u + 1)
                        x_settled(u)
                        v.tensor_tensor(x[:, u].rearrange("p t d -> p (t d)"), x[:, u].rearrange("p t d -> p (t d)"),
                                        bank_a(u), ALU.add).then_inc(x_base, 1)
                        x_written[u] = (x_base, u + 1)

                    def expert_added(n):
                        u, e = n // E, n % E
                        dve.wait_ge(y0_done, n + 1)
                        x_settled(u)
                        for t in range(T):
                            last = v.scalar_tensor_tensor(out=x[:, u, t], in0=cols(bank_y(n), t),
                                                          scalar=gate_a[:, u, t, e:e + 1], in1=x[:, u, t],
                                                          op0=ALU.mult, op1=ALU.add)
                        last.then_inc(y_added, 1)
                        x_written[u] = (y_added, n + 1)

                    def sums(u, l, t):
                        dve.wait_ge(sq_ready[u], l * T + t + 1)
                        step(v.reduce_sum(ssq[:, u], a1["t1"][:, u].rearrange("p (g d) -> p g d", d=D1), AX_X))
                        settle()
                        v.tensor_scalar(ssq[:, u, 0:H1], ssq[:, u, 0:H1], 1e-24, QK_SCALE ** -2, ALU.max, ALU.mult)
                        v.tensor_scalar(ssq[:, u, H1:16], ssq[:, u, H1:16], 1e-24, None, ALU.max).then_inc(ss_ready[u], 1)

                    rotate1_step = [0, 0]

                    def rotate1(u, l, t):
                        step(v.tensor_tensor(a1["t1"][:, u].rearrange("p (q h d) -> p q h d", q=2, h=H1),
                                             a1["qn"][:, u].rearrange("p (q h d) -> p q h d", q=2, h=H1),
                                             bc(tabs[:, l, 0, t], 2, H1), ALU.mult))
                        rotate1_step[u] = steps[0]

                    def rotate(u, l, t):
                        dve.wait_ge(rot2_ready[u], l * T + t + 1)
                        dve.wait_ge(dve_step, rotate1_step[u])
                        v.tensor_tensor(a1["t1"][:, u], a1["t1"][:, u], a1["t2"][:, u], ALU.add).then_inc(rot_sum[u], 1)

                    def mask_max(u, l, s):
                        t, hp = s // HP, s % HP
                        ui = l * SLOTS + s
                        k0, k1, b0 = keys_of(t)
                        n = k1 - k0
                        dve.wait_ge(scores1_done[u], ui + 1)
                        if ui >= 2:
                            dve.wait_ge(exp_done[u], ui - 1)
                        if hp == 0:
                            dve.wait_ge(rn_ready[u], l * T + t + 1)
                        for i in range(2):
                            smv = a1["sm"][:, u].rearrange("p (r i k) -> p r i k", r=2, i=2)[:, s % 2, i, 0:n]
                            last = v.tensor_tensor_reduce(out=smv, in0=ps[:, SCORE[i], 0:n],
                                                          in1=band[:, b0:b0 + n], scale=1.0, scalar=3 * NEG,
                                                          op0=ALU.add, op1=ALU.max, accum_out=mx[:, u, s % 2, i:i + 1])
                        step(last)
                        settle()
                        v.scalar_tensor_tensor(out=nmx[:, u, s % 2], in0=mx[:, u, s % 2], scalar=-1.0,
                                               in1=rn[:, u, t % 2, 2 * hp:2 * hp + 2], op0=ALU.mult, op1=ALU.mult).then_inc(masked[u], 1)

                    def probs_moved(u, l, s):
                        t, ui = s // HP, l * SLOTS + s
                        dve.wait_ge(PT_done[u], ui + 1)
                        if ui >= 2:
                            dve.wait_ge(av_done[u], ui - 1)
                        b0 = 0 if t else 1
                        dst = a1["PT"][:, u, (s % 2) * 512:(s % 2 + 1) * 512].rearrange("p (i b k) -> p i b k", i=2, b=2)[:, :, b0:2]
                        v.tensor_copy(dst, ps[:, TB[u], :].rearrange("p (i b k) -> p i b k", i=2, b=2)[:, :, b0:2]).then_inc(PT_ready[u], 1)

                    for name, i, *rest in plan:
                        if name == "expert" and i % FC == 1 and i >= 2 * FC + 1:
                            expert_added(i // FC - 2)
                        if name == "last_expert":
                            expert_added(U * E - 1)
                        if name == "qkvg":
                            biased(i)
                        if name == "gates":
                            gates(i)
                        if name == "gating":
                            gating(i)
                        if name == "elu":
                            elu(i)
                        if name == "states":
                            states(i)
                        if name == "from_tile":
                            times_q_of(i)
                        if name == "summed":
                            summed(i)
                        if name == "attended":
                            attended(i)
                        if name == "project0":
                            projected(i)
                        if name == "norm1":
                            x_settled(i)
                            norm_stats(i, lambda t: x[:, i, t])
                            norm_apply(2, i, lambda t: xn[:, i, t], lambda t: x[:, i, t], xn_ready[i])
                        if name == "l1_qkv":
                            if i == 0:
                                dve.wait_ge(l1_loaded, N_L1)
                            dve.wait_ge(l1_qkv, 3 * i + 3)
                            v.tensor_tensor(a2["vt"][:, i].rearrange("p (t c) -> p t c", t=T), lin(i, 3).rearrange("p (t c) -> p t c", t=T),
                                            bc(bvo[:, 0, :], 1, T), ALU.add).then_inc(l1_v, 1)
                        if name == "l1_kv":
                            dve.wait_ge(l1_kv, i + 1)
                            v.tensor_tensor(a2["kve"][:, i, 0:P].rearrange("p (h d) -> p h d", h=H0),
                                            lin(i, 2)[:, 0:P].rearrange("p (h d) -> p h d", h=H0),
                                            bc(headmask, 2, D0), ALU.mult).then_inc(l1_kve, 1)
                        if name == "l1_num":
                            dve.wait_ge(l1_num, i + 1)
                            for half in range(2):
                                o = lin(i, 3 - half)[:, 0:2 * HV].rearrange("p (t c) -> p t c", t=2)
                                last = v.tensor_scalar(den0[:, i, 2 * half:2 * half + 2], o[:, :, P:HV], 1e-8, None, ALU.add)
                            step(last)
                            settle()
                            step(v.reciprocal(den0[:, i], den0[:, i]))
                            settle()
                            for t in range(T):
                                o = lin(i, 3 - t // 2)[:, (t % 2) * HV:(t % 2) * HV + P].rearrange("p (h d) -> p h d", h=H0)
                                last = v.tensor_tensor(tiles(a2["o1"], i, t).rearrange("p (h d) -> p h d", h=H0), o,
                                                       bc(den0[:, i, t], 2, D0), ALU.mult)
                            last.then_inc(l1_o, 1)
                        if name == "l1_out":
                            dve.wait_ge(l1_out, i + 1)
                            dve.wait_ge(l1_bo, i + 1)
                            v.tensor_tensor(x[:, i].rearrange("p t d -> p (t d)"), x[:, i].rearrange("p t d -> p (t d)"),
                                            lin(i, 1), ALU.add).then_inc(x_l1, 1)
                        if name == "norms":
                            sums(i, *rest)
                            rotate1(i, *rest)
                        if name == "rotate":
                            rotate(i, *rest)
                        if name == "scores":
                            mask_max(i, *rest)
                        if name == "probs_moved" and i == 1:
                            probs_moved(i, *rest)
                        if name == "normalise_out":
                            l, t = rest
                            step(v.reciprocal(rsi[:, i], rs[:, i, t % 2]))
                            dve.wait_ge(av_done[i], l * SLOTS + HP * (t + 1))
                            settle()
                            v.tensor_tensor(a1["on"][:, i].rearrange("p (h d) -> p h d", h=H1),
                                            ps[:, OB[i], :].rearrange("p (h d) -> p h d", h=H1),
                                            bc(rsi[:, i], 2, D1), ALU.mult).then_inc(o_normed[i], 1)
                        if name == "project_out":
                            l, t = rest
                            dve.wait_ge(wo_done[i], l * T + t + 1)
                            v.tensor_tensor(xn[:, i, t], xn[:, i, t], ps[:, TB[i], 0:P], ALU.add).then_inc(y_updated[i], 1)
                        if name == "shift_back":
                            l = rest[0]
                            dve.wait_ge(h_back[i], l + 1)
                            norm_stats(i, lambda t: cols(ps[:, OB[i], :], t))
                        if name == "normed_T":
                            l = rest[0]
                            norm_apply(3 + l, i, lambda t: tiles(hn, i, t), lambda t: cols(ps[:, OB[i], :], t), hn_ready[i])
                        if name == "hidden":
                            l, j = rest
                            gi, n = l * 3 + j, HC[j][1]
                            dve.wait_ge(a_done[i], gi + 1)
                            dve.wait_ge(gelu1_done[i], gi + 1)
                            v.scalar_tensor_tensor(out=hid[0:n, i, j * N:(j + 1) * N], in0=ps[0:n, PREP[1]],
                                                   scalar=b1l[0:n, l, 0, j:j + 1], in1=gg[0:n, i, (j % 2) * N:(j % 2 + 1) * N],
                                                   op0=ALU.add, op1=ALU.mult).then_inc(hid_ready[i], 1)
                        if name == "ffn_out":
                            l = rest[0]
                            dve.wait_ge(ffn_out[i], l + 1)
                            dve.wait_ge(y_b2[i], l + 1)
                            v.tensor_tensor(xn[:, i].rearrange("p t d -> p (t d)"), xn[:, i].rearrange("p t d -> p (t d)"),
                                            ps[:, OB[i], :], ALU.add).then_inc(y_final[i], 1)
                        if name == "final":
                            dve.wait_ge(y_final[i], L)
                            v.tensor_tensor(x[:, i], x[:, i], xn[:, i], ALU.add).then_inc(out_ready, 1)

                @block.tensor
                def _(pe):
                    mm = nc.tensor.matmul

                    def transpose(dst, src):
                        return nc.tensor.transpose(dst, src, ident)

                    for u in range(U):
                        pe.wait_ge(xn_ready[u], 1)
                        for t in range(T):
                            last = transpose(cols(bank_a(u), t), xn[:, u, t])
                        last.then_inc(norm_transposed, 1)
                        pe.wait_ge(xhat_ready, u + 1)
                        for t in range(T):
                            last = transpose(cols(bank_b(u), t), tiles(a0["xhat"], u, t))
                        last.then_inc(norm_transposed, 1)
                    pe.wait_ge(first_loaded, N_FIRST)
                    for u in range(U):
                        pe.wait_ge(normT_ready, 2 * u + 1)
                        for t in range(T):
                            last = mm(bank_a(u)[:, t * E:(t + 1) * E], tiles(a0["xnT"], u, t), rW[:], start=True, stop=True)
                        last.then_inc(logits_done, 1)

                    qk = a0["qk"]

                    def qkvg(k):
                        u, t = k // T, k % T
                        if k == 0:
                            pe.wait_ge(normT_ready, 2 * U)
                            pe.wait_ge(logits_read, U)
                        if k >= 4:
                            pe.wait_ge(qkvg_biased, k - 3)
                        mm(ps[:, k % 4, 0:384], tiles(a0["xnormT"], u, t), w0[:, 0:384], start=True, stop=True)
                        mm(ps[:, k % 4, 384:512], tiles(a0["xnT"], u, t), w0[:, 384:512], start=True, stop=True).then_inc(qkvg_done, 1)

                    def transpose_q0(u):
                        pe.wait_ge(qk_ready, u + 1)
                        pe.wait_ge(qkvg_biased, U * T)
                        for t in range(T):
                            last = transpose(cols(bank_a(u), t), qk[:, u, t * 256:t * 256 + P])
                        last.then_inc(qT_done, 1)

                    def states(u):
                        pe.wait_ge(v_ready, u + 1)
                        for c in range(1, T):
                            for t in range(c):
                                last = mm(bank_b(u)[:, (c - 1) * HV:c * HV], qk[:, u, t * 256 + P:(t + 1) * 256],
                                          a0["vext"][:, u, t * HV:(t + 1) * HV], start=(t == 0), stop=(t == c - 1))
                        last.then_inc(state_done, 1)

                    def from_tile(i):
                        t, hg, u = item(i)
                        if hg == 0:
                            pe.wait_ge(kv_ready, t * U + u + 1)
                        if i < U:
                            pe.wait_ge(qT_ready, u + 1)
                        else:
                            pe.wait_ge(times_q, i - U + 1)
                        mm(bank_a(u)[:, 0:288], causal, kv_cols(u, t, 4 * hg, 4 * hg + 4), start=True, stop=True).then_inc(tile_part_done, 1)

                    def from_state(n):
                        t, u = n // U, n % U
                        if t == 1:
                            pe.wait_ge(state_ready, u + 1)
                        else:
                            pe.wait_ge(att_ready, n - U + 1)
                        mm(bank_b(u)[:, 0:HV], tiles(a0["qT"], u, t), a0["S"][:, u, (t - 1) * HV:t * HV],
                           start=True, stop=True).then_inc(state_part_done, 1)

                    def transpose_att(u):
                        pe.wait_ge(att_ready, (T - 1) * U + u + 1)
                        for t in range(T):
                            last = transpose(cols(bank_a(u), t), tiles(a0["att"], u, t))
                        last.then_inc(attT_done, 1)
                        pe.wait_ge(gates_ready, u + 1)
                        for t in range(T):
                            last = transpose(cols(bank_b(u), t)[0:E + 1], gate_a[:, u, t])
                        last.then_inc(attT_done, 1)

                    def project(u):
                        pe.wait_ge(attT_ready, 2 * u + 2)
                        for t in range(T):
                            mm(cols(bank_a(u), t), tiles(a0["attT"], u, t), wproj[:], start=True, stop=False)
                            last = mm(cols(bank_a(u), t), a0["gT"][0:E + 1, u, t * P:(t + 1) * P], b2ext[:], start=False, stop=True)
                        last.then_inc(proj_done, 1)

                    def expert_step(j):
                        n, f = j // FC, j % FC
                        if n < U * E:
                            if j == 0:
                                pe.wait_ge(experts_loaded, N_EXPERTS)
                            if f == 0:
                                pe.wait_ge(xe_ready, n + 1)
                            if j >= 2:
                                pe.wait_ge(gelu_done, j - 1)
                            mm(bank_h(j), W1[:, n % E, f * P:(f + 1) * P], a0["xe"][:, n // E, (n % 2) * N:(n % 2 + 1) * N],
                               start=True, stop=True).then_inc(h0_done, 1)
                        m = n - 1
                        if m >= 0:
                            if f == 0:
                                pe.wait_ge(gelu_done, FC * n)
                                if m >= 2:
                                    pe.wait_ge(y_added, m - 1)
                            for c in range(FC):
                                last = mm(cols(bank_y(m), f), ring[:, m % 2, c * N + f * P:c * N + (f + 1) * P],
                                          W2[:, m % E, c, :], start=(c == 0), stop=(c == FC - 1))
                            if f == FC - 1:
                                last.then_inc(y0_done, 1)

                    read = {}

                    def free(*banks):
                        for b in banks:
                            if b in read:
                                pe.wait_ge(*read[b])

                    def transpose_state(u, inst):
                        if inst in (1, 3):
                            pe.wait_ge(y_updated[u], T * (inst + 1) // 2)
                        elif inst == 2:
                            pe.wait_ge(y_final[u], 1)
                        free(TB[u])
                        for t in range(T):
                            last = transpose(cols(ps[:, TB[u], :], t), xn[:, u, t])
                        last.then_inc(y_transposed[u], 1)
                        read[TB[u]] = (hT_ready[u], inst + 1)

                    def lin_free(u, *which):
                        free(*(LIN[u][c] for c in which))

                    def lin_read(u, which, sem, value):
                        read[LIN[u][which]] = (sem, value)

                    def project_qk(u, l, t):
                        pi = l * T + t
                        if t == 0:
                            pe.wait_ge(hT_ready[u], 1 + 2 * l)
                        free(*PREP)
                        for c in range(2):
                            last = mm(ps[:, PREP[c], :], tiles(a1["hT"], u, t), wqkv[:, l, c * 512:(c + 1) * 512], start=True, stop=True)
                            read[PREP[c]] = (raw_ready[u], pi + 1)
                        last.then_inc(qk1_done[u], 1)

                    def project_v(u, l, t):
                        free(PREP[0])
                        mm(ps[:, PREP[0], :], tiles(a1["hT"], u, t), wqkv[:, l, 1024:1536], start=True, stop=True).then_inc(v1_done[u], 1)
                        read[PREP[0]] = (v1_ready[u], l * T + t + 1)

                    def transpose_qk(u, l, t):
                        pi = l * T + t
                        pe.wait_ge(rotated[u], pi + 1)
                        for i, bk in enumerate((PREP[1], PREP[0])):
                            free(bk)
                            for c in range(HP):
                                last = transpose(cols(ps[:, bk, :], c), a1["t1"][:, u, i * 512 + c * P:i * 512 + (c + 1) * P])
                            last.then_inc(qkT1_done[u], 1)
                            read[bk] = (qkT1_ready[u], 2 * pi + i + 1)

                    def scores(u, l, s):
                        t, hp = s // HP, s % HP
                        ui = l * SLOTS + s
                        k0, k1, _ = keys_of(t)
                        pe.wait_ge(qkT1_ready[u], 2 * (l * T + t) + 2)
                        free(*SCORE)
                        for i in range(2):
                            r = slice(64 * i, 64 * i + 64)
                            last = mm(ps[:, SCORE[i], 0:k1 - k0],
                                      a1["qT"][r, u, (t % 2) * 512 + hp * P:(t % 2) * 512 + (hp + 1) * P],
                                      a1["kT"][r, u, hp * N + k0:hp * N + k1], start=True, stop=True)
                            read[SCORE[i]] = (masked[u], ui + 1)
                        last.then_inc(scores1_done[u], 1)

                    def transpose_probs(u, l, s):
                        t, ui = s // HP, l * SLOTS + s
                        pe.wait_ge(exp_done[u], ui + 1)
                        free(TB[u])
                        for i in range(2):
                            for b in range(0 if t else 1, 2):
                                src = a1["P"][:, u, ((s % 2) * 2 + i) * 256 + b * P:((s % 2) * 2 + i) * 256 + (b + 1) * P]
                                last = transpose(cols(ps[:, TB[u], :], 2 * i + b), src)
                        last.then_inc(PT_done[u], 1)
                        read[TB[u]] = (PT_ready[u], ui + 1)

                    def weigh_values(u, l, s):
                        t, hp = s // HP, s % HP
                        ui = l * SLOTS + s
                        pe.wait_ge(PT_ready[u], ui + 1)
                        if hp == 0:
                            pe.wait_ge(v1_ready[u], l * T + t + 1)
                            free(OB[u])
                        for i in range(2):
                            h = 2 * hp + i
                            for b in range(0 if t else 1, 2):
                                last = mm(ps[:, OB[u], h * D1:(h + 1) * D1],
                                          a1["PT"][:, u, (s % 2) * 512 + (2 * i + b) * P:(s % 2) * 512 + (2 * i + b + 1) * P],
                                          v_tile(u, t - 1 + b)[:, h * D1:(h + 1) * D1],
                                          start=(b == 0 or t == 0), stop=(b == 1))
                        last.then_inc(av_done[u], 1)
                        read[OB[u]] = (o_normed[u], l * T + t + 1)

                    def transpose_out(u, l, t):
                        pe.wait_ge(o_normed[u], l * T + t + 1)
                        free(TB[u])
                        for c in range(HP):
                            last = transpose(cols(ps[:, TB[u], :], c), a1["on"][:, u, c * P:(c + 1) * P])
                        last.then_inc(oT_done[u], 1)
                        read[TB[u]] = (oT_ready[u], l * T + t + 1)

                    def project_out(u, l, t):
                        pe.wait_ge(oT_ready[u], l * T + t + 1)
                        free(TB[u])
                        for c in range(HP):
                            last = mm(ps[:, TB[u], 0:P], a1["oT"][:, u, c * P:(c + 1) * P], wo[:, l, c, :],
                                      start=(c == 0), stop=(c == HP - 1))
                        last.then_inc(wo_done[u], 1)
                        read[TB[u]] = (y_updated[u], l * T + t + 1)

                    shifts = [0, 0]
                    for name, i, *rest in plan:
                        if name == "expert":
                            expert_step(i)
                        if name == "last_expert":
                            for b in (4, 5):
                                read[b] = (y_added, U * E)
                            for b in (6, 7):
                                read[b] = (gelu_done, U * E * FC)
                        if name == "qkvg":
                            qkvg(i)
                        if name == "q_T":
                            transpose_q0(i)
                        if name == "states":
                            states(i)
                        if name == "from_tile":
                            from_tile(i)
                        if name == "from_state":
                            from_state(i)
                        if name == "att_T":
                            transpose_att(i)
                        if name == "project0":
                            project(i)
                            read[2 * i] = (x_base, i + 1)
                            read[2 * i + 1] = (attT_ready, 2 * i + 2)
                        if name == "state_T":
                            if shifts[i] == 0:
                                pe.wait_ge(xn_ready[i], 2)
                            transpose_state(i, shifts[i])
                            shifts[i] += 1
                        if name == "l1_qkv":
                            if i == 0:
                                pe.wait_ge(l1_loaded, N_L1)
                            pe.wait_ge(hT_ready[i], 1)
                            lin_free(i, 0, 1, 3)
                            for c in range(2):
                                mm(lin(i, c), wl1[:, c, :], a2["x1T"][:, i], start=True, stop=True).then_inc(l1_qkv, 1)
                                lin_read(i, c, l1_qs, 2 * i + c + 1)
                            for t in range(T):
                                last = mm(cols(lin(i, 3), t), tiles(a2["x1T"], i, t), wl1[:, 2, :], start=True, stop=True)
                            last.then_inc(l1_qkv, 1)
                            lin_read(i, 3, l1_v, i + 1)
                        if name == "l1_feat":
                            pe.wait_ge(l1_sq, 2 * i + 1)
                            lin_free(i, 0, 1)
                            mm(lin(i, 0), Rblk[:], a2["qs"][:, i], start=True, stop=False)
                            mm(lin(i, 0), nhb, a2["sqq"][:, i], start=False, stop=True).then_inc(l1_feat, 1)
                            pe.wait_ge(l1_sq, 2 * i + 2)
                            for t in range(T):
                                mm(cols(lin(i, 1), t), tiles(a2["ks"], i, t), Rblk[:], start=True, stop=False)
                                last = mm(cols(lin(i, 1), t), tiles(a2["sqk"], i, t), nhb, start=False, stop=True)
                            last.then_inc(l1_feat, 1)
                            for c in range(2):
                                lin_read(i, c, l1_exp, 2 * i + c + 1)
                        if name == "l1_kv":
                            pe.wait_ge(l1_exp, 2 * i + 2)
                            pe.wait_ge(l1_v, i + 1)
                            lin_free(i, 2)
                            for t in range(T):
                                last = mm(lin(i, 2)[:, 0:P], tiles(a2["kp"], i, t), tiles(a2["vt"], i, t), start=(t == 0), stop=(t == T - 1))
                            last.then_inc(l1_kv, 1)
                            lin_read(i, 2, l1_kve, i + 1)
                        if name == "l1_num":
                            pe.wait_ge(l1_kve, i + 1)
                            lin_free(i, 2, 3)
                            for t in range(T):
                                last = mm(lin(i, 3 - t // 2)[:, (t % 2) * HV:(t % 2 + 1) * HV], tiles(a2["qp"], i, t), a2["kve"][:, i],
                                          start=True, stop=True)
                            last.then_inc(l1_num, 1)
                            lin_read(i, 2, l1_o, i + 1)
                            lin_read(i, 3, l1_o, i + 1)
                        if name == "l1_oT":
                            pe.wait_ge(l1_o, i + 1)
                            lin_free(i, 0)
                            for t in range(T):
                                last = transpose(cols(lin(i, 0), t), tiles(a2["o1"], i, t))
                            last.then_inc(l1_oT_done, 1)
                            lin_read(i, 0, l1_oT, i + 1)
                        if name == "l1_out":
                            pe.wait_ge(l1_oT, i + 1)
                            lin_free(i, 1)
                            for t in range(T):
                                last = mm(cols(lin(i, 1), t), tiles(a2["o1T"], i, t), wl1[:, 3, :], start=True, stop=True)
                            last.then_inc(l1_out, 1)
                            lin_read(i, 1, x_l1, i + 1)
                        if name == "project_qk":
                            if i == 0 and rest == [0, 0]:
                                pe.wait_ge(layers_loaded, N_LAYERS)
                            project_qk(i, *rest)
                        if name == "project_v":
                            project_v(i, *rest)
                        if name == "transpose_qk":
                            transpose_qk(i, *rest)
                        if name == "scores":
                            scores(i, *rest)
                        if name == "transpose_probs":
                            transpose_probs(i, *rest)
                        if name == "weigh_values":
                            weigh_values(i, *rest)
                        if name == "transpose_out":
                            transpose_out(i, *rest)
                        if name == "project_out":
                            project_out(i, *rest)
                        if name == "shift_back":
                            l = rest[0]
                            pe.wait_ge(hT_ready[i], 2 + 2 * l)
                            free(OB[i])
                            for t in range(T):
                                last = transpose(cols(ps[:, OB[i], :], t), tiles(a1["hT"], i, t))
                            last.then_inc(h_back[i], 1)
                            read[OB[i]] = (hn_ready[i], l + 1)
                        if name == "normed_T":
                            l = rest[0]
                            pe.wait_ge(hn_ready[i], l + 1)
                            free(TB[i])
                            for t in range(T):
                                last = transpose(cols(ps[:, TB[i], :], t), tiles(hn, i, t))
                            last.then_inc(hnT_done[i], 1)
                            read[TB[i]] = (hnT_ready[i], l + 1)
                        if name == "hidden":
                            l, j = rest
                            c0, n = HC[j]
                            if j == 0:
                                pe.wait_ge(hnT_ready[i], l + 1)
                            free(*PREP)
                            mm(ps[0:n, PREP[0]], w1[:, l, HID + c0:HID + c0 + n], hnT[:, i], start=True, stop=True).then_inc(g_done[i], 1)
                            mm(ps[0:n, PREP[1]], w1[:, l, c0:c0 + n], hnT[:, i], start=True, stop=True).then_inc(a_done[i], 1)
                            read[PREP[0]] = (gelu1_done[i], l * 3 + j + 1)
                            read[PREP[1]] = (hid_ready[i], l * 3 + j + 1)
                        if name == "ffn_out":
                            l = rest[0]
                            pe.wait_ge(hid_ready[i], l * 3 + 3)
                            free(OB[i])
                            for t in range(T):
                                for j, (_, n) in enumerate(HC):
                                    last = mm(cols(ps[:, OB[i], :], t), hid[0:n, i, j * N + t * P:j * N + (t + 1) * P], w2[0:n, l, j, :],
                                              start=(j == 0), stop=(j == 2))
                            last.then_inc(ffn_out[i], 1)
                            read[OB[i]] = (y_final[i], l + 1)

            nc.all_engine_barrier()
            for s in loop_sems:
                nc.sync.sem_clear(s)
            nc.all_engine_barrier()


_INS = ["L0_attn_w_qkv", "L0_attn_w_gate", "L0_attn_w_proj", "L0_attn_b_proj", "L0_ffn_router_W", "L0_ffn_W1",
        "L0_ffn_W2", "L0_ffn_b2", "L1_attn_R", "L1_ffn_wqkv", "L1_ffn_wo", "L1_ffn_w1", "L1_ffn_w2"]


def kernel(**inputs):
    import numpy as np
    import concourse.bacc as bacc
    from concourse.bass_utils import run_bass_kernel_spmd

    inputs = {name: np.asarray(a) for name, a in inputs.items()}
    arrays = {name: np.ascontiguousarray(inputs[name]) for name in _INS}
    arrays["x"] = np.ascontiguousarray(inputs["L0_attn_x"])
    for n in "qkvo":
        arrays[f"W{n}T"] = np.ascontiguousarray(inputs[f"L1_attn_W{n}"].T)
    arrays["rows"] = np.concatenate([inputs[n].reshape(-1) for n in (
        "L0_attn_b_qkv", "L0_attn_b_gate", "L0_ffn_router_b", "L1_attn_bv", "L1_attn_bo", "L1_ffn_b2")])
    qk = np.stack([inputs["L1_ffn_q_scale"], inputs["L1_ffn_k_scale"]], 1)
    swapped = np.concatenate([qk[..., D1 // 2:], qk[..., :D1 // 2]], -1)
    arrays["qksc"] = np.concatenate([qk.reshape(-1), swapped.reshape(-1)])
    b1l = np.zeros((L, 2, 3, P), np.float32)
    for j, (c0, n) in enumerate(HC):
        b1l[:, :, j, :n] = inputs["L1_ffn_b1"].reshape(L, 2, HID)[:, :, c0:c0 + n]
    lgb = np.stack([inputs["L1_ffn_ln_g"], inputs["L1_ffn_ln_b"]], 1).reshape(2 * L, P)
    arrays["colv"] = np.ascontiguousarray(np.concatenate([
        inputs["L0_attn_ln_g"][None], inputs["L0_attn_ln_b"][None], inputs["L0_ffn_ln_g"], inputs["L0_ffn_ln_b"],
        inputs["L0_ffn_b1"].reshape(E * FC, P), lgb, b1l.reshape(-1, P), inputs["L1_attn_bq"][None],
        inputs["L1_attn_bk"][None]]).T)
    arrays["cst"], arrays["rot"] = shape_constants(np)

    nc = bacc.Bacc("TRN2", target_bir_lowering=False, num_devices=1)
    A, feed = {}, {}
    for name, a in arrays.items():
        A[name] = nc.dram_tensor(f"in_{name}", a.shape, mybir.dt.from_np(a.dtype), kind="ExternalInput").ap()
        feed[f"in_{name}"] = a
    out = nc.dram_tensor("out", (B, N, P), F32, kind="ExternalOutput").ap()
    build(nc, A, out)
    r = run_bass_kernel_spmd(nc, [feed], core_ids=[0])
    return r.results[0]["out"]
```

```python
from contextlib import ExitStack

import concourse.bass as bass
from concourse import mybir

F32 = mybir.dt.float32
U32 = mybir.dt.uint32
ALU = mybir.AluOpType
ACT = mybir.ActivationFunctionType
AX_X = mybir.AxisListType.X

P = 128
B, N = 4, 512
T = N // P
U = 2
H0, D0 = 16, 8
HV = H0 * (D0 + 1)
E, FF = 8, 512
FC = FF // P
L, H1, D1, W = 2, 8, 64, 64
EXPERT_STEPS = (U * E + 1) * FC
ITEMS = T * 4 * U
HP = H1 // 2
SLOTS = T * HP
AHEAD = 11
LEAD = 4
HID = 341
HC = [(0, 128), (128, 128), (256, 85)]
KEYS = P + W
EPS = 1e-5
QK_SCALE = 8.0
NEG = -1.0e30

C_ID, C_CAUSAL, C_HM, C_BAND, C_IOTA, C_MHALF, C_NHB, C_BAND_EVEN = 0, 128, 256, 272, 464, 472, 488, 616
NC = 808
NR, NCV = 1032, 68


def shape_constants(np):
    c = np.zeros((P, NC), np.float32)
    p, k = np.arange(P)[:, None], np.arange(P)[None, :]
    c[:, C_ID:C_ID + P] = p == k
    c[:, C_CAUSAL:C_CAUSAL + P] = p <= k
    c[:, C_HM:C_HM + H0] = p // D0 == np.arange(H0)[None, :]
    kk = np.arange(KEYS)[None, :]
    c[:, C_BAND:C_BAND + KEYS] = np.where((p <= kk) & (kk <= p + W), 0.0, NEG)
    c[:, C_BAND_EVEN:C_BAND_EVEN + P] = c[:, C_BAND + W:C_BAND + KEYS]
    c[:, C_BAND_EVEN + P:C_BAND_EVEN + KEYS] = c[:, C_BAND:C_BAND + W]
    c[:, C_IOTA:C_IOTA + E] = np.arange(E)[None, :]
    c[:, C_MHALF:C_MHALF + 16] = -0.5
    c[:, C_NHB:C_NHB + P] = np.where(p // D0 == k // D0, -0.5, 0.0)
    half = np.arange(0, D1, 2, dtype=np.float32)
    inv = (1.0 / 10000.0 ** (half / D1)).astype(np.float32)
    t = np.arange(N, dtype=np.float32)
    f = t[:, None] * inv[None, :]
    f = np.concatenate([f, f], -1).astype(np.float32)
    base = ((half + 0.4 * D1) / (1.4 * D1)).astype(np.float32)
    power = ((t - N // 2) / float(W // 2)).astype(np.float32)
    s = base[None, :] ** power[:, None]
    s = np.concatenate([s, s], -1)
    sign = np.where(np.arange(D1) < D1 // 2, -1.0, 1.0).astype(np.float32)
    rot = np.stack([np.stack([np.cos(f) * s, np.cos(f) / s], 1),
                    np.stack([np.sin(f) * s * sign, np.sin(f) / s * sign], 1)], 1)
    rot = rot.reshape(T, P, 2, 2, D1).transpose(1, 2, 0, 3, 4)
    return c, np.ascontiguousarray(rot, dtype=np.float32).reshape(P, -1)


SLOT_STAGES = {"scores": 0, "transpose_probs": 1, "weigh_values": 2, "probs_moved": 1}
TILE_STAGES = {"project_qk": -4, "squares": -4, "project_v": -3, "norms": -3, "rotate1": -3, "rotate": -2,
               "transpose_qk": -1, "normalise_out": 5, "transpose_out": 6, "project_out": 7, "prev_values": 0}
ORDER = ("scores", "project_v", "project_qk", "prev_values", "norms", "transpose_probs", "transpose_out",
         "normalise_out", "squares", "probs_moved", "project_out", "transpose_qk", "weigh_values", "rotate1",
         "rotate")
FFN_GROUPS = ((0, 1, 2), ("out",))
EXPERTS_AT = {"qkvg": (0, 2), "gates": (3, 1), "gating": (5, 4), "elu": (1, 1), "states": (1, 1),
              "item": (0, 1), "project": (1, 0, 1, 1), "ahead": 2}


def stream_groups(u):
    groups = [[(name, u)] for name in ("norm1", "state_T", "l1_qkv", "l1_feat", "l1_kv", "l1_num", "l1_oT", "l1_out")]
    for l in range(L):
        for s in range(-HP, SLOTS + HP):
            group = []
            for name in ORDER:
                if name in SLOT_STAGES:
                    at = s - SLOT_STAGES[name]
                    if 0 <= at < SLOTS:
                        group.append((name, u, l, at))
                else:
                    t, behind = divmod(s - TILE_STAGES[name], HP)
                    if behind == 0 and 0 <= t < T:
                        group.append((name, u, l, t))
            groups.append(group)
        groups += [[("state_T", u)], [("shift_back", u, l)], [("normed_T", u, l)]]
        groups += [[("ffn_out", u, l) if j == "out" else ("hidden", u, l, j) for j in pieces] for pieces in FFN_GROUPS]
        if l + 1 < L:
            groups.append([("state_T", u)])
    return groups + [[("final", u)]]


def make_plan():
    plan, at = [], [0]

    def experts(k):
        for _ in range(k):
            if at[0] < EXPERT_STEPS:
                plan.append(("expert", at[0]))
                at[0] += 1

    for k in range(U * T):
        plan.append(("qkvg", k))
        if k % T == T - 1:
            plan.append(("gate_exp", k // T))
        experts(EXPERTS_AT["qkvg"][k % 2])
    for name in ("gates", "gating", "elu"):
        for u in range(U):
            plan.append((name, u))
            experts(EXPERTS_AT[name][u])
    for u in range(U):
        plan.append(("q_T", u))
        plan.append(("states", u))
        experts(EXPERTS_AT["states"][u])
    for i in range(ITEMS + 1):
        if i < ITEMS:
            if i // U % 4 == 0 and i >= 4 * U:
                plan.append(("from_state", i // (4 * U) * U + i % U))
            plan.append(("from_tile", i))
            experts(EXPERTS_AT["item"][i % 2])
        if i:
            plan.append(("summed", i - 1))
            if (i - 1) // U % 4 == 3:
                plan.append(("attended", (i - 1) // (4 * U) * U + (i - 1) % U))
    for k, (name, u) in enumerate((name, u) for name in ("att_T", "project0") for u in range(U)):
        plan.append((name, u))
        experts(EXPERTS_AT["project"][k])
    first, second = stream_groups(0), stream_groups(1)
    assert at[0] > (E + 1) * FC + 1
    assert not {stage[0] for group in first[:AHEAD] for stage in group} & {"scores", "weigh_values"}
    for group in first[:AHEAD]:
        plan += group
        experts(EXPERTS_AT["ahead"])
    experts(EXPERT_STEPS)
    plan.append(("last_expert", 0))
    plan += second.pop(0)
    for group in first[AHEAD:AHEAD + LEAD]:
        plan += group
    for k in range(len(second)):
        plan += second[k]
        if AHEAD + LEAD + k < len(first):
            plan += first[AHEAD + LEAD + k]
    return plan


def build(nc, A, out):
    with ExitStack() as ctx:
        def sb(name, shape, dt=F32):
            return ctx.enter_context(nc.sbuf_tensor(name, shape, dt))

        def sem(name):
            return ctx.enter_context(nc.semaphore(name))

        def bc(ap, axis, n):
            v = ap.unsqueeze(axis)
            return v.broadcast_to(v.shape[:axis] + (n,) + v.shape[axis + 1:])

        cst = sb("cst", [P, NC])
        ident = cst[:, C_ID:C_ID + P]
        causal = cst[:, C_CAUSAL:C_CAUSAL + P]
        headmask = cst[:, C_HM:C_HM + H0]
        band = cst[:, C_BAND:C_BAND + KEYS]
        band_even = cst[:, C_BAND_EVEN:C_BAND_EVEN + KEYS]
        iota = cst[:, C_IOTA:C_IOTA + E]
        mhalf = cst[:, C_MHALF:C_MHALF + 16]
        nhb = cst[:, C_NHB:C_NHB + P]
        tabs = sb("tabs", [P, L, 2, T, 2, D1])
        w0 = sb("w0", [P, 512])
        rows = sb("rows", [P, NR])
        colv = sb("colv", [P, NCV])
        bias0 = rows[:, 0:512]
        rb = rows[:, 512:520]
        bvo = rows[:, 520:776].rearrange("p (i d) -> p i d", i=2)
        b2l = rows[:, 776:1032].rearrange("p (l d) -> p l d", l=L)
        lncol = colv[:, 0:2]
        elg = colv[:, 2:18].rearrange("p (i e) -> p i e", i=2)
        b1c = colv[:, 18:50].rearrange("p (e f) -> p e f", e=E)
        lgb = colv[:, 50:54].rearrange("p (l i) -> p l i", l=L)
        b1l = colv[:, 54:66].rearrange("p (l i j) -> p l i j", l=L, i=2)
        rW = sb("rW", [P, E])
        wproj = sb("wproj", [P, P])
        b2ext = sb("b2ext", [E + 1, P])
        W1 = sb("W1", [P, E, FF])
        W2 = sb("W2", [P, E, FC, P])
        wl1 = sb("wl1", [P, 4, P])
        bl1 = sb("bl1", [P, 2])
        Rblk = sb("Rblk", [P, P])
        wqkv = sb("wqkv", [P, L, 3 * H1 * D1])
        wo = sb("wo", [P, L, HP, P])
        w1 = sb("w1", [P, L, 2 * HID])
        w2 = sb("w2", [P, L, 3, P])

        x_in = sb("x_in", [P, B, T, P])
        x = sb("x", [P, U, T, P])
        xn = sb("xn", [P, U, T, P])
        ring = sb("ring", [P, 2, FC * N])
        stats = sb("stats", [P, U, T, 6])
        mv = sb("mv", [P, U, T, 2])
        ve = sb("ve", [P, U, T])
        rstd = sb("rstd", [P, U, T])
        lg = sb("lg", [P, U, T, E])
        top = sb("top", [P, U, T, 8])
        topi = sb("topi", [P, U, T, 8], U32)
        topf = sb("topf", [P, U, T, 2])
        wts = sb("wts", [P, U, 4, T])
        gate_a = sb("gate_a", [P, U, T, E + 1])
        gate_b = sb("gate_b", [P, U, T, E])
        gsum = sb("gsum", [P, U, T])
        gs = sb("gs", [P, U, T])
        den0 = sb("den0", [P, U, T, H0])
        ssq = sb("ssq", [P, U, 16])
        rn = sb("rn", [P, U, 2, 16])
        mx = sb("mx", [P, U, 2, 2])
        nmx = sb("nmx", [P, U, 2, 2])
        rs = sb("rs", [P, U, 2, H1])
        rsi = sb("rsi", [P, U, H1])
        NA = 12160
        arena = sb("arena", [P, U, NA])

        def carve(sizes, at=0):
            got = {}
            for name, size in sizes:
                got[name] = arena[:, :, at:at + size]
                at += size
            assert at <= NA, at
            return got

        a0 = carve([("xhat", 512), ("xnT", 512), ("xnormT", 512), ("xhatT", 512), ("qkvg", 2048),
                    ("gn", 512), ("me", 1024), ("qk", 1024), ("vext", T * HV), ("qT", 512),
                    ("prod", 576), ("sums", HV), ("att", 512), ("attT", 512), ("gT", 512), ("S", 3 * HV), ("xe", 1024)])
        kv_at = 4 * 512
        a0["kv"] = arena[:, :, kv_at:kv_at + 2 * HV * D0]
        assert 2 * HV * D0 <= 2048 + 512
        a1 = carve([("kT", 2048), ("qT", 1024), ("qn", 1024), ("t1", 1024), ("t2", 1024),
                    ("sm", 768), ("P", 768), ("PT", 768), ("v_prev", 512), ("on", 512), ("oT", 512), ("hT", 512), ("v0", 512)])
        a2 = carve([("x1T", 512), ("qs", 512), ("ks", 512), ("sqq", 512), ("sqk", 512), ("qp", 512),
                    ("kp", 512), ("vt", 512), ("kve", HV), ("o1", 512), ("o1T", 512)])
        hid = a1["kT"][:, :, 0:1536]
        gg = a1["qn"]
        hn, hnT = a1["on"], a1["oT"]

        def tiles(ap, u, t):
            return ap[:, u, t * P:(t + 1) * P]

        def v_tile(u, t):
            return ring[:, u, t * 512:(t + 1) * 512] if t else a1["v0"][:, u]

        def v_prev(u, t):
            return ring[:, u, 0:512] if t % 2 else a1["v_prev"][:, u]

        def probs_of(u, s):
            return a1["P"][:, u, (s % 2) * 2 * KEYS:(s % 2 + 1) * 2 * KEYS]

        ps = ctx.enter_context(nc.psum_tensor("ps", [P, 8, 512], F32))

        def bank_a(u):
            return ps[:, 2 * u, :]

        def bank_b(u):
            return ps[:, 2 * u + 1, :]

        def bank_y(n):
            return ps[:, 4 + n % 2, :]

        def bank_h(hc):
            return ps[:, 6 + hc % 2, :]

        def cols(ap, t, w=P):
            return ap[:, t * w:(t + 1) * w]

        x_loaded = sem("x_loaded")
        x_rest_loaded = sem("x_rest_loaded")
        small_loaded = sem("small_loaded")
        first_loaded = sem("first_loaded")
        experts_loaded = sem("experts_loaded")
        l1_loaded = sem("l1_loaded")
        layers_loaded = sem("layers_loaded")
        tabs_made = sem("tabs_made")
        out_stored = sem("out_stored")

        loop_sems = []

        def lsem(name):
            s = sem(name)
            loop_sems.append(s)
            return s

        def lsem2(name):
            return [lsem(name + "0"), lsem(name + "1")]

        dve_step = lsem("dve_step")
        xhat_ready = lsem("xhat_ready"); norm_transposed = lsem("norm_transposed"); normT_ready = lsem("normT_ready")
        logits_done = lsem("logits_done"); logits_read = lsem("logits_read")
        top2_ready = lsem("top2_ready"); ew_ready = lsem("ew_ready"); gates_ready = lsem("gates_ready")
        qkvg_done = lsem("qkvg_done"); qkvg_biased = lsem("qkvg_biased")
        gate_exp = lsem("gate_exp"); qk_min = lsem("qk_min"); qk_exp = lsem("qk_exp")
        qk_ready = lsem("qk_ready"); v_ready = lsem("v_ready")
        qT_done = lsem("qT_done"); qT_ready = lsem("qT_ready")
        state_done = lsem("state_done"); state_ready = lsem("state_ready")
        kv_ready = lsem("kv_ready"); tile_part_done = lsem("tile_part_done"); times_q = lsem("times_q")
        state_part_done = lsem("state_part_done"); state_part_added = lsem("state_part_added"); att_ready = lsem("att_ready")
        attT_done = lsem("attT_done"); attT_ready = lsem("attT_ready"); proj_done = lsem("proj_done")
        x_base = lsem("x_base")
        xe_ready = lsem("xe_ready"); h0_done = lsem("h0_done"); gelu_done = lsem("gelu_done")
        y0_done = lsem("y0_done"); y_added = lsem("y_added")
        zeros_ready = lsem("zeros_ready")
        l1_qkv = lsem("l1_qkv"); l1_qs = lsem("l1_qs"); l1_sq = lsem("l1_sq"); l1_v = lsem("l1_v")
        l1_feat = lsem("l1_feat"); l1_exp = lsem("l1_exp"); l1_kv = lsem("l1_kv"); l1_kve = lsem("l1_kve")
        l1_num = lsem("l1_num"); l1_o = lsem("l1_o"); l1_oT_done = lsem("l1_oT_done")
        l1_oT = lsem("l1_oT"); l1_out = lsem("l1_out"); l1_bo = lsem("l1_bo"); x_l1 = lsem("x_l1")
        x_copied = lsem("x_copied")
        var_ready = lsem2("var_ready"); rstd_ready = lsem2("rstd_ready"); xn_ready = lsem2("xn_ready")
        y_transposed = lsem2("y_transposed"); hT_ready = lsem2("hT_ready")
        qk1_done = lsem2("qk1_done"); raw_ready = lsem2("raw_ready"); sq_ready = lsem2("sq_ready")
        ss_ready = lsem2("ss_ready"); rn_ready = lsem2("rn_ready"); rot2_ready = lsem2("rot2_ready")
        rot_sum = lsem2("rot_sum"); rotated = lsem2("rotated"); v1_done = lsem2("v1_done"); v1_ready = lsem2("v1_ready")
        v_prev_ready = lsem2("v_prev_ready")
        qkT1_done = lsem2("qkT1_done"); qkT1_ready = lsem2("qkT1_ready")
        scores1_done = lsem2("scores1_done"); masked = lsem2("masked"); exp_done = lsem2("exp_done")
        PT_done = lsem2("PT_done"); PT_ready = lsem2("PT_ready"); av_done = lsem2("av_done")
        o_normed = lsem2("o_normed"); oT_done = lsem2("oT_done"); oT_ready = lsem2("oT_ready")
        wo_done = lsem2("wo_done"); y_updated = lsem2("y_updated")
        h_back = lsem2("h_back"); hn_ready = lsem2("hn_ready"); hnT_done = lsem2("hnT_done")
        hnT_ready = lsem2("hnT_ready"); g_done = lsem2("g_done"); a_done = lsem2("a_done")
        gelu1_done = lsem2("gelu1_done"); hid_ready = lsem2("hid_ready"); ffn_out = lsem2("ffn_out")
        y_b2 = lsem2("y_b2"); y_final = lsem2("y_final")
        out_ready = lsem("out_ready")

        rot_raw = arena[:, 0, 0:1024].rearrange("p (c t q d) -> p c t q d", c=2, t=T, q=2)
        qksc = arena[:, 0, 1024:1536].rearrange("p (c l q d) -> p c l q d", c=2, l=L, q=2)
        R8 = arena[:, 0, 1536:1536 + D0]
        bl1_raw = colv[:, 66:68]
        HD = D1 // 2

        def load(sp):
            small = [(arena[:, 0, 0:1024], A["rot"]), (arena[:, 0, 1024:1536], A["qksc"].partition_broadcast(P)),
                     (R8, A["L1_attn_R"].partition_broadcast(H0)), (cst[:], A["cst"]), (colv[:], A["colv"])]
            for dst, src in small:
                sp.dma_start(dst, src).then_inc(small_loaded, 16)
            xv = A["x"].rearrange("b (t p) d -> p b t d", p=P)
            for b in range(0, B, U):
                sp.dma_start(x_in[:, b:b + U], xv[:, b:b + U]).then_inc(x_loaded if b == 0 else x_rest_loaded, 16)
            first = [(w0[:, 0:384], A["L0_attn_w_qkv"]), (w0[:, 384:512], A["L0_attn_w_gate"]),
                     (rW[:], A["L0_ffn_router_W"]), (rows[:], A["rows"].partition_broadcast(P)),
                     (wproj[:], A["L0_attn_w_proj"]), (b2ext[0:E, :], A["L0_ffn_b2"]),
                     (b2ext[E:E + 1, :], A["L0_attn_b_proj"].unsqueeze(0))]
            for dst, src in first:
                sp.dma_start(dst, src).then_inc(first_loaded, 16)
            sp.dma_start(W1[:], A["L0_ffn_W1"].rearrange("e h f -> h e f")).then_inc(experts_loaded, 16)
            for e in range(E):
                sp.dma_start(W2[:, e], A["L0_ffn_W2"][e].rearrange("(f p) h -> p f h", p=P)).then_inc(experts_loaded, 16)
            for i, name in enumerate(("WqT", "WkT", "WvT", "WoT")):
                sp.dma_start(wl1[:, i, :], A[name]).then_inc(l1_loaded, 16)
            sp.dma_start(wqkv[:], A["L1_ffn_wqkv"].rearrange("l h n -> h l n")).then_inc(layers_loaded, 16)
            sp.dma_start(w1[:], A["L1_ffn_w1"].rearrange("l h n -> h l n")).then_inc(layers_loaded, 16)
            for l in range(L):
                sp.dma_start(wo[:, l], A["L1_ffn_wo"][l].rearrange("(c p) h -> p c h", p=P)).then_inc(layers_loaded, 16)
                for j, (c0, n) in enumerate(HC):
                    sp.dma_start(w2[0:n, l, j], A["L1_ffn_w2"][l][c0:c0 + n]).then_inc(layers_loaded, 16)

        def make_tables(dve):
            dve.wait_ge(small_loaded, 16 * 5)
            for l in range(L):
                for c in range(2):
                    for q in range(2):
                        nc.vector.tensor_tensor(tabs[:, l, c, :, q, :], rot_raw[:, c, :, q, :],
                                                bc(qksc[:, c, l, q, :], 1, T), ALU.mult)
            nc.vector.tensor_scalar(bl1[:], bl1_raw, D0 ** -0.5, None, ALU.mult)
            nc.vector.tensor_tensor(Rblk[:].rearrange("p (h d) -> p h d", h=H0), bc(R8, 1, H0),
                                    bc(headmask, 2, D0), ALU.mult).then_inc(tabs_made, 1)
            dve.wait_ge(tabs_made, 1)

        load(nc.sync)
        make_tables(nc.vector)
        N_FIRST, N_EXPERTS, N_L1, N_LAYERS = 16 * 7, 16 * (1 + E), 16 * 4, 16 * (2 + L * 4)

        ov = out.rearrange("b (t p) d -> p b t d", p=P)

        PREP, TB, OB, SCORE = (0, 1), (2, 3), (4, 5), (6, 7)
        LIN = ((0, 1, 2, 3), (0, 1, 3, 5))

        def lin(u, i):
            return ps[:, LIN[u][i], :]

        def hidden_banks(u, j):
            return (TB[u], OB[u]) if j == 1 else PREP

        def keys_of(t):
            return (t * P - W, (t + 1) * P, 0) if t else (0, P, W)

        plan = make_plan()

        def item(i):
            return i // (4 * U), i // U % 4, i % U

        def kv_cols(u, t, h0, h1):
            at = (t % 2) * HV * D0
            return a0["kv"][:, u, at + h0 * 72:at + h1 * 72]

        with nc.Fori(0, B // U) as it:
            with nc.Block() as block:

                @block.sync
                def _(sp):
                    for u in range(U):
                        sp.wait_ge(out_ready, u + 1)
                        sp.dma_start(ov[:, bass.ds(it * U + u, 1)].rearrange("p b t d -> p (b t) d"),
                                     x_in[:, bass.ds(it * U + u, 1)].rearrange("p b t d -> p (b t) d")).then_inc(out_stored, 16)

                @block.gpsimd
                def _(pool):
                    g = nc.gpsimd

                    def rsqrt_var(u, n):
                        pool.wait_ge(var_ready[u], n + 1)
                        g.tensor_tensor(rstd[:, u], ve[:, u], mhalf[:, 0:T], ALU.pow).then_inc(rstd_ready[u], 1)

                    def ones_behind_v(u):
                        pool.wait_ge(qkvg_biased, T * (u + 1))
                        v = a0["vext"][:, u].rearrange("p (t h d) -> p t h d", t=T, h=H0)
                        g.memset(v[:, :, :, D0:D0 + 1], 1.0)
                        src = a0["qkvg"][:, u].rearrange("p (t c) -> p t c", t=T)[:, :, 256:384]
                        for t in range(T):
                            last = g.tensor_copy(v[:, t, :, 0:D0], src[:, t].rearrange("p (h d) -> p h d", h=H0))
                        last.then_inc(v_ready, 1)

                    def k_times_v(n):
                        t, u = n // U, n % U
                        if t == 0:
                            pool.wait_ge(qk_ready, u + 1)
                            pool.wait_ge(v_ready, u + 1)
                        if t >= 2:
                            pool.wait_ge(tile_part_done, ((t - 2) * 4 + 3) * U + u + 1)
                        k = a0["qk"][:, u, t * 256 + P:(t + 1) * 256].rearrange("p (h d) -> p h d", h=H0)
                        v = a0["vext"][:, u, t * HV:(t + 1) * HV].rearrange("p (h m) -> p h m", h=H0)
                        g.tensor_tensor(kv_cols(u, t, 0, H0).rearrange("p (h d m) -> p h d m", h=H0, d=D0),
                                        bc(k, 3, D0 + 1), bc(v, 2, D0), ALU.mult).then_inc(kv_ready, 1)

                    def expert_input(n):
                        u, e = n // E, n % E
                        if n == 0:
                            pool.wait_ge(experts_loaded, N_EXPERTS)
                        if e == 0:
                            pool.wait_ge(normT_ready, 2 * u + 2)
                        else:
                            pool.wait_ge(h0_done, 4 * (n - 1))
                        g.tensor_scalar(a0["xe"][:, u, (e % 2) * N:(e % 2 + 1) * N], a0["xhatT"][:, u],
                                        elg[:, 0, e:e + 1], elg[:, 1, e:e + 1], ALU.mult, ALU.add).then_inc(xe_ready, 1)

                    def rotate2(u, l, t):
                        pool.wait_ge(raw_ready[u], l * T + t + 1)
                        q = a1["qn"][:, u].rearrange("p (q h d) -> p q h d", q=2, h=H1)
                        o = a1["t2"][:, u].rearrange("p (q h d) -> p q h d", q=2, h=H1)
                        for a, b in ((0, HD), (HD, 0)):
                            last = g.tensor_tensor(o[:, :, :, a:a + HD], q[:, :, :, b:b + HD],
                                                   bc(tabs[:, l, 1, t, :, a:a + HD], 2, H1), ALU.mult)
                        last.then_inc(rot2_ready[u], 1)

                    def inverse_norms(u, l, t):
                        pool.wait_ge(ss_ready[u], l * T + t + 1)
                        g.tensor_tensor(rn[:, u, t % 2], ssq[:, u], mhalf, ALU.pow).then_inc(rn_ready[u], 1)

                    def scale_k(u, l, t):
                        pool.wait_ge(rot_sum[u], l * T + t + 1)
                        pool.wait_ge(rn_ready[u], l * T + t + 1)
                        k = a1["t1"][:, u, 512:1024].rearrange("p (h d) -> p h d", h=H1)
                        g.tensor_tensor(k, k, bc(rn[:, u, t % 2, H1:16], 2, D1), ALU.mult).then_inc(rotated[u], 1)

                    pool.wait_ge(tabs_made, 1)
                    for n in range(2):
                        for u in range(U):
                            rsqrt_var(u, n)
                    expert_input(0)
                    for name, i, *rest in plan:
                        if name == "expert" and i % FC == 0 and i // FC + 1 < U * E:
                            expert_input(i // FC + 1)
                        if name == "gates":
                            ones_behind_v(i)
                        if name == "elu":
                            k_times_v(i)
                        if name == "from_tile" and i % (4 * U) < U and i + 4 * U < ITEMS:
                            k_times_v((i // (4 * U) + 1) * U + i % U)
                        if name == "norm1":
                            rsqrt_var(i, 2)
                            if i == 0:
                                pool.wait_ge(l1_loaded, N_L1)
                            pool.wait_ge(xn_ready[i], 2)
                            g.memset(a1["hT"][:, i, 0:1], 0.0)
                            g.tensor_copy(a2["kve"][:, i, P:HV], headmask).then_inc(zeros_ready, 1)
                            g.tensor_tensor(x[:, i], x[:, i], bc(bvo[:, 1, :], 1, T), ALU.add).then_inc(l1_bo, 1)
                        if name == "l1_qkv":
                            for c, (a, b) in enumerate((("qs", "sqq"), ("ks", "sqk"))):
                                pool.wait_ge(l1_qs, 2 * i + c + 1)
                                g.tensor_tensor(a2[b][:, i], a2[a][:, i], a2[a][:, i], ALU.mult).then_inc(l1_sq, 1)
                        if name == "project_qk":
                            if i == 0 and rest == [0, 0]:
                                pool.wait_ge(layers_loaded, N_LAYERS)
                            rotate2(i, *rest)
                        if name == "norms":
                            inverse_norms(i, *rest)
                        if name == "rotate":
                            scale_k(i, *rest)
                        if name == "shift_back":
                            l = rest[0]
                            pool.wait_ge(y_transposed[i], 2 + 2 * l)
                            g.tensor_tensor(xn[:, i], xn[:, i], bc(b2l[:, l], 1, T), ALU.add).then_inc(y_b2[i], 1)
                            rsqrt_var(i, 3 + l)

                @block.scalar
                def _(act):
                    a = nc.scalar

                    act.wait_ge(x_loaded, 16)
                    act.wait_ge(tabs_made, 1)
                    for u in range(U):
                        a.activation(x[:, u].rearrange("p t d -> p (t d)"), x_in[:, bass.ds(it * U + u, 1)].rearrange("p b t d -> p (b t) d"),
                                     ACT.Copy).then_inc(x_copied, 1)
                    act.wait_ge(first_loaded, N_FIRST)
                    for u in range(U):
                        act.wait_ge(norm_transposed, 2 * u + 1)
                        a.activation(a0["xnT"][:, u], bank_a(u), ACT.Copy).then_inc(normT_ready, 1)
                        act.wait_ge(norm_transposed, 2 * u + 2)
                        a.activation(a0["xnormT"][:, u], bank_b(u), ACT.Identity, bias=lncol[:, 1:2], scale=lncol[:, 0:1])
                        a.activation(a0["xhatT"][:, u], bank_b(u), ACT.Copy).then_inc(normT_ready, 1)
                    for u in range(U):
                        act.wait_ge(top2_ready, u + 1)
                        a.activation(wts[:, u, 1], wts[:, u, 0], ACT.Exp).then_inc(ew_ready, 1)

                    def shifted(u, inst):
                        act.wait_ge(y_transposed[u], inst + 1)
                        if inst == 0:
                            a.activation(a2["x1T"][:, u], ps[:, TB[u]], ACT.Copy)
                            act.wait_ge(zeros_ready, u + 1)
                        a.activation(a1["hT"][0:64, u], ps[0:64, TB[u]], ACT.Copy)
                        a.activation(a1["hT"][64:128, u, 1:N], ps[64:128, TB[u], 0:N - 1], ACT.Copy).then_inc(hT_ready[u], 1)

                    def raw(u, l, t):
                        pi = l * T + t
                        act.wait_ge(qk1_done[u], pi + 1)
                        if pi:
                            act.wait_ge(rot2_ready[u], pi)
                            act.wait_ge(rot_sum[u], pi)
                        if pi and t == 0:
                            act.wait_ge(hid_ready[u], 3 * l)
                        a.activation(a1["qn"][:, u].rearrange("p (q c) -> p q c", q=2), ps[:, PREP[0]:PREP[1] + 1, :], ACT.Copy).then_inc(raw_ready[u], 1)

                    def squares(u, l, t):
                        pi = l * T + t
                        act.wait_ge(raw_ready[u], pi + 1)
                        if pi:
                            act.wait_ge(qkT1_done[u], 2 * pi)
                        a.activation(a1["t1"][:, u], a1["qn"][:, u], ACT.Square).then_inc(sq_ready[u], 1)

                    def values(u, l, t):
                        act.wait_ge(v1_done[u], l * T + t + 1)
                        a.activation(v_tile(u, t), ps[:, PREP[0], :], ACT.Copy).then_inc(v1_ready[u], 1)

                    def qk_transposed(u, l, t):
                        pi = l * T + t
                        act.wait_ge(qkT1_done[u], 2 * pi + 1)
                        a.activation(a1["qT"][:, u, (t % 2) * 512:(t % 2 + 1) * 512], ps[:, PREP[1], :], ACT.Copy).then_inc(qkT1_ready[u], 1)
                        act.wait_ge(qkT1_done[u], 2 * pi + 2)
                        kv = a1["kT"][:, u].rearrange("p (c k) -> p c k", c=HP)[:, :, t * P:(t + 1) * P]
                        a.activation(kv, ps[:, PREP[0], :].rearrange("p (c k) -> p c k", c=HP), ACT.Copy).then_inc(qkT1_ready[u], 1)

                    def exps(u, l, s):
                        t, hp = s // HP, s % HP
                        ui = l * SLOTS + s
                        k0, k1, _ = keys_of(t)
                        n = k1 - k0
                        act.wait_ge(masked[u], ui + 1)
                        if ui >= 2:
                            act.wait_ge(PT_done[u], ui - 1)
                        for i in range(2):
                            smv = a1["sm"][:, u].rearrange("p (r i k) -> p r i k", r=2, i=2)[:, s % 2, i, 0:n]
                            pv = probs_of(u, s)[:, KEYS + (KEYS - n):2 * KEYS] if i else probs_of(u, s)[:, 0:n]
                            last = a.activation(pv, smv, ACT.Exp, scale=rn[:, u, t % 2, 2 * hp + i:2 * hp + i + 1],
                                                bias=nmx[:, u, s % 2, i:i + 1],
                                                accum_out=rs[:, u, t % 2, 2 * hp + i:2 * hp + i + 1])
                        last.then_inc(exp_done[u], 1)

                    def probs_moved(u, l, s):
                        t, ui = s // HP, l * SLOTS + s
                        act.wait_ge(PT_done[u], ui + 1)
                        if ui >= 2:
                            act.wait_ge(av_done[u], ui - 1)
                        c0 = 0 if t else P
                        a.activation(a1["PT"][:, u, (s % 2) * 384 + c0:(s % 2 + 1) * 384], ps[:, TB[u], c0:384],
                                     ACT.Copy).then_inc(PT_ready[u], 1)

                    shifts = [0, 0]
                    for name, i, *rest in plan:
                        if name == "expert" and i // FC < U * E:
                            n, f = i // FC, i % FC
                            if f == 0 and n == 0:
                                act.wait_ge(experts_loaded, N_EXPERTS)
                            if f == 0 and n >= 2:
                                act.wait_ge(y0_done, n - 1)
                            act.wait_ge(h0_done, i + 1)
                            a.activation(ring[:, n % 2, f * N:(f + 1) * N], bank_h(i), ACT.Gelu,
                                         bias=b1c[:, n % E, f:f + 1]).then_inc(gelu_done, 1)
                        if name == "gate_exp":
                            act.wait_ge(qkvg_biased, T * (i + 1))
                            src = a0["qkvg"][:, i].rearrange("p (t c) -> p t c", t=T)[:, :, 384:512]
                            a.activation(a0["gn"][:, i].rearrange("p (t c) -> p t c", t=T), src, ACT.Exp, scale=-1.0).then_inc(gate_exp, 1)
                        if name == "elu":
                            act.wait_ge(qk_min, i + 1)
                            a.activation(a0["me"][:, i], a0["me"][:, i], ACT.Exp).then_inc(qk_exp, 1)
                        if name == "q_T":
                            act.wait_ge(qT_done, i + 1)
                            a.activation(a0["qT"][:, i], bank_a(i), ACT.Copy).then_inc(qT_ready, 1)
                        if name == "att_T":
                            act.wait_ge(attT_done, 2 * i + 1)
                            a.activation(a0["attT"][:, i], bank_a(i), ACT.Copy).then_inc(attT_ready, 1)
                            act.wait_ge(attT_done, 2 * i + 2)
                            a.activation(a0["gT"][0:E + 1, i], bank_b(i)[0:E + 1], ACT.Copy).then_inc(attT_ready, 1)
                        if name == "state_T":
                            shifted(i, shifts[i])
                            shifts[i] += 1
                        if name == "l1_qkv":
                            for c, dst in enumerate(("qs", "ks")):
                                act.wait_ge(l1_qkv, 3 * i + c + 1)
                                a.activation(a2[dst][:, i], lin(i, c), ACT.Identity, bias=bl1[:, c:c + 1],
                                             scale=D0 ** -0.5).then_inc(l1_qs, 1)
                        if name == "l1_feat":
                            for c, dst in enumerate(("qp", "kp")):
                                act.wait_ge(l1_feat, 2 * i + c + 1)
                                a.activation(a2[dst][:, i], lin(i, c), ACT.Exp).then_inc(l1_exp, 1)
                        if name == "l1_oT":
                            act.wait_ge(l1_oT_done, i + 1)
                            a.activation(a2["o1T"][:, i], lin(i, 0), ACT.Copy).then_inc(l1_oT, 1)
                        if name == "project_qk":
                            if i == 0 and rest == [0, 0]:
                                act.wait_ge(layers_loaded, N_LAYERS)
                            raw(i, *rest)
                        if name == "squares":
                            squares(i, *rest)
                        if name == "project_v":
                            values(i, *rest)
                        if name == "transpose_qk":
                            qk_transposed(i, *rest)
                        if name == "scores":
                            exps(i, *rest)
                        if name == "probs_moved" and i == 0:
                            probs_moved(i, *rest)
                        if name == "transpose_out":
                            pi = rest[0] * T + rest[1]
                            act.wait_ge(oT_done[i], pi + 1)
                            a.activation(a1["oT"][:, i], ps[:, PREP[1], :], ACT.Copy).then_inc(oT_ready[i], 1)
                        if name == "normed_T":
                            l = rest[0]
                            act.wait_ge(hnT_done[i], l + 1)
                            a.activation(hnT[:, i], ps[:, TB[i], :], ACT.Identity, bias=lgb[:, l, 1:2], scale=lgb[:, l, 0:1]).then_inc(hnT_ready[i], 1)
                        if name == "hidden":
                            l, j = rest
                            gi, n = l * 3 + j, HC[j][1]
                            act.wait_ge(g_done[i], gi + 1)
                            if j == 2:
                                act.wait_ge(hid_ready[i], gi - 1)
                            a.activation(gg[0:n, i, (j % 2) * N:(j % 2 + 1) * N], ps[0:n, hidden_banks(i, j)[0]], ACT.Gelu,
                                         bias=b1l[0:n, l, 1, j:j + 1]).then_inc(gelu1_done[i], 1)
                    act.wait_ge(x_rest_loaded, 16 * (B // U - 1))

                @block.vector
                def _(dve):
                    v = nc.vector
                    steps = [0]

                    def step(ins):
                        steps[0] += 1
                        return ins.then_inc(dve_step, 1)

                    def settle():
                        dve.wait_ge(dve_step, steps[0])

                    def norm_stats(u, src):
                        for t in range(T):
                            last = v.bn_stats(stats[:, u, t], src(t))
                        step(last)
                        settle()
                        for t in range(T):
                            last = v.bn_aggr(mv[:, u, t], stats[:, u, t])
                        step(last)
                        settle()
                        v.tensor_scalar(ve[:, u], mv[:, u, :, 1], EPS, None, ALU.add).then_inc(var_ready[u], 1)

                    def norm_apply(n, u, dst, src, ready):
                        dve.wait_ge(rstd_ready[u], n + 1)
                        for t in range(T):
                            last = v.tensor_scalar(dst(t), src(t), mv[:, u, t, 0:1], rstd[:, u, t:t + 1], ALU.subtract, ALU.mult)
                        last.then_inc(ready, 1)

                    dve.wait_ge(x_loaded, 16)
                    for u in range(U):
                        norm_stats(u, lambda t: x_in[:, bass.ds(it * U + u, 1), t].rearrange("p b d -> p (b d)"))
                    for u in range(U):
                        norm_apply(0, u, lambda t: xn[:, u, t],
                                   lambda t: x_in[:, bass.ds(it * U + u, 1), t].rearrange("p b d -> p (b d)"), xn_ready[u])
                    for u in range(U):
                        dve.wait_ge(xn_ready[u], 1)
                        norm_stats(u, lambda t: xn[:, u, t])
                    for u in range(U):
                        norm_apply(1, u, lambda t: tiles(a0["xhat"], u, t), lambda t: xn[:, u, t], xhat_ready)

                    dve.wait_ge(first_loaded, N_FIRST)
                    for u in range(U):
                        dve.wait_ge(logits_done, u + 1)
                        v.tensor_tensor(lg[:, u], bank_a(u)[:, 0:T * E].rearrange("p (t e) -> p t e", t=T),
                                        bc(rb, 1, T), ALU.add).then_inc(logits_read, 1)
                        dve.wait_ge(logits_read, u + 1)
                        for t in range(T):
                            last = v.max(top[:, u, t], lg[:, u, t])
                        step(last)
                        settle()
                        v.tensor_tensor(wts[:, u, 0], top[:, u, :, 1], top[:, u, :, 0], ALU.subtract).then_inc(top2_ready, 1)
                        for t in range(T):
                            last = v.max_index(topi[:, u, t], top[:, u, t], lg[:, u, t])
                        step(last)
                        settle()
                        step(v.tensor_copy(topf[:, u], topi[:, u, :, 0:2]))

                    x_written = [None, None]

                    def x_settled(u):
                        if x_written[u]:
                            dve.wait_ge(*x_written[u])

                    def biased(k):
                        u, t = k // T, k % T
                        dve.wait_ge(qkvg_done, k + 1)
                        v.tensor_tensor(a0["qkvg"][:, u, t * 512:(t + 1) * 512], ps[:, k % 4, :], bias0, ALU.add).then_inc(qkvg_biased, 1)

                    def gates(u):
                        dve.wait_ge(ew_ready, u + 1)
                        step(v.tensor_scalar(wts[:, u, 2], wts[:, u, 1], 1.0, None, ALU.add))
                        settle()
                        step(v.reciprocal(wts[:, u, 2], wts[:, u, 2]))
                        settle()
                        step(v.tensor_tensor(wts[:, u, 3], wts[:, u, 1], wts[:, u, 2], ALU.mult))
                        settle()
                        v.tensor_tensor(gsum[:, u], wts[:, u, 2], wts[:, u, 3], ALU.add)
                        v.memset(gate_a[:, u, :, E:E + 1], 1.0)
                        for t in range(T):
                            v.tensor_scalar(gate_a[:, u, t, 0:E], iota, topf[:, u, t, 0:1], wts[:, u, 2, t:t + 1], ALU.is_equal, ALU.mult)
                            last = v.tensor_scalar(gate_b[:, u, t], iota, topf[:, u, t, 1:2], wts[:, u, 3, t:t + 1], ALU.is_equal, ALU.mult)
                        step(last)
                        settle()
                        v.tensor_tensor(gate_a[:, u, :, 0:E], gate_a[:, u, :, 0:E], gate_b[:, u], ALU.add).then_inc(gates_ready, 1)
                        dve.wait_ge(x_copied, u + 1)
                        for t in range(T):
                            last = v.scalar_tensor_tensor(out=x[:, u, t], in0=xn[:, u, t], scalar=gsum[:, u, t:t + 1],
                                                          in1=x[:, u, t], op0=ALU.mult, op1=ALU.add)
                        step(last)
                        x_written[u] = (dve_step, steps[0])
                        dve.wait_ge(gates_ready, u + 1)

                    def gating(u):
                        gn = a0["gn"][:, u]
                        gn3 = gn.rearrange("p (t c) -> p t c", t=T)
                        qk3 = a0["qkvg"][:, u].rearrange("p (t c) -> p t c", t=T)[:, :, 0:256]
                        dve.wait_ge(gate_exp, u + 1)
                        step(v.tensor_scalar(gn, gn, 1.0, None, ALU.add))
                        settle()
                        step(v.reciprocal(gn, gn))
                        settle()
                        step(v.reduce_sum(gs[:, u], gn3, AX_X))
                        settle()
                        step(v.tensor_scalar(gs[:, u], gs[:, u], 1.0 / P, EPS, ALU.mult, ALU.add))
                        settle()
                        step(v.reciprocal(gs[:, u], gs[:, u]))
                        settle()
                        step(v.tensor_tensor(gn3, gn3, bc(gs[:, u], 2, P), ALU.mult))
                        settle()
                        for i in range(2):
                            last = v.tensor_tensor(qk3[:, :, i * P:(i + 1) * P], qk3[:, :, i * P:(i + 1) * P], gn3, ALU.mult)
                        step(last)
                        settle()
                        v.tensor_scalar(a0["me"][:, u].rearrange("p (t c) -> p t c", t=T), qk3, 0.0, None, ALU.min).then_inc(qk_min, 1)

                    def elu(u):
                        qk3 = a0["qkvg"][:, u].rearrange("p (t c) -> p t c", t=T)[:, :, 0:256]
                        dve.wait_ge(qk_exp, u + 1)
                        v.scalar_tensor_tensor(out=a0["qk"][:, u].rearrange("p (t c) -> p t c", t=T), in0=qk3, scalar=0.0,
                                               in1=a0["me"][:, u].rearrange("p (t c) -> p t c", t=T),
                                               op0=ALU.max, op1=ALU.add).then_inc(qk_ready, 1)

                    def states(u):
                        dve.wait_ge(state_done, u + 1)
                        v.tensor_tensor(a0["S"][:, u].rearrange("p (c h d) -> p c h d", c=3, h=H0),
                                        bank_b(u)[:, 0:3 * HV].rearrange("p (c h d) -> p c h d", c=3, h=H0),
                                        bc(bc(headmask, 2, D0 + 1), 1, 3), ALU.mult).then_inc(state_ready, 1)

                    def times_q_of(i):
                        t, hg, u = item(i)
                        dve.wait_ge(tile_part_done, i + 1)
                        q = a0["qk"][:, u, t * 256 + hg * 32:t * 256 + (hg + 1) * 32]
                        v.tensor_tensor(a0["prod"][:, u, (hg % 2) * 288:(hg % 2 + 1) * 288].rearrange("p (c m) -> p c m", m=D0 + 1),
                                        bank_a(u)[:, 0:288].rearrange("p (c m) -> p c m", m=D0 + 1), bc(q, 2, D0 + 1),
                                        ALU.mult).then_inc(times_q, 1)

                    def summed(i):
                        t, hg, u = item(i)
                        dve.wait_ge(times_q, i + 1)
                        step(v.reduce_sum(a0["sums"][:, u, hg * 36:(hg + 1) * 36].rearrange("p (h m) -> p h m", h=4),
                                          a0["prod"][:, u, (hg % 2) * 288:(hg % 2 + 1) * 288].rearrange("p (h d m) -> p h m d", h=4, d=D0), AX_X))

                    def attended(n):
                        t, u = n // U, n % U
                        settle()
                        o = a0["sums"][:, u]
                        if t:
                            dve.wait_ge(state_part_done, n - U + 1)
                            v.tensor_tensor(o, o, bank_b(u)[:, 0:HV], ALU.add).then_inc(state_part_added, 1)
                            dve.wait_ge(state_part_added, n - U + 1)
                        o = o.rearrange("p (h d) -> p h d", h=H0)
                        step(v.tensor_scalar(den0[:, u, t], o[:, :, D0], EPS, None, ALU.add))
                        settle()
                        step(v.reciprocal(den0[:, u, t], den0[:, u, t]))
                        settle()
                        v.tensor_tensor(tiles(a0["att"], u, t).rearrange("p (h d) -> p h d", h=H0), o[:, :, 0:D0],
                                        bc(den0[:, u, t], 2, D0), ALU.mult).then_inc(att_ready, 1)

                    def projected(u):
                        dve.wait_ge(proj_done, u + 1)
                        x_settled(u)
                        v.tensor_tensor(x[:, u].rearrange("p t d -> p (t d)"), x[:, u].rearrange("p t d -> p (t d)"),
                                        bank_a(u), ALU.add).then_inc(x_base, 1)
                        x_written[u] = (x_base, u + 1)

                    def expert_added(n):
                        u, e = n // E, n % E
                        dve.wait_ge(y0_done, n + 1)
                        x_settled(u)
                        for t in range(T):
                            last = v.scalar_tensor_tensor(out=x[:, u, t], in0=cols(bank_y(n), t),
                                                          scalar=gate_a[:, u, t, e:e + 1], in1=x[:, u, t],
                                                          op0=ALU.mult, op1=ALU.add)
                        last.then_inc(y_added, 1)
                        x_written[u] = (y_added, n + 1)

                    def sums(u, l, t):
                        dve.wait_ge(sq_ready[u], l * T + t + 1)
                        step(v.reduce_sum(ssq[:, u], a1["t1"][:, u].rearrange("p (g d) -> p g d", d=D1), AX_X))
                        settle()
                        v.tensor_scalar(ssq[:, u, 0:H1], ssq[:, u, 0:H1], 1e-24, QK_SCALE ** -2, ALU.max, ALU.mult)
                        v.tensor_scalar(ssq[:, u, H1:16], ssq[:, u, H1:16], 1e-24, None, ALU.max).then_inc(ss_ready[u], 1)

                    rotate1_step = [0, 0]

                    def rotate1(u, l, t):
                        step(v.tensor_tensor(a1["t1"][:, u].rearrange("p (q h d) -> p q h d", q=2, h=H1),
                                             a1["qn"][:, u].rearrange("p (q h d) -> p q h d", q=2, h=H1),
                                             bc(tabs[:, l, 0, t], 2, H1), ALU.mult))
                        rotate1_step[u] = steps[0]

                    def rotate(u, l, t):
                        dve.wait_ge(rot2_ready[u], l * T + t + 1)
                        dve.wait_ge(dve_step, rotate1_step[u])
                        v.tensor_tensor(a1["t1"][:, u], a1["t1"][:, u], a1["t2"][:, u], ALU.add).then_inc(rot_sum[u], 1)

                    def mask_max(u, l, s):
                        t, hp = s // HP, s % HP
                        ui = l * SLOTS + s
                        k0, k1, b0 = keys_of(t)
                        n = k1 - k0
                        dve.wait_ge(scores1_done[u], ui + 1)
                        if ui >= 2:
                            dve.wait_ge(exp_done[u], ui - 1)
                        if hp == 0:
                            dve.wait_ge(rn_ready[u], l * T + t + 1)
                        for i in range(2):
                            smv = a1["sm"][:, u].rearrange("p (r i k) -> p r i k", r=2, i=2)[:, s % 2, i, 0:n]
                            last = v.tensor_tensor_reduce(out=smv, in0=ps[:, SCORE[i], 0:n],
                                                          in1=band[:, b0:b0 + n] if i else band_even[:, 0:n], scale=1.0, scalar=3 * NEG,
                                                          op0=ALU.add, op1=ALU.max, accum_out=mx[:, u, s % 2, i:i + 1])
                        step(last)
                        settle()
                        v.scalar_tensor_tensor(out=nmx[:, u, s % 2], in0=mx[:, u, s % 2], scalar=-1.0,
                                               in1=rn[:, u, t % 2, 2 * hp:2 * hp + 2], op0=ALU.mult, op1=ALU.mult).then_inc(masked[u], 1)

                    def probs_moved(u, l, s):
                        t, ui = s // HP, l * SLOTS + s
                        dve.wait_ge(PT_done[u], ui + 1)
                        if ui >= 2:
                            dve.wait_ge(av_done[u], ui - 1)
                        c0 = 0 if t else P
                        v.tensor_copy(a1["PT"][:, u, (s % 2) * 384 + c0:(s % 2 + 1) * 384],
                                      ps[:, TB[u], c0:384]).then_inc(PT_ready[u], 1)

                    def prev_values(u, l, t):
                        dve.wait_ge(v1_ready[u], l * T + t)
                        if l or t >= 2:
                            dve.wait_ge(av_done[u], l * SLOTS + (t - 1) * HP)
                        src = v_tile(u, t - 1).rearrange("p (c i d) -> p c i d", c=HP, i=2)
                        dst = v_prev(u, t).rearrange("p (c i d) -> p c i d", c=HP, i=2)
                        for i in range(2):
                            last = v.tensor_copy(dst[64 * i:64 * i + 64, :, i], src[64:128, :, i])
                        last.then_inc(v_prev_ready[u], 1)

                    for name, i, *rest in plan:
                        if name == "expert" and i % FC == 1 and i >= 2 * FC + 1:
                            expert_added(i // FC - 2)
                        if name == "last_expert":
                            expert_added(U * E - 1)
                            for u in range(U):
                                for t in range(2):
                                    v.memset(v_prev(u, t), 0.0)
                        if name == "qkvg":
                            biased(i)
                        if name == "gates":
                            gates(i)
                        if name == "gating":
                            gating(i)
                        if name == "elu":
                            elu(i)
                        if name == "states":
                            states(i)
                        if name == "from_tile":
                            times_q_of(i)
                        if name == "summed":
                            summed(i)
                        if name == "attended":
                            attended(i)
                        if name == "project0":
                            projected(i)
                        if name == "norm1":
                            x_settled(i)
                            norm_stats(i, lambda t: x[:, i, t])
                            norm_apply(2, i, lambda t: xn[:, i, t], lambda t: x[:, i, t], xn_ready[i])
                        if name == "l1_qkv":
                            if i == 0:
                                dve.wait_ge(l1_loaded, N_L1)
                            dve.wait_ge(l1_qkv, 3 * i + 3)
                            v.tensor_tensor(a2["vt"][:, i].rearrange("p (t c) -> p t c", t=T), lin(i, 3).rearrange("p (t c) -> p t c", t=T),
                                            bc(bvo[:, 0, :], 1, T), ALU.add).then_inc(l1_v, 1)
                        if name == "l1_kv":
                            dve.wait_ge(l1_kv, i + 1)
                            v.tensor_tensor(a2["kve"][:, i, 0:P].rearrange("p (h d) -> p h d", h=H0),
                                            lin(i, 2)[:, 0:P].rearrange("p (h d) -> p h d", h=H0),
                                            bc(headmask, 2, D0), ALU.mult).then_inc(l1_kve, 1)
                        if name == "l1_num":
                            dve.wait_ge(l1_num, i + 1)
                            for half in range(2):
                                o = lin(i, 3 - half)[:, 0:2 * HV].rearrange("p (t c) -> p t c", t=2)
                                last = v.tensor_scalar(den0[:, i, 2 * half:2 * half + 2], o[:, :, P:HV], 1e-8, None, ALU.add)
                            step(last)
                            settle()
                            step(v.reciprocal(den0[:, i], den0[:, i]))
                            settle()
                            for t in range(T):
                                o = lin(i, 3 - t // 2)[:, (t % 2) * HV:(t % 2) * HV + P].rearrange("p (h d) -> p h d", h=H0)
                                last = v.tensor_tensor(tiles(a2["o1"], i, t).rearrange("p (h d) -> p h d", h=H0), o,
                                                       bc(den0[:, i, t], 2, D0), ALU.mult)
                            last.then_inc(l1_o, 1)
                        if name == "l1_out":
                            dve.wait_ge(l1_out, i + 1)
                            dve.wait_ge(l1_bo, i + 1)
                            v.tensor_tensor(x[:, i].rearrange("p t d -> p (t d)"), x[:, i].rearrange("p t d -> p (t d)"),
                                            lin(i, 1), ALU.add).then_inc(x_l1, 1)
                        if name == "norms":
                            sums(i, *rest)
                        if name == "rotate1":
                            rotate1(i, *rest)
                        if name == "rotate":
                            rotate(i, *rest)
                        if name == "scores":
                            mask_max(i, *rest)
                        if name == "probs_moved" and i == 1:
                            probs_moved(i, *rest)
                        if name == "prev_values" and rest[1]:
                            prev_values(i, *rest)
                        if name == "normalise_out":
                            l, t = rest
                            dve.wait_ge(exp_done[i], l * SLOTS + HP * (t + 1))
                            step(v.reciprocal(rsi[:, i], rs[:, i, t % 2]))
                            dve.wait_ge(av_done[i], l * SLOTS + HP * (t + 1))
                            settle()
                            v.tensor_tensor(a1["on"][:, i].rearrange("p (h d) -> p h d", h=H1),
                                            ps[:, OB[i], :].rearrange("p (h d) -> p h d", h=H1),
                                            bc(rsi[:, i], 2, D1), ALU.mult).then_inc(o_normed[i], 1)
                        if name == "project_out":
                            l, t = rest
                            dve.wait_ge(wo_done[i], l * T + t + 1)
                            v.tensor_tensor(xn[:, i, t], xn[:, i, t], ps[:, PREP[0], 0:P], ALU.add).then_inc(y_updated[i], 1)
                        if name == "shift_back":
                            l = rest[0]
                            dve.wait_ge(h_back[i], l + 1)
                            norm_stats(i, lambda t: cols(ps[:, OB[i], :], t))
                        if name == "normed_T":
                            l = rest[0]
                            norm_apply(3 + l, i, lambda t: tiles(hn, i, t), lambda t: cols(ps[:, OB[i], :], t), hn_ready[i])
                        if name == "hidden":
                            l, j = rest
                            gi, n = l * 3 + j, HC[j][1]
                            dve.wait_ge(a_done[i], gi + 1)
                            dve.wait_ge(gelu1_done[i], gi + 1)
                            v.scalar_tensor_tensor(out=hid[0:n, i, j * N:(j + 1) * N], in0=ps[0:n, hidden_banks(i, j)[1]],
                                                   scalar=b1l[0:n, l, 0, j:j + 1], in1=gg[0:n, i, (j % 2) * N:(j % 2 + 1) * N],
                                                   op0=ALU.add, op1=ALU.mult).then_inc(hid_ready[i], 1)
                        if name == "ffn_out":
                            l = rest[0]
                            dve.wait_ge(ffn_out[i], l + 1)
                            dve.wait_ge(y_b2[i], l + 1)
                            v.tensor_tensor(xn[:, i].rearrange("p t d -> p (t d)"), xn[:, i].rearrange("p t d -> p (t d)"),
                                            ps[:, OB[i], :], ALU.add).then_inc(y_final[i], 1)
                        if name == "final":
                            dve.wait_ge(y_final[i], L)
                            v.tensor_tensor(x_in[:, bass.ds(it * U + i, 1)].rearrange("p b t d -> p (b t) d"), x[:, i].rearrange("p t d -> p (t d)"),
                                            xn[:, i].rearrange("p t d -> p (t d)"),
                                            ALU.add).then_inc(out_ready, 1)

                @block.tensor
                def _(pe):
                    mm = nc.tensor.matmul

                    def transpose(dst, src):
                        return nc.tensor.transpose(dst, src, ident)

                    pe.wait_ge(tabs_made, 1)
                    for u in range(U):
                        pe.wait_ge(xn_ready[u], 1)
                        for t in range(T):
                            last = transpose(cols(bank_a(u), t), xn[:, u, t])
                        last.then_inc(norm_transposed, 1)
                        pe.wait_ge(xhat_ready, u + 1)
                        for t in range(T):
                            last = transpose(cols(bank_b(u), t), tiles(a0["xhat"], u, t))
                        last.then_inc(norm_transposed, 1)
                    pe.wait_ge(first_loaded, N_FIRST)
                    for u in range(U):
                        pe.wait_ge(normT_ready, 2 * u + 1)
                        for t in range(T):
                            last = mm(bank_a(u)[:, t * E:(t + 1) * E], tiles(a0["xnT"], u, t), rW[:], start=True, stop=True)
                        last.then_inc(logits_done, 1)

                    qk = a0["qk"]

                    def qkvg(k):
                        u, t = k // T, k % T
                        if k == 0:
                            pe.wait_ge(normT_ready, 2 * U)
                            pe.wait_ge(logits_read, U)
                        if k >= 4:
                            pe.wait_ge(qkvg_biased, k - 3)
                        mm(ps[:, k % 4, 0:384], tiles(a0["xnormT"], u, t), w0[:, 0:384], start=True, stop=True)
                        mm(ps[:, k % 4, 384:512], tiles(a0["xnT"], u, t), w0[:, 384:512], start=True, stop=True).then_inc(qkvg_done, 1)

                    def transpose_q0(u):
                        pe.wait_ge(qk_ready, u + 1)
                        pe.wait_ge(qkvg_biased, U * T)
                        for t in range(T):
                            last = transpose(cols(bank_a(u), t), qk[:, u, t * 256:t * 256 + P])
                        last.then_inc(qT_done, 1)

                    def states(u):
                        pe.wait_ge(v_ready, u + 1)
                        for c in range(1, T):
                            for t in range(c):
                                last = mm(bank_b(u)[:, (c - 1) * HV:c * HV], qk[:, u, t * 256 + P:(t + 1) * 256],
                                          a0["vext"][:, u, t * HV:(t + 1) * HV], start=(t == 0), stop=(t == c - 1))
                        last.then_inc(state_done, 1)

                    def from_tile(i):
                        t, hg, u = item(i)
                        if hg == 0:
                            pe.wait_ge(kv_ready, t * U + u + 1)
                        if i < U:
                            pe.wait_ge(qT_ready, u + 1)
                        else:
                            pe.wait_ge(times_q, i - U + 1)
                        mm(bank_a(u)[:, 0:288], causal, kv_cols(u, t, 4 * hg, 4 * hg + 4), start=True, stop=True).then_inc(tile_part_done, 1)

                    def from_state(n):
                        t, u = n // U, n % U
                        if t == 1:
                            pe.wait_ge(state_ready, u + 1)
                        else:
                            pe.wait_ge(state_part_added, n - 2 * U + 1)
                        mm(bank_b(u)[:, 0:HV], tiles(a0["qT"], u, t), a0["S"][:, u, (t - 1) * HV:t * HV],
                           start=True, stop=True).then_inc(state_part_done, 1)

                    def transpose_att(u):
                        pe.wait_ge(att_ready, (T - 1) * U + u + 1)
                        for t in range(T):
                            last = transpose(cols(bank_a(u), t), tiles(a0["att"], u, t))
                        last.then_inc(attT_done, 1)
                        pe.wait_ge(gates_ready, u + 1)
                        for t in range(T):
                            last = transpose(cols(bank_b(u), t)[0:E + 1], gate_a[:, u, t])
                        last.then_inc(attT_done, 1)

                    def project(u):
                        pe.wait_ge(attT_ready, 2 * u + 2)
                        for t in range(T):
                            mm(cols(bank_a(u), t), tiles(a0["attT"], u, t), wproj[:], start=True, stop=False)
                            last = mm(cols(bank_a(u), t), a0["gT"][0:E + 1, u, t * P:(t + 1) * P], b2ext[:], start=False, stop=True)
                        last.then_inc(proj_done, 1)

                    def expert_step(j):
                        n, f = j // FC, j % FC
                        if n < U * E:
                            if j == 0:
                                pe.wait_ge(experts_loaded, N_EXPERTS)
                            if f == 0:
                                pe.wait_ge(xe_ready, n + 1)
                            if j >= 2:
                                pe.wait_ge(gelu_done, j - 1)
                            mm(bank_h(j), W1[:, n % E, f * P:(f + 1) * P], a0["xe"][:, n // E, (n % 2) * N:(n % 2 + 1) * N],
                               start=True, stop=True).then_inc(h0_done, 1)
                        m = n - 1
                        if m >= 0:
                            if f == 0:
                                pe.wait_ge(gelu_done, FC * n)
                                if m >= 2:
                                    pe.wait_ge(y_added, m - 1)
                            for c in range(FC):
                                last = mm(cols(bank_y(m), f), ring[:, m % 2, c * N + f * P:c * N + (f + 1) * P],
                                          W2[:, m % E, c, :], start=(c == 0), stop=(c == FC - 1))
                            if f == FC - 1:
                                last.then_inc(y0_done, 1)

                    read = {}

                    def free(*banks):
                        for b in banks:
                            if b in read:
                                pe.wait_ge(*read[b])

                    def transpose_state(u, inst):
                        if inst in (1, 3):
                            pe.wait_ge(y_updated[u], T * (inst + 1) // 2)
                        elif inst == 2:
                            pe.wait_ge(y_final[u], 1)
                        free(TB[u])
                        for t in range(T):
                            last = transpose(cols(ps[:, TB[u], :], t), xn[:, u, t])
                        last.then_inc(y_transposed[u], 1)
                        read[TB[u]] = (hT_ready[u], inst + 1)

                    def lin_free(u, *which):
                        free(*(LIN[u][c] for c in which))

                    def lin_read(u, which, sem, value):
                        read[LIN[u][which]] = (sem, value)

                    def project_qk(u, l, t):
                        pi = l * T + t
                        if t == 0:
                            pe.wait_ge(hT_ready[u], 1 + 2 * l)
                        free(*PREP)
                        for c in range(2):
                            last = mm(ps[:, PREP[c], :], tiles(a1["hT"], u, t), wqkv[:, l, c * 512:(c + 1) * 512], start=True, stop=True)
                            read[PREP[c]] = (raw_ready[u], pi + 1)
                        last.then_inc(qk1_done[u], 1)

                    def project_v(u, l, t):
                        free(PREP[0])
                        mm(ps[:, PREP[0], :], tiles(a1["hT"], u, t), wqkv[:, l, 1024:1536], start=True, stop=True).then_inc(v1_done[u], 1)
                        read[PREP[0]] = (v1_ready[u], l * T + t + 1)

                    def transpose_qk(u, l, t):
                        pi = l * T + t
                        pe.wait_ge(rotated[u], pi + 1)
                        for i, bk in enumerate((PREP[1], PREP[0])):
                            free(bk)
                            for c in range(HP):
                                last = transpose(cols(ps[:, bk, :], c), a1["t1"][:, u, i * 512 + c * P:i * 512 + (c + 1) * P])
                            last.then_inc(qkT1_done[u], 1)
                            read[bk] = (qkT1_ready[u], 2 * pi + i + 1)

                    def scores(u, l, s):
                        t, hp = s // HP, s % HP
                        ui = l * SLOTS + s
                        k0, k1, _ = keys_of(t)
                        pe.wait_ge(qkT1_ready[u], 2 * (l * T + t) + 2)
                        free(*SCORE)
                        for i in range(2):
                            r = slice(64 * i, 64 * i + 64)
                            q = a1["qT"][r, u, (t % 2) * 512 + hp * P:(t % 2) * 512 + (hp + 1) * P]
                            keys = a1["kT"][r, u, hp * N + k0:hp * N + k1]
                            if i == 0 and t:
                                mm(ps[:, SCORE[i], 0:P], q, keys[:, W:KEYS], start=True, stop=True)
                                last = mm(ps[:, SCORE[i], P:KEYS], q, keys[:, 0:W], start=True, stop=True)
                            else:
                                last = mm(ps[:, SCORE[i], 0:k1 - k0], q, keys, start=True, stop=True)
                            read[SCORE[i]] = (masked[u], ui + 1)
                        last.then_inc(scores1_done[u], 1)

                    def transpose_probs(u, l, s):
                        t, ui = s // HP, l * SLOTS + s
                        pe.wait_ge(exp_done[u], ui + 1)
                        free(TB[u])
                        if t:
                            transpose(cols(ps[:, TB[u], :], 0), probs_of(u, s)[:, P:P + 2 * W])
                        for i in range(2):
                            last = transpose(cols(ps[:, TB[u], :], 1 + i), probs_of(u, s)[:, i * 2 * P:i * 2 * P + P])
                        last.then_inc(PT_done[u], 1)
                        read[TB[u]] = (PT_ready[u], ui + 1)

                    def weigh_values(u, l, s):
                        t, hp = s // HP, s % HP
                        ui = l * SLOTS + s
                        pe.wait_ge(PT_ready[u], ui + 1)
                        if hp == 0:
                            pe.wait_ge(v1_ready[u], l * T + t + 1)
                            if t:
                                pe.wait_ge(v_prev_ready[u], l * (T - 1) + t)
                            free(OB[u])
                        pt = a1["PT"][:, u, (s % 2) * 384:(s % 2 + 1) * 384]
                        if t:
                            mm(cols(ps[:, OB[u], :], hp), cols(pt, 0), cols(v_prev(u, t), hp), start=True, stop=False)
                        for i in range(2):
                            h = 2 * hp + i
                            last = mm(ps[:, OB[u], h * D1:(h + 1) * D1], cols(pt, 1 + i), v_tile(u, t)[:, h * D1:(h + 1) * D1],
                                      start=(t == 0), stop=(t == 0 or i == 1))
                        last.then_inc(av_done[u], 1)
                        read[OB[u]] = (o_normed[u], l * T + t + 1)

                    def transpose_out(u, l, t):
                        pe.wait_ge(o_normed[u], l * T + t + 1)
                        free(PREP[1])
                        for c in range(HP):
                            last = transpose(cols(ps[:, PREP[1], :], c), a1["on"][:, u, c * P:(c + 1) * P])
                        last.then_inc(oT_done[u], 1)
                        read[PREP[1]] = (oT_ready[u], l * T + t + 1)

                    def project_out(u, l, t):
                        pe.wait_ge(oT_ready[u], l * T + t + 1)
                        free(PREP[0])
                        for c in range(HP):
                            last = mm(ps[:, PREP[0], 0:P], a1["oT"][:, u, c * P:(c + 1) * P], wo[:, l, c, :],
                                      start=(c == 0), stop=(c == HP - 1))
                        last.then_inc(wo_done[u], 1)
                        read[PREP[0]] = (y_updated[u], l * T + t + 1)

                    shifts = [0, 0]
                    for name, i, *rest in plan:
                        if name == "expert":
                            expert_step(i)
                        if name == "last_expert":
                            for b in (4, 5):
                                read[b] = (y_added, U * E)
                            for b in (6, 7):
                                read[b] = (gelu_done, U * E * FC)
                        if name == "qkvg":
                            qkvg(i)
                        if name == "q_T":
                            transpose_q0(i)
                        if name == "states":
                            states(i)
                        if name == "from_tile":
                            from_tile(i)
                        if name == "from_state":
                            from_state(i)
                        if name == "att_T":
                            transpose_att(i)
                        if name == "project0":
                            project(i)
                            read[2 * i] = (x_base, i + 1)
                            read[2 * i + 1] = (attT_ready, 2 * i + 2)
                        if name == "state_T":
                            if shifts[i] == 0:
                                pe.wait_ge(xn_ready[i], 2)
                            transpose_state(i, shifts[i])
                            shifts[i] += 1
                        if name == "l1_qkv":
                            if i == 0:
                                pe.wait_ge(l1_loaded, N_L1)
                            pe.wait_ge(hT_ready[i], 1)
                            lin_free(i, 0, 1, 3)
                            for c in range(2):
                                mm(lin(i, c), wl1[:, c, :], a2["x1T"][:, i], start=True, stop=True).then_inc(l1_qkv, 1)
                                lin_read(i, c, l1_qs, 2 * i + c + 1)
                            for t in range(T):
                                last = mm(cols(lin(i, 3), t), tiles(a2["x1T"], i, t), wl1[:, 2, :], start=True, stop=True)
                            last.then_inc(l1_qkv, 1)
                            lin_read(i, 3, l1_v, i + 1)
                        if name == "l1_feat":
                            pe.wait_ge(l1_sq, 2 * i + 1)
                            lin_free(i, 0, 1)
                            mm(lin(i, 0), Rblk[:], a2["qs"][:, i], start=True, stop=False)
                            mm(lin(i, 0), nhb, a2["sqq"][:, i], start=False, stop=True).then_inc(l1_feat, 1)
                            pe.wait_ge(l1_sq, 2 * i + 2)
                            for t in range(T):
                                mm(cols(lin(i, 1), t), tiles(a2["ks"], i, t), Rblk[:], start=True, stop=False)
                                last = mm(cols(lin(i, 1), t), tiles(a2["sqk"], i, t), nhb, start=False, stop=True)
                            last.then_inc(l1_feat, 1)
                            for c in range(2):
                                lin_read(i, c, l1_exp, 2 * i + c + 1)
                        if name == "l1_kv":
                            pe.wait_ge(l1_exp, 2 * i + 2)
                            pe.wait_ge(l1_v, i + 1)
                            lin_free(i, 2)
                            for t in range(T):
                                last = mm(lin(i, 2)[:, 0:P], tiles(a2["kp"], i, t), tiles(a2["vt"], i, t), start=(t == 0), stop=(t == T - 1))
                            last.then_inc(l1_kv, 1)
                            lin_read(i, 2, l1_kve, i + 1)
                        if name == "l1_num":
                            pe.wait_ge(l1_kve, i + 1)
                            lin_free(i, 2, 3)
                            for t in range(T):
                                last = mm(lin(i, 3 - t // 2)[:, (t % 2) * HV:(t % 2 + 1) * HV], tiles(a2["qp"], i, t), a2["kve"][:, i],
                                          start=True, stop=True)
                            last.then_inc(l1_num, 1)
                            lin_read(i, 2, l1_o, i + 1)
                            lin_read(i, 3, l1_o, i + 1)
                        if name == "l1_oT":
                            pe.wait_ge(l1_o, i + 1)
                            lin_free(i, 0)
                            for t in range(T):
                                last = transpose(cols(lin(i, 0), t), tiles(a2["o1"], i, t))
                            last.then_inc(l1_oT_done, 1)
                            lin_read(i, 0, l1_oT, i + 1)
                        if name == "l1_out":
                            pe.wait_ge(l1_oT, i + 1)
                            lin_free(i, 1)
                            for t in range(T):
                                last = mm(cols(lin(i, 1), t), tiles(a2["o1T"], i, t), wl1[:, 3, :], start=True, stop=True)
                            last.then_inc(l1_out, 1)
                            lin_read(i, 1, x_l1, i + 1)
                        if name == "project_qk":
                            if i == 0 and rest == [0, 0]:
                                pe.wait_ge(layers_loaded, N_LAYERS)
                            project_qk(i, *rest)
                        if name == "project_v":
                            project_v(i, *rest)
                        if name == "transpose_qk":
                            transpose_qk(i, *rest)
                        if name == "scores":
                            scores(i, *rest)
                        if name == "transpose_probs":
                            transpose_probs(i, *rest)
                        if name == "weigh_values":
                            weigh_values(i, *rest)
                        if name == "transpose_out":
                            transpose_out(i, *rest)
                        if name == "project_out":
                            project_out(i, *rest)
                        if name == "shift_back":
                            l = rest[0]
                            pe.wait_ge(hT_ready[i], 2 + 2 * l)
                            free(OB[i])
                            for t in range(T):
                                last = transpose(cols(ps[:, OB[i], :], t), tiles(a1["hT"], i, t))
                            last.then_inc(h_back[i], 1)
                            read[OB[i]] = (hn_ready[i], l + 1)
                        if name == "normed_T":
                            l = rest[0]
                            pe.wait_ge(hn_ready[i], l + 1)
                            free(TB[i])
                            for t in range(T):
                                last = transpose(cols(ps[:, TB[i], :], t), tiles(hn, i, t))
                            last.then_inc(hnT_done[i], 1)
                            read[TB[i]] = (hnT_ready[i], l + 1)
                        if name == "hidden":
                            l, j = rest
                            c0, n = HC[j]
                            if j == 0:
                                pe.wait_ge(hnT_ready[i], l + 1)
                            gate_bank, bank = hidden_banks(i, j)
                            free(gate_bank, bank)
                            mm(ps[0:n, gate_bank], w1[:, l, HID + c0:HID + c0 + n], hnT[:, i], start=True, stop=True).then_inc(g_done[i], 1)
                            mm(ps[0:n, bank], w1[:, l, c0:c0 + n], hnT[:, i], start=True, stop=True).then_inc(a_done[i], 1)
                            read[gate_bank] = (gelu1_done[i], l * 3 + j + 1)
                            read[bank] = (hid_ready[i], l * 3 + j + 1)
                        if name == "ffn_out":
                            l = rest[0]
                            pe.wait_ge(hid_ready[i], l * 3 + 3)
                            free(OB[i])
                            for t in range(T):
                                for j, (_, n) in enumerate(HC):
                                    last = mm(cols(ps[:, OB[i], :], t), hid[0:n, i, j * N + t * P:j * N + (t + 1) * P], w2[0:n, l, j, :],
                                              start=(j == 0), stop=(j == 2))
                            last.then_inc(ffn_out[i], 1)
                            read[OB[i]] = (y_final[i], l + 1)

            engines = (nc.sync, nc.gpsimd, nc.scalar, nc.vector, nc.tensor)
            for k, s in enumerate(loop_sems):
                engines[k % len(engines)].sem_clear(s)
            nc.all_engine_barrier()
        nc.sync.wait_ge(out_stored, 16 * B)


_INS = ["L0_attn_w_qkv", "L0_attn_w_gate", "L0_attn_w_proj", "L0_attn_b_proj", "L0_ffn_router_W", "L0_ffn_W1",
        "L0_ffn_W2", "L0_ffn_b2", "L1_attn_R", "L1_ffn_wqkv", "L1_ffn_wo", "L1_ffn_w1", "L1_ffn_w2"]


def kernel(**inputs):
    import numpy as np
    import concourse.bacc as bacc
    from concourse.bass_utils import run_bass_kernel_spmd

    inputs = {name: np.asarray(a) for name, a in inputs.items()}
    arrays = {name: np.ascontiguousarray(inputs[name]) for name in _INS}
    arrays["x"] = np.ascontiguousarray(inputs["L0_attn_x"])
    for n in "qkvo":
        arrays[f"W{n}T"] = np.ascontiguousarray(inputs[f"L1_attn_W{n}"].T)
    arrays["rows"] = np.concatenate([inputs[n].reshape(-1) for n in (
        "L0_attn_b_qkv", "L0_attn_b_gate", "L0_ffn_router_b", "L1_attn_bv", "L1_attn_bo", "L1_ffn_b2")])
    qk = np.stack([inputs["L1_ffn_q_scale"], inputs["L1_ffn_k_scale"]], 1)
    swapped = np.concatenate([qk[..., D1 // 2:], qk[..., :D1 // 2]], -1)
    arrays["qksc"] = np.concatenate([qk.reshape(-1), swapped.reshape(-1)])
    b1l = np.zeros((L, 2, 3, P), np.float32)
    for j, (c0, n) in enumerate(HC):
        b1l[:, :, j, :n] = inputs["L1_ffn_b1"].reshape(L, 2, HID)[:, :, c0:c0 + n]
    lgb = np.stack([inputs["L1_ffn_ln_g"], inputs["L1_ffn_ln_b"]], 1).reshape(2 * L, P)
    arrays["colv"] = np.ascontiguousarray(np.concatenate([
        inputs["L0_attn_ln_g"][None], inputs["L0_attn_ln_b"][None], inputs["L0_ffn_ln_g"], inputs["L0_ffn_ln_b"],
        inputs["L0_ffn_b1"].reshape(E * FC, P), lgb, b1l.reshape(-1, P), inputs["L1_attn_bq"][None],
        inputs["L1_attn_bk"][None]]).T)
    arrays["cst"], arrays["rot"] = shape_constants(np)

    nc = bacc.Bacc("TRN2", target_bir_lowering=False, num_devices=1)
    A, feed = {}, {}
    for name, a in arrays.items():
        A[name] = nc.dram_tensor(f"in_{name}", a.shape, mybir.dt.from_np(a.dtype), kind="ExternalInput").ap()
        feed[f"in_{name}"] = a
    out = nc.dram_tensor("out", (B, N, P), F32, kind="ExternalOutput").ap()
    build(nc, A, out)
    r = run_bass_kernel_spmd(nc, [feed], core_ids=[0])
    return r.results[0]["out"]
```
